# Optimizing a Trainium2 kernel written in Bass

```python
import numpy as np
import jax
import jax.numpy as jnp

def _softmax(x, axis=-1):
    return jax.nn.softmax(x, axis=axis)

def _gelu(x):
    return jax.nn.gelu(x, approximate=True)

def _silu(x):
    return jax.nn.silu(x)

def _sigmoid(x):
    return jax.nn.sigmoid(x)

def _layernorm(x, axis=-1, eps=1e-05):
    m = jnp.mean(x, axis=axis, keepdims=True)
    v = jnp.var(x, axis=axis, keepdims=True)
    return (x - m) / jnp.sqrt(v + eps)

def _scatter_add(tgt, idx, src, axis=0):
    return tgt.at[idx].add(src)

def _segment_sum(src, seg, n):
    return jax.ops.segment_sum(src, seg, n)
kernel_name = 'mk_xattn_ffn_d1_seqx_r8_7ddd89'

def setup_inputs(seed: int=0):
    np.random.seed(seed)
    _w = jnp.asarray

    def _rec_inputs():
        import jax
        import jax.numpy as jnp
        _rk = jax.random.key(seed)
        x = 7.22e-05 + 1 * jax.random.normal(jax.random.fold_in(_rk, 1), (64, 64, 256), jnp.float32)
        _lenS = 64 - jax.random.randint(jax.random.fold_in(_rk, 7), (64,), 0, max(1, 64 // 4) + 1, jnp.int32)
        _lenS2 = 64 - jax.random.randint(jax.random.fold_in(_rk, 8), (64,), 0, max(1, 64 // 4) + 1, jnp.int32)
        _ctx_1024P = jax.random.normal(jax.random.fold_in(_rk, 11), (64, 16, 128), jnp.float32)
        _ctx_1024c = jax.random.dirichlet(jax.random.fold_in(_rk, 511), 0.3 * jnp.ones((16,), jnp.float32), (64, 64))
        _ctx_1024t = jnp.einsum('bsk,bkd->bsd', _ctx_1024c, _ctx_1024P)
        _ctx_1024t = _ctx_1024t * jax.lax.rsqrt(jnp.mean(jnp.square(_ctx_1024t)) + 1e-12) * 0.953939
        ctx_1024 = -0.000673644 + 1.00013 * (_ctx_1024t + 0.3 * jax.random.normal(jax.random.fold_in(_rk, 611), (64, 64, 128), jnp.float32))
        return (x, ctx_1024)
    x, ctx_1024 = _rec_inputs()

    def _L0_xattn_setup():
        import jax, jax.numpy as jnp
        import numpy as np
        B, S1, S2, DCA = (2, 256, 128, 16)
        QDIM, KDIM, H = (256, 128, 16)
        HD = QDIM // H
        SCALE = HD ** (-0.5)
        EPS = 1e-06
        DCA_WEIGHT = 1.0

        def _ln(t, w, b):
            m = jnp.mean(t, axis=-1, keepdims=True)
            v = jnp.var(t, axis=-1, keepdims=True)
            return (t - m) * jax.lax.rsqrt(v + EPS) * w + b

        def _attn(q, k, v):
            s = jnp.einsum('bhqd,bhkd->bhqk', q, k) * SCALE
            p = jax.nn.softmax(s, axis=-1)
            return jnp.einsum('bhqk,bhkd->bhqd', p, v)
        key = jax.random.key(seed)
        ks = jax.random.split(key, 8)
        w = lambda k, shape: jax.random.normal(k, shape, jnp.float32) * 0.02
        return {'x': jax.random.normal(ks[0], (B, S1, QDIM), jnp.float32), 'y': jax.random.normal(ks[1], (B, S2 + DCA, KDIM), jnp.float32), 'Wq': w(ks[2], (QDIM, QDIM)), 'bq': jnp.zeros((QDIM,), jnp.float32), 'Wk': w(ks[3], (KDIM, QDIM)), 'bk': jnp.zeros((QDIM,), jnp.float32), 'Wv': w(ks[4], (KDIM, QDIM)), 'bv': jnp.zeros((QDIM,), jnp.float32), 'Wkv_dca': w(ks[5], (KDIM, 2 * QDIM)), 'bkv_dca': jnp.zeros((2 * QDIM,), jnp.float32), 'qn_w': jnp.ones((HD,), jnp.float32), 'qn_b': jnp.zeros((HD,), jnp.float32), 'kn_w': jnp.ones((HD,), jnp.float32), 'kn_b': jnp.zeros((HD,), jnp.float32), 'kn_dca_w': jnp.ones((HD,), jnp.float32), 'kn_dca_b': jnp.zeros((HD,), jnp.float32), 'Wo': w(ks[6], (QDIM, QDIM)), 'bo': jnp.zeros((QDIM,), jnp.float32)}
    _L0_xattn_all = _L0_xattn_setup()
    _L0_xattn_in = {k: v for k, v in _L0_xattn_all.items() if k in ('Wq', 'bq', 'Wk', 'bk', 'Wv', 'bv', 'Wkv_dca', 'bkv_dca', 'qn_w', 'qn_b', 'kn_w', 'kn_b', 'kn_dca_w', 'kn_dca_b', 'Wo', 'bo')}
    del _L0_xattn_all

    def _L0_ffn_setup():
        import jax, jax.numpy as jnp
        import numpy as np
        HIDDEN = 256
        MOE_INTER = 128
        SHARED_INTER = 512
        N_EXPERTS = 16
        TOP_K = 2
        N_GROUP = 4
        TOPK_GROUP = 2
        NORM_TOPK_PROB = True
        ROUTED_SCALING = 1.0

        def relu2(x):
            r = jax.nn.relu(x)
            return r * r

        def _get_topk_indices(scores, e_bias):
            T, E = scores.shape
            s = scores + e_bias[None, :]
            gsz = E // N_GROUP
            group_scores = jax.lax.top_k(s.reshape(T, N_GROUP, gsz), 2)[0].sum(-1)
            group_idx = jax.lax.top_k(group_scores, TOPK_GROUP)[1]
            group_mask = jnp.zeros((T, N_GROUP), dtype=bool).at[jnp.arange(T)[:, None], group_idx].set(True)
            score_mask = jnp.repeat(group_mask, gsz, axis=1)
            masked = jnp.where(score_mask, s, 0.0)
            topk_indices = jax.lax.top_k(masked, TOP_K)[1]
            return jax.lax.stop_gradient(topk_indices)

        def _router(x_flat, router_weight, e_bias):
            logits = jnp.einsum('th,eh->te', x_flat.astype(jnp.float32), router_weight.astype(jnp.float32))
            scores = jax.nn.sigmoid(logits)
            topk_indices = _get_topk_indices(scores, e_bias)
            topk_weights = jnp.take_along_axis(scores, topk_indices, axis=1)
            if NORM_TOPK_PROB:
                topk_weights = topk_weights / (topk_weights.sum(-1, keepdims=True) + 1e-20)
            return (topk_indices, topk_weights * ROUTED_SCALING)
        key = jax.random.key(seed)
        ks = jax.random.split(key, 6)
        s = 0.02
        hidden_states = jax.random.normal(ks[0], (1, 256, HIDDEN), dtype=jnp.float32)
        router_weight = jax.random.normal(ks[1], (N_EXPERTS, HIDDEN), dtype=jnp.float32) * s
        e_bias = jnp.zeros((N_EXPERTS,), dtype=jnp.float32)
        w_up = jax.random.normal(ks[2], (N_EXPERTS, HIDDEN, MOE_INTER), dtype=jnp.float32) * s
        w_down = jax.random.normal(ks[3], (N_EXPERTS, MOE_INTER, HIDDEN), dtype=jnp.float32) * s
        shared_up = jax.random.normal(ks[4], (HIDDEN, SHARED_INTER), dtype=jnp.float32) * s
        shared_down = jax.random.normal(ks[5], (SHARED_INTER, HIDDEN), dtype=jnp.float32) * s
        return {'hidden_states': hidden_states, 'router_weight': router_weight, 'e_bias': e_bias, 'w_up': w_up, 'w_down': w_down, 'shared_up': shared_up, 'shared_down': shared_down}
    _L0_ffn_all = _L0_ffn_setup()
    _L0_ffn_in = {k: v for k, v in _L0_ffn_all.items() if k in ('router_weight', 'e_bias', 'w_up', 'w_down', 'shared_up', 'shared_down')}
    del _L0_ffn_all
    return {'x': x, 'ctx_1024': ctx_1024, 'L0_xattn_Wq': _L0_xattn_in['Wq'], 'L0_xattn_bq': _L0_xattn_in['bq'], 'L0_xattn_Wk': _L0_xattn_in['Wk'], 'L0_xattn_bk': _L0_xattn_in['bk'], 'L0_xattn_Wv': _L0_xattn_in['Wv'], 'L0_xattn_bv': _L0_xattn_in['bv'], 'L0_xattn_Wkv_dca': _L0_xattn_in['Wkv_dca'], 'L0_xattn_bkv_dca': _L0_xattn_in['bkv_dca'], 'L0_xattn_qn_w': _L0_xattn_in['qn_w'], 'L0_xattn_qn_b': _L0_xattn_in['qn_b'], 'L0_xattn_kn_w': _L0_xattn_in['kn_w'], 'L0_xattn_kn_b': _L0_xattn_in['kn_b'], 'L0_xattn_kn_dca_w': _L0_xattn_in['kn_dca_w'], 'L0_xattn_kn_dca_b': _L0_xattn_in['kn_dca_b'], 'L0_xattn_Wo': _L0_xattn_in['Wo'], 'L0_xattn_bo': _L0_xattn_in['bo'], 'L0_ffn_router_weight': _L0_ffn_in['router_weight'], 'L0_ffn_e_bias': _L0_ffn_in['e_bias'], 'L0_ffn_w_up': _L0_ffn_in['w_up'], 'L0_ffn_w_down': _L0_ffn_in['w_down'], 'L0_ffn_shared_up': _L0_ffn_in['shared_up'], 'L0_ffn_shared_down': _L0_ffn_in['shared_down']}

def reference(x, ctx_1024, L0_xattn_Wq, L0_xattn_bq, L0_xattn_Wk, L0_xattn_bk, L0_xattn_Wv, L0_xattn_bv, L0_xattn_Wkv_dca, L0_xattn_bkv_dca, L0_xattn_qn_w, L0_xattn_qn_b, L0_xattn_kn_w, L0_xattn_kn_b, L0_xattn_kn_dca_w, L0_xattn_kn_dca_b, L0_xattn_Wo, L0_xattn_bo, L0_ffn_router_weight, L0_ffn_e_bias, L0_ffn_w_up, L0_ffn_w_down, L0_ffn_shared_up, L0_ffn_shared_down):
    import jax
    import jax.numpy as jnp

    def _L0_xattn_ref(x, y, Wq, bq, Wk, bk, Wv, bv, Wkv_dca, bkv_dca, qn_w, qn_b, kn_w, kn_b, kn_dca_w, kn_dca_b, Wo, bo):
        import jax, jax.numpy as jnp
        import numpy as np
        B, S1, S2, DCA = (2, 256, 128, 16)
        QDIM, KDIM, H = (256, 128, 16)
        HD = QDIM // H
        SCALE = HD ** (-0.5)
        EPS = 1e-06
        DCA_WEIGHT = 1.0

        def _ln(t, w, b):
            m = jnp.mean(t, axis=-1, keepdims=True)
            v = jnp.var(t, axis=-1, keepdims=True)
            return (t - m) * jax.lax.rsqrt(v + EPS) * w + b

        def _attn(q, k, v):
            s = jnp.einsum('bhqd,bhkd->bhqk', q, k) * SCALE
            p = jax.nn.softmax(s, axis=-1)
            return jnp.einsum('bhqk,bhkd->bhqd', p, v)
        b, s1, _ = x.shape
        y_dca = y[:, -DCA:, :]
        y_main = y[:, :-DCA, :]
        kv_dca = (y_dca @ Wkv_dca + bkv_dca).reshape(b, DCA, 2, H, HD)
        k_dca = _ln(kv_dca[:, :, 0], kn_dca_w, kn_dca_b)
        v_dca = kv_dca[:, :, 1]
        s2 = y_main.shape[1]
        q = _ln((x @ Wq + bq).reshape(b, s1, H, HD), qn_w, qn_b)
        kv = jnp.concatenate([y_main @ Wk + bk, y_main @ Wv + bv], axis=-1)
        kv = kv.reshape(b, s2, H, 2 * HD)
        k = _ln(kv[..., :HD], kn_w, kn_b)
        v = kv[..., HD:]
        qT = q.transpose(0, 2, 1, 3)
        ctx = _attn(qT, k.transpose(0, 2, 1, 3), v.transpose(0, 2, 1, 3))
        ctx = ctx.transpose(0, 2, 1, 3).reshape(b, s1, QDIM)
        ctx_dca = _attn(qT, k_dca.transpose(0, 2, 1, 3), v_dca.transpose(0, 2, 1, 3))
        ctx_dca = ctx_dca.transpose(0, 2, 1, 3).reshape(b, s1, QDIM)
        ctx = ctx + DCA_WEIGHT * ctx_dca
        return ctx @ Wo + bo

    def _L0_ffn_ref(hidden_states, router_weight, e_bias, w_up, w_down, shared_up, shared_down):
        import jax, jax.numpy as jnp
        import numpy as np
        HIDDEN = 256
        MOE_INTER = 128
        SHARED_INTER = 512
        N_EXPERTS = 16
        TOP_K = 2
        N_GROUP = 4
        TOPK_GROUP = 2
        NORM_TOPK_PROB = True
        ROUTED_SCALING = 1.0

        def relu2(x):
            r = jax.nn.relu(x)
            return r * r

        def _get_topk_indices(scores, e_bias):
            T, E = scores.shape
            s = scores + e_bias[None, :]
            gsz = E // N_GROUP
            group_scores = jax.lax.top_k(s.reshape(T, N_GROUP, gsz), 2)[0].sum(-1)
            group_idx = jax.lax.top_k(group_scores, TOPK_GROUP)[1]
            group_mask = jnp.zeros((T, N_GROUP), dtype=bool).at[jnp.arange(T)[:, None], group_idx].set(True)
            score_mask = jnp.repeat(group_mask, gsz, axis=1)
            masked = jnp.where(score_mask, s, 0.0)
            topk_indices = jax.lax.top_k(masked, TOP_K)[1]
            return jax.lax.stop_gradient(topk_indices)

        def _router(x_flat, router_weight, e_bias):
            logits = jnp.einsum('th,eh->te', x_flat.astype(jnp.float32), router_weight.astype(jnp.float32))
            scores = jax.nn.sigmoid(logits)
            topk_indices = _get_topk_indices(scores, e_bias)
            topk_weights = jnp.take_along_axis(scores, topk_indices, axis=1)
            if NORM_TOPK_PROB:
                topk_weights = topk_weights / (topk_weights.sum(-1, keepdims=True) + 1e-20)
            return (topk_indices, topk_weights * ROUTED_SCALING)
        orig_shape = hidden_states.shape
        x = hidden_states.reshape(-1, HIDDEN)
        T = x.shape[0]
        topk_indices, topk_weights = _router(x, router_weight, e_bias)
        combine = jnp.zeros((T, N_EXPERTS), dtype=topk_weights.dtype).at[jnp.arange(T)[:, None], topk_indices].add(topk_weights)
        h1 = jnp.einsum('th,ehi->tei', x, w_up)
        a = relu2(h1) * combine[:, :, None]
        routed = jnp.einsum('tei,eih->th', a, w_down)
        shared = relu2(hidden_states @ shared_up) @ shared_down
        return routed.reshape(orig_shape) + shared
    x = x + _L0_xattn_ref(_layernorm(x, axis=-1), ctx_1024, L0_xattn_Wq, L0_xattn_bq, L0_xattn_Wk, L0_xattn_bk, L0_xattn_Wv, L0_xattn_bv, L0_xattn_Wkv_dca, L0_xattn_bkv_dca, L0_xattn_qn_w, L0_xattn_qn_b, L0_xattn_kn_w, L0_xattn_kn_b, L0_xattn_kn_dca_w, L0_xattn_kn_dca_b, L0_xattn_Wo, L0_xattn_bo)
    x = x + _L0_ffn_ref(_layernorm(x, axis=-1), L0_ffn_router_weight, L0_ffn_e_bias, L0_ffn_w_up, L0_ffn_w_down, L0_ffn_shared_up, L0_ffn_shared_down)
    return x

_drawn_inputs = setup_inputs


def setup_inputs(seed=0):
    import zlib

    import numpy as np

    out = dict(_drawn_inputs(seed))
    spreads = {'L0_xattn_bq': (0.0, 0.8),
     'L0_xattn_bk': (0.0, 0.398),
     'L0_xattn_bv': (0.0, 0.33),
     'L0_xattn_bkv_dca': (0.0, 0.1),
     'L0_xattn_qn_w': (1.0, 0.6),
     'L0_xattn_qn_b': (0.0, 0.8),
     'L0_xattn_kn_w': (1.0, 0.6),
     'L0_xattn_kn_b': (0.0, 0.8),
     'L0_xattn_kn_dca_w': (1.0, 0.6),
     'L0_xattn_kn_dca_b': (0.0, 0.8),
     'L0_xattn_bo': (0.0, 0.1),
     'L0_ffn_e_bias': (0.0, 0.336)}
    factors = {'L0_ffn_router_weight': 4.46, 'L0_ffn_w_up': 3.11, 'L0_ffn_w_down': 2.842}
    for name, (base, spread) in spreads.items():
        noise = np.random.default_rng([zlib.crc32(name.encode()), seed]).standard_normal(out[name].shape)
        drawn = base * np.exp(spread * noise) if base else spread * noise
        out[name] = jnp.asarray(drawn.astype(out[name].dtype))
    for name, factor in factors.items():
        out[name] = (out[name] * factor).astype(out[name].dtype)
    return out
```

```python
from contextlib import ExitStack

import concourse.bass as bass
from concourse import mybir

F32 = mybir.dt.float32
I32 = mybir.dt.int32
ALU = mybir.AluOpType
ACT = mybir.ActivationFunctionType
AX = mybir.AxisListType

P = 128
NB, SQ, D = 64, 64, 256
SK, KD = 64, 128
DCA = 16
SM = SK - DCA
H = 16
HD = D // H
SCALE = HD ** -0.5
EPS_HEAD = 1e-6
EPS_LN = 1e-5
E, MI, SI = 16, 128, 512
NG, GSZ = 4, 4
PAIRS = NB // 2
GROUPS = PAIRS // 2
SETS = H // 4
MR = 2 * SM
CW = 4 * SK
HP = H // 2
SLOT_TILES = 80
N_CONST = 11
UNROLL = 4
SLOTS = SLOT_TILES * P
KC = D // P
SCH = 512
NCH = NB * SQ // SCH
NM = SI // P
STEPS = SLOT_TILES // UNROLL
BIG = 1e30


class Chain:

    def __init__(self, eng, sem, per_step, step):
        self.eng, self.sem, self.per, self.n = eng, sem, per_step, 0
        self.base = step * per_step

    def done(self, ins):
        self.n += 1
        ins.then_inc(self.sem, 1)
        return self.n

    def need(self, k):
        self.eng.wait_ge(self.sem, self.base + k)

    def need_alone(self, k):
        self.wait_alone(self.eng, self.sem, self.base + k)

    def link(self, ins):
        self.need(self.done(ins))

    def end(self):
        assert self.n == self.per, (self.n, self.per)


def xattn_moe(nc, x, ctx, Wq, bq, Wk, bk, Wv, bv, Wkvd, bkvd, qn_w, qn_b, kn_w, kn_b, kd_w, kd_b, Wo, bo,
              router, e_bias, w_up, w_down, sh_up, sh_down, out):
    stack = ExitStack()
    with stack:
        def sb(name, shape, dt=F32):
            return stack.enter_context(nc.sbuf_tensor(name, shape, dt))

        def sem(name):
            return stack.enter_context(nc.semaphore(name))

        bank = [stack.enter_context(nc.psum_tensor(f"bank{i}", [P, 512], F32)) for i in range(4, 8)]
        score_ps = stack.enter_context(nc.psum_tensor("score_ps", [P, 2 * 512], F32))
        probsT_ps = stack.enter_context(nc.psum_tensor("probsT_ps", [P, 2, 512], F32))
        bank = [score_ps[:, 0:512], score_ps[:, 512:1024], probsT_ps[:, 0, :], probsT_ps[:, 1, :]] + \
               [b[:, :] for b in bank]

        vd_dram = nc.dram_tensor("vd_dram", [PAIRS * DCA, 2 * D], F32, kind="Internal").ap()
        xn2T_dram = nc.dram_tensor("xn2T_dram", [KC, P, NB * SQ], F32, kind="Internal").ap()
        slot_x = nc.dram_tensor("slot_x", [SLOTS, D], F32, kind="Internal").ap()
        slot_y = nc.dram_tensor("slot_y", [SLOTS, D], F32, kind="Internal").ap()

        ident = sb("ident", [P, P])
        tri = sb("tri", [P, P])
        ones = sb("ones", [P, P])
        zeros = sb("zeros", [P, D])
        half = sb("half", [P, 2])
        slotm = sb("slotm", [P, 2])
        quad = sb("quad", [P, 4])
        wq_sb = sb("wq_sb", [P, KC, D])
        wkv_sb = sb("wkv_sb", [P, 2 * D])
        wkvd_sb = sb("wkvd_sb", [P, 2 * D])
        wo_sb = sb("wo_sb", [P, KC, D])
        bq_sb = sb("bq_sb", [P, D])
        bkv_sb = sb("bkv_sb", [P, 2 * D])
        bkvd_sb = sb("bkvd_sb", [P, 2 * D])
        bo_sb = sb("bo_sb", [P, D])
        router_in = sb("router_in", [E, D])
        router_sb = sb("router_sb", [P, KC, E])
        ebias_sb = sb("ebias_sb", [P, E])
        ln_in = sb("ln_in", [6, P])
        ln_col = sb("ln_col", [P, 6])
        q_bias2 = sb("q_bias2", [P, 2])
        k_w4 = sb("k_w4", [P, 4])
        k_b4 = sb("k_b4", [P, 4])
        up_sb = sb("up_sb", [P, E, KC, MI])
        down_sb = sb("down_sb", [P, E, D])
        su_sb = sb("su_sb", [P, KC, SI])
        sd_sb = sb("sd_sb", [P, SI // P, D])
        wmean = sb("wmean", [P, 7, H])
        X2 = sb("X2", [P, PAIRS, D])
        XN2 = sb("XN2", [P, PAIRS, D])
        logits = sb("logits", [P, PAIRS, E])
        kdT = sb("kdT", [P, PAIRS, SETS, DCA])
        loop_stack = ExitStack()

        def sbl(name, shape, dt=F32):
            return loop_stack.enter_context(nc.sbuf_tensor(name, shape, dt))

        x_in = sbl("x_in", [P, 2, D])
        y_in = sbl("y_in", [P, 2, KD])
        xn = sbl("xn", [P, 2, D])
        xnT = sbl("xnT", [P, 2, KC, P])
        yT = sbl("yT", [P, 2, P])
        q_sb = sbl("q_sb", [P, 2, D])
        kv_sb = sbl("kv_sb", [P, 2, 2 * D])
        sq = sbl("sq", [P, 2, 2, D])
        stat = sbl("stat", [P, 64])
        rst = sbl("rst", [P, 3, 64])
        q_rstd2 = sbl("q_rstd2", [P, 2, H, 2])
        qn = sbl("qn", [P, 2, 2 * D])
        kn = sbl("kn", [P, 2 * D])
        qT = sbl("qT", [P, 2, SETS, P])
        k_bd = sbl("k_bd", [P, 2, SETS, 4, SK])
        v_rep = sbl("v_rep", [P, 2, 2 * D])
        v_bd = sbl("v_bd", [P, 2, 2 * D])
        probs = sbl("probs", [P, 2, H, SK])
        pmax = sbl("pmax", [P, 2, 2, H])
        psum_ = sbl("psum_", [P, 2, 2, H])
        prec = sbl("prec", [P, 2, 2, H])
        probsT = sbl("probsT", [P, 2, 2, 512])
        ctxT = sbl("ctxT", [P, 2, KC, P])
        xn2 = sbl("xn2", [P, 2, D])
        xn2T = sbl("xn2T", [P, KC, 2, P])
        bn = sbl("bn", [P, 2, 6])
        mv = sbl("mv", [P, 2, 2])
        lr = sbl("lr", [P, 4, 2])
        bn2 = sbl("bn2", [P, 2, 6])
        mv2 = sbl("mv2", [P, 2, 2])
        lr2 = sbl("lr2", [P, 4, 2])

        loop_stack.close()
        xT_ch = sb("xT_ch", [P, 2, KC, SCH])
        relu = sb("relu", [P, 2, SCH])
        hid = sb("hid", [P, 2, SI // P, SCH])
        sig = sb("sig", [P, PAIRS, E])
        sel = sb("sel", [P, PAIRS, E])
        pair_sums = sb("pair_sums", [P, PAIRS * NG, 6])
        gsum = sb("gsum", [P, PAIRS, NG])
        gtmp = sb("gtmp", [P, PAIRS, NG])
        goh = sb("goh", [P, 2, PAIRS, NG])
        oh = sb("oh", [P, 2, PAIRS, E])
        etmp = sb("etmp", [P, PAIRS, E])
        top = sb("top", [P, PAIRS])
        gate = sb("gate", [P, 3, PAIRS])
        slot = sb("slot", [P, 2, PAIRS])
        slot_i = sb("slot_i", [P, 2, PAIRS], I32)
        count = sb("count", [P, 6, E])
        count_i = sb("count_i", [P, 2, E], I32)
        tile_no = sb("tile_no", [1, SLOT_TILES, 1])
        past = sb("past", [1, SLOT_TILES, E])
        eoff = sb("eoff", [1, SLOT_TILES])
        eoff_i = sb("eoff_i", [1, SLOT_TILES], I32)
        desc = sb("desc", [P, 1, E])
        xt = sb("xt", [P, UNROLL, D])
        xtT = sb("xtT", [P, UNROLL, KC, P])
        er = sb("er", [P, UNROLL * MI])
        ea = sb("ea", [P, UNROLL * MI])
        eaT = sb("eaT", [P, UNROLL * P])
        ey = sb("ey", [P, UNROLL, D])
        gidx = sb("gidx", [P, 2, 2, UNROLL], I32)
        gath = XN2[:, 0:4 * UNROLL, :].rearrange("p (h k j) d -> p h k j d", h=2, k=2)
        res = XN2[:, 4 * UNROLL:6 * UNROLL, :].rearrange("p (h j) d -> p h j d", h=2)

        s_alone = sem("waits_alone")
        s_w = sem("weights_loaded")
        s_w2 = sem("ffn_weights_loaded")
        s_zero = sem("slots_zeroed")
        s_const = sem("constants_ready")
        s_prep = sem("weights_prepared")
        s_prep_ps = sem("prep_transposed")
        s_in = sem("inputs_loaded")
        s_ch = sem("dve_setup_chain")
        s_cha = sem("dve_chain_a")
        s_chb = sem("dve_chain_b")
        s_chd = sem("dve_chain_dca")
        s_xbo = sem("x_plus_bo_stored")
        s_xn = sem("xn_ready")
        s_yT_ps = sem("yT_in_psum")
        s_xT_ps = sem("xT_in_psum")
        s_yT = sem("yT_ready")
        s_xT = sem("xT_ready")
        s_kv_ps = sem("kv_in_psum")
        s_q_ps = sem("q_in_psum")
        s_kv = sem("kv_ready")
        s_q = sem("q_ready")
        s_sq = sem("squares_ready")
        s_rstd = sem("head_rstd_ready")
        s_kn = sem("kn_ready")
        s_qn = sem("qn_ready")
        s_kT_ps = sem("kT_in_psum")
        s_qT_ps = sem("qT_in_psum")
        s_kbd = sem("k_main_blocks_ready")
        s_kbdd = sem("k_dca_blocks_ready")
        s_qT = sem("qT_ready")
        s_v = sem("v_replicated")
        s_vbd = sem("v_blocks_ready")
        s_s_ps = sem("scores_in_psum")
        s_sub = sem("scores_minus_max")
        s_exp = sem("exp_ready")
        s_rsum = sem("inverse_sums_ready")
        s_p = sem("probs_ready")
        s_pT_ps = sem("probsT_in_psum")
        s_pT0 = sem("probsT_first_half")
        s_pT1 = sem("probsT_second_half")
        s_c_ps = sem("ctxT_in_psum")
        s_c = sem("ctxT_ready")
        s_o_ps = sem("attn_out_in_psum")
        s_x2 = sem("residual_stored")
        s_xn2 = sem("xn2_ready")
        s_x2T_ps = sem("xn2T_in_psum")
        s_x2T = sem("xn2T_ready")
        s_l_ps = sem("logits_in_psum")
        s_l = sem("logits_stored")
        s_st = sem("xn2_stores")
        d_in = sem("dca_rows_loaded")
        d_yT_ps = sem("dca_yT_in_psum")
        d_yT = sem("dca_yT_ready")
        d_kv_ps = sem("dca_kv_in_psum")
        d_kv = sem("dca_kv_ready")
        d_sq = sem("dca_squares_ready")
        d_kn = sem("dca_kn_ready")
        d_kT_ps = sem("dca_kT_in_psum")
        d_kT = sem("dca_kT_stored")
        d_vst = sem("dca_v_stored")

        s_iota = sem("tile_numbers_ready")
        s_xTc = [sem(f"xT_chunk_loaded{j}") for j in range(2)]
        s_u_ps = sem("shared_up_in_psum")
        s_r = sem("shared_relu_ready")
        s_hid = sem("shared_hidden_ready")
        s_d_ps = sem("shared_down_in_psum")
        s_x3 = sem("shared_added")
        s_ex = sem("router_exp_ready")
        s_oh = sem("experts_chosen")
        s_cnt_ps = sem("ranks_in_psum")
        s_cnt = sem("ranks_copied")
        s_slot = sem("slots_ready")
        s_eoff = sem("tile_experts_ready")
        s_rt = sem("routing_chain")
        s_scat = sem("rows_scattered")
        s_xt = sem("slot_tiles_loaded")
        s_eT_ps = sem("slot_tilesT_in_psum")
        s_eT = sem("slot_tilesT_ready")
        s_h_ps = sem("expert_up_in_psum")
        s_er = sem("expert_relu_ready")
        s_ea = sem("expert_act_ready")
        s_aT_ps = sem("expert_actT_in_psum")
        s_aT = sem("expert_actT_ready")
        s_y_ps = sem("expert_out_in_psum")
        s_y = sem("expert_out_ready")
        s_ys = sem("expert_out_stored")
        s_gidx = sem("gather_indices_ready")
        s_g = [sem(f"rows_gathered{h}") for h in range(2)]
        s_gc = sem("combine_chain")
        s_res = sem("result_ready")
        s_out = [sem(f"result_stored{h}") for h in range(2)]

        x_rows = x.rearrange("b s d -> (b s) d")
        out_rows = out.rearrange("b s d -> (b s) d")

        def row1(v):
            return v.rearrange("(a n) -> a n", a=1)

        def all_rows(v, n=P):
            return v.partition_broadcast(n)

        def rsqrt(ch, dve, v, r, t):
            ch.link(dve.tensor_scalar(r.bitcast(I32), v.bitcast(I32), -0.5, float(0x5F3759DF), ALU.mult, ALU.add))
            for _ in range(3):
                ch.link(dve.tensor_tensor(t, r, r, ALU.mult))
                ch.link(dve.scalar_tensor_tensor(t, t, -0.5, v, ALU.mult, ALU.mult))
                ch.link(dve.scalar_tensor_tensor(r, t, 1.5, r, ALU.add, ALU.mult))

        def kv_heads(ap):
            return ap.rearrange("p (h c d) -> p c h d", c=2, d=HD)

        def wait_alone(eng, sem_, value):
            eng.wait_ge(sem_, value)
            eng.sem_inc(s_alone, 1)

        Chain.wait_alone = staticmethod(wait_alone)

        def is_first(g):
            return isinstance(g, int) and g == 0

        ctx_ps = [bank[5], bank[7]]

        block = stack.enter_context(nc.Block())

        @block.sync
        def _(sp):
            for k in range(KC):
                sp.dma_start(wq_sb[:, k, :], Wq[k * P:(k + 1) * P, :]).then_inc(s_w, 16)
                sp.dma_start(wo_sb[:, k, :], Wo[k * P:(k + 1) * P, :]).then_inc(s_w, 16)
            sp.dma_start(wkv_sb[:, 0:D], Wk).then_inc(s_w, 16)
            sp.dma_start(wkv_sb[:, D:], Wv).then_inc(s_w, 16)
            sp.dma_start(wkvd_sb[:, :], Wkvd).then_inc(s_w, 16)
            sp.dma_start(bq_sb[:, :], all_rows(bq)).then_inc(s_w, 16)
            sp.dma_start(bkv_sb[:, 0:D], all_rows(bk)).then_inc(s_w, 16)
            sp.dma_start(bkv_sb[:, D:], all_rows(bv)).then_inc(s_w, 16)
            sp.dma_start(bkvd_sb[:, :], all_rows(bkvd)).then_inc(s_w, 16)
            sp.dma_start(bo_sb[:, :], all_rows(bo)).then_inc(s_w, 16)
            sp.dma_start(ebias_sb[:, :], all_rows(e_bias)).then_inc(s_w, 16)
            sp.dma_start(router_in[:, :], router).then_inc(s_w, 16)
            for i, v in enumerate((qn_w, qn_b, kn_w, kn_b, kd_w, kd_b)):
                sp.dma_start(ln_in[i:i + 1, :].rearrange("a (r d) -> a r d", d=HD),
                             row1(v).unsqueeze(1).to_broadcast([1, P // HD, HD])).then_inc(s_w, 16)

            ctx_dca = ctx.rearrange("(t u b) k d -> t u b k d", u=8, b=2)
            with sp.Fori(0, PAIRS // 8) as t:
                sp.wait_ge(d_vst, 32 * t)
                sp.wait_ge(d_yT_ps, t)
                for b in range(2):
                    for u in range(8):
                        sp.dma_start(y_in[u * DCA:(u + 1) * DCA, b, :],
                                     ctx[bass.ds(16 * t + (2 * u + b), 1), SM:SK, :].rearrange("a k d -> (a k) d"))\
                            .then_inc(d_in, 16)
                sp.wait_ge(d_kv, t + 1)
                for b in range(2):
                    sp.dma_start(vd_dram[bass.ds(P * t, P), b * D:(b + 1) * D], kv_sb[:, b, D:]).then_inc(d_vst, 16)
            sp.wait_ge(d_vst, 32 * (PAIRS // 8))

            def load(g):
                for u in range(2):
                    sp.dma_start(x_in[:, u, :], x_rows[bass.ds(256 * g + P * u, P), :]).then_inc(s_in, 16)
                    for b in range(2):
                        sp.dma_start(y_in[u * SM:(u + 1) * SM, b, :],
                                     ctx[bass.ds(4 * g + (2 * u + b), 1), 0:SM, :].rearrange("a k d -> (a k) d"))\
                            .then_inc(s_in, 16)

            def replicate_v(g):
                sp.wait_ge(s_kv, g + 1)
                if not is_first(g):
                    sp.wait_ge(s_vbd, g)
                for c in range(2):
                    for u in range(2):
                        sp.dma_start(v_rep[64 * c:64 * c + SM, u, :].rearrange("p (b n) -> p b n", b=2),
                                     kv_sb[u * SM:(u + 1) * SM, :, D:]).then_inc(s_v, 16)
                        sp.dma_start(v_rep[64 * c + SM:64 * c + SK, u, :],
                                     vd_dram[bass.ds(2 * DCA * g + DCA * u, DCA), :]).then_inc(s_v, 16)

            def store(g):
                sp.wait_ge(s_st, 48 * g)
                sp.wait_ge(s_xn2, g + 1)
                sp.dma_start(XN2[:, bass.ds(2 * g, 2), :], xn2[:, :, :]).then_inc(s_st, 16)
                sp.wait_ge(s_x2T, g + 1)
                for k in range(KC):
                    sp.dma_start(xn2T_dram[k, :, bass.ds(256 * g, 256)],
                                 xn2T[:, k, :, :].rearrange("p u n -> p (u n)")).then_inc(s_st, 16)

            load(0)
            replicate_v(0)

            def body(g, more):
                if more:
                    loaded = 96 * (g + 1) if isinstance(g, int) else sp.snap(96 * (g + 1))
                    sp.wait_ge(s_in, loaded)
                    sp.wait_ge(s_xn, g + 1)
                    sp.wait_ge(s_xbo, g + 1)
                    sp.wait_ge(s_yT_ps, g + 1)
                    load(g + 1)
                    replicate_v(g + 1)
                store(g)

            body(0, True)
            with sp.Fori(1, GROUPS - 1) as g:
                body(g, True)
            body(GROUPS - 1, False)

            sp.wait_ge(s_st, 48 * GROUPS)
            sp.wait_ge(s_l, GROUPS)
            with sp.Fori(0, NCH // 2) as i:
                for j in range(2):
                    sp.wait_ge(s_u_ps, 2 * NM * i)
                    sp.dma_start(xT_ch[:, j, :, :],
                                 xn2T_dram[:, :, bass.ds(SCH * 2 * i + SCH * j, SCH)].rearrange("k p n -> p k n"))\
                        .then_inc(s_xTc[j], 16)
            sp.wait_ge(s_scat, 16 * 2 * PAIRS)

            def tiles(dram, i):
                return dram[bass.ds(UNROLL * P * i, UNROLL * P), :].rearrange("(j p) d -> p j d", p=P)

            def load_tiles(i):
                if not is_first(i):
                    wait_alone(sp, s_eT_ps, i)
                    sp.wait_ge(s_xt, 16 * i)
                sp.dma_start(xt[:, :, :], tiles(slot_x, i)).then_inc(s_xt, 16)

            def store_tiles(i):
                wait_alone(sp, s_y, 2 * i + 2)
                sp.wait_ge(s_ys, 16 * i)
                sp.dma_start(tiles(slot_y, i), ey[:, :, :]).then_inc(s_ys, 16)

            load_tiles(0)
            load_tiles(1)
            with sp.Fori(0, STEPS - 2) as i:
                load_tiles(i + 2)
                store_tiles(i)
            for i in (STEPS - 2, STEPS - 1):
                store_tiles(i)
            with sp.Fori(0, PAIRS // (2 * UNROLL)) as i:
                for h in range(2):
                    sp.wait_ge(s_res, 2 * i + (h + 1))
                    sp.dma_start(out_rows[bass.ds(UNROLL * P * (2 * i + h), UNROLL * P), :]
                                 .rearrange("(j p) d -> p j d", p=P), res[:, h, :, :]).then_inc(s_out[h], 16)
            for h in range(2):
                sp.wait_ge(s_out[h], 16 * (PAIRS // (2 * UNROLL)))
            sp.wait_ge(s_alone, 5 * GROUPS + PAIRS // UNROLL + 2 * STEPS - 1)

        @block.gpsimd
        def _(pool):
            pool.memset(ones[:, :], 1.0).then_inc(s_const, 1)
            pool.memset(zeros[:, :], 0.0).then_inc(s_const, 1)
            pool.memset(ident[:, :], 0.0).then_inc(s_const, 1)
            pool.memset(stat[:, :], 1.0).then_inc(s_const, 1)
            pool.memset(kv_sb[:, :, :], 0.0).then_inc(s_const, 1)
            pool.wait_ge(s_const, 5)
            pool.affine_select(out=ident[:, :], in_=ident[:, :], compare_op=ALU.not_equal, fill=1.0, base=0,
                               pattern=[[-1, P]], channel_multiplier=1).then_inc(s_const, 1)
            pool.affine_select(out=tri[:, :], in_=ones[:, :], compare_op=ALU.is_gt, fill=0.0, base=0,
                               pattern=[[1, P]], channel_multiplier=-1).then_inc(s_const, 1)
            pool.affine_select(out=half[:, :], in_=ones[:, 0:2], compare_op=ALU.is_ge, fill=0.0, base=0,
                               pattern=[[-64, 2]], channel_multiplier=1).then_inc(s_const, 1)
            pool.affine_select(out=quad[:, :], in_=ones[:, 0:4], compare_op=ALU.is_ge, fill=0.0, base=0,
                               pattern=[[-32, 4]], channel_multiplier=1).then_inc(s_const, 1)
            pool.wait_ge(s_const, 9)
            pool.affine_select(out=half[:, :], in_=half[:, :], compare_op=ALU.is_ge, fill=0.0, base=63,
                               pattern=[[64, 2]], channel_multiplier=-1).then_inc(s_const, 1)
            pool.affine_select(out=quad[:, :], in_=quad[:, :], compare_op=ALU.is_ge, fill=0.0, base=31,
                               pattern=[[32, 4]], channel_multiplier=-1).then_inc(s_const, 1)

            def a_residual(g):
                pool.wait_ge(s_in, 96 * g + 96)
                pool.tensor_tensor(X2[:, bass.ds(2 * g, 2), :], x_in[:, :, :],
                                   bo_sb[:, :].unsqueeze(1).to_broadcast([P, 2, D]), ALU.add).then_inc(s_xbo, 1)

            def a_qn(g):
                pool.wait_ge(s_rstd, g + 1)
                if not is_first(g):
                    pool.wait_ge(s_qT_ps, 2 * g)
                for u in range(2):
                    pool.tensor_tensor(qn[:, u, :].rearrange("p (h s d) -> p h s d", h=H, s=2),
                                       q_sb[:, u, :].rearrange("p (h d) -> p h d", h=H).unsqueeze(2)
                                       .to_broadcast([P, H, 2, HD]),
                                       q_rstd2[:, u, :, :].unsqueeze(3).to_broadcast([P, H, 2, HD]),
                                       ALU.mult).then_inc(s_qn, 1)

            def a_kdca(g):
                if is_first(g):
                    pool.wait_ge(d_kT, PAIRS // 8)
                    pool.wait_ge(s_prep, 1)
                else:
                    pool.wait_ge(s_s_ps, 2 * g)
                for j in range(4):
                    last = pool.tensor_tensor(k_bd[:, :, :, j, SM:SK], kdT[:, bass.ds(2 * g, 2), :, :],
                                              quad[:, j:j + 1].unsqueeze(1).unsqueeze(1)
                                              .to_broadcast([P, 2, SETS, DCA]), ALU.mult)
                last.then_inc(s_kbdd, 1)

            def a_vbd(g):
                if not is_first(g):
                    pool.wait_ge(s_c_ps, 2 * g)
                wait_alone(pool, s_v, 128 * g + 128)
                vr = v_rep[:, :, :].rearrange("p u (n s d) -> p (u n) s d", s=2, d=HD)
                vb = v_bd[:, :, :].rearrange("p u (n s d) -> p (u n) s d", s=2, d=HD)
                for s in range(2):
                    last = pool.tensor_scalar(vb[:, :, s, :], vr[:, :, s, :], half[:, s:s + 1], None, ALU.mult)
                last.then_inc(s_vbd, 1)

            def b_normalise(g, u):
                pool.wait_ge(s_rsum, 2 * g + (u + 1))
                for c, (lo, hi) in enumerate(((0, SM), (SM, SK))):
                    last = pool.tensor_tensor(probs[:, u, :, lo:hi], probs[:, u, :, lo:hi],
                                              prec[:, u, c, :].unsqueeze(2).to_broadcast([P, H, hi - lo]), ALU.mult)
                last.then_inc(s_p, 1)

            def stage_a(g):
                a_residual(g)

            pool.wait_ge(s_w, 16 * 20)
            pool.wait_ge(s_const, N_CONST)
            a_residual(0)
            a_qn(0)
            a_kdca(0)
            a_vbd(0)

            def body(g, more):
                b_normalise(g, 0)
                if more:
                    a_residual(g + 1)
                b_normalise(g, 1)
                if more:
                    a_qn(g + 1)
                    a_kdca(g + 1)
                    a_vbd(g + 1)

            body(0, True)
            with pool.Fori(1, GROUPS - 1) as g:
                body(g, True)
            body(GROUPS - 1, False)

            pool.wait_ge(s_l, GROUPS)
            pool.iota(tile_no[:, :, :], pattern=[[1, SLOT_TILES]], base=0, channel_multiplier=0,
                      allow_small_or_imprecise_dtypes=True).then_inc(s_iota, 1)
            pool.iota(desc[:, :, :], pattern=[[-1, E]], base=E, channel_multiplier=0,
                      allow_small_or_imprecise_dtypes=True).then_inc(s_iota, 1)
            pool.wait_ge(s_slot, 1)
            pool.wait_ge(s_zero, 16)
            pool.wait_ge(s_st, 48 * GROUPS)
            for t in range(PAIRS):
                for k in range(2):
                    pool.indirect_dma_start(slot_x[:, :], bass.IndirectOffsetOnAxis(ap=slot_i[:, k, t:t + 1], axis=0),
                                            XN2[:, t, :], None).then_inc(s_scat, 16)

            pool.wait_ge(s_ys, 16 * STEPS)
            with pool.Fori(0, PAIRS // (2 * UNROLL)) as i:
                for h in range(2):
                    pool.wait_ge(s_res, 2 * i)
                    pool.tensor_copy(gidx[:, h, :, :], slot_i[:, :, bass.ds(UNROLL * (2 * i + h), UNROLL)])\
                        .then_inc(s_gidx, 1)
                    wait_alone(pool, s_gidx, 2 * i + (h + 1))
                    for j in range(UNROLL):
                        for k in range(2):
                            pool.indirect_dma_start(gath[:, h, k, j, :], None, slot_y[:, :],
                                                    bass.IndirectOffsetOnAxis(ap=gidx[:, h, k, j:j + 1], axis=0))\
                                .then_inc(s_g[h], 16)

        @block.scalar
        def _(act):
            def evac(dst, src):
                return act.activation(dst, src, ACT.Copy)

            act.dma_start(up_sb[:, :, :, :], w_up.rearrange("e (k p) i -> p e k i", p=P)).then_inc(s_w2, 16)
            act.dma_start(down_sb[:, :, :], w_down.rearrange("e i d -> i e d")).then_inc(s_w2, 16)
            act.dma_start(su_sb[:, :, :], sh_up.rearrange("(k p) n -> p k n", p=P)).then_inc(s_w2, 16)
            act.dma_start(sd_sb[:, :, :], sh_down.rearrange("(k p) n -> p k n", p=P)).then_inc(s_w2, 16)
            act.wait_ge(s_const, 5)
            act.dma_start(slot_x.rearrange("(t p) d -> p t d", p=P),
                          zeros[:, :].unsqueeze(1).to_broadcast([P, SLOT_TILES, D])).then_inc(s_zero, 16)

            act.wait_ge(s_prep_ps, 1)
            evac(ln_col[:, :], bank[4][:, 0:6]).then_inc(s_prep_ps, 1)
            evac(router_sb[:, :, :], bank[4][:, 16:16 + KC * E].rearrange("p (k e) -> p k e", k=KC))\
                .then_inc(s_prep_ps, 1)

            with act.Fori(0, PAIRS // 8) as t:
                act.wait_ge(d_yT_ps, t + 1)
                evac(yT[:, :, :], bank[4][:, 0:2 * P].rearrange("p (b n) -> p b n", b=2)).then_inc(d_yT, 1)
                act.wait_ge(d_kv, t + 1)
                act.activation(sq[:, 0, :, :], kv_sb[:, :, 0:D], ACT.Square).then_inc(d_sq, 1)
                act.wait_ge(d_kT_ps, t + 1)
                act.wait_ge(s_prep, 1)
                act.activation(kdT[:, bass.ds(8 * t, 8), :, :],
                               bank[5].rearrange("p (s u k) -> p u s k", s=SETS, u=8), ACT.Identity,
                               bias=ln_col[:, 5:6], scale=ln_col[:, 4:5]).then_inc(d_kT, 1)

            def a_transposed(g):
                act.wait_ge(s_yT_ps, g + 1)
                evac(yT[:, :, 0:MR], bank[4][:, 0:2 * MR].rearrange("p (b n) -> p b n", b=2)).then_inc(s_yT, 1)
                act.wait_ge(s_xT_ps, g + 1)
                evac(xnT[:, :, :, :], bank[6].rearrange("p (u k n) -> p u k n", u=2, k=KC)).then_inc(s_xT, 1)

            def a_squares(g):
                act.wait_ge(s_q, g + 1)
                act.activation(sq[:, 1, :, :], q_sb[:, :, :], ACT.Square).then_inc(s_sq, 1)
                act.wait_ge(s_kv, g + 1)
                act.activation(sq[0:MR, 0, :, :], kv_sb[0:MR, :, 0:D], ACT.Square).then_inc(s_sq, 1)

            def a_kbd(g):
                act.wait_ge(s_kT_ps, g + 1)
                if not is_first(g):
                    act.wait_ge(s_s_ps, 2 * g)
                src = bank[4][:, 0:SETS * MR].rearrange("p (s u k) -> p s u k", s=SETS, u=2)
                for j in range(4):
                    dst = k_bd[:, :, :, j, 0:SM].rearrange("p u s k -> p s u k")
                    last = act.activation(dst, src, ACT.Identity, bias=k_b4[:, j:j + 1], scale=k_w4[:, j:j + 1])
                last.then_inc(s_kbd, 1)

            def a_qT(g):
                for u in range(2):
                    act.wait_ge(s_qT_ps, 2 * g + (u + 1))
                    src = bank[6 + u].rearrange("p (s n) -> p s n", s=SETS)
                    for s in range(2):
                        last = act.activation(qT[:, u, :, 64 * s:64 * s + 64], src[:, :, 64 * s:64 * s + 64],
                                              ACT.Identity, bias=q_bias2[:, s:s + 1], scale=ln_col[:, 0:1])
                    last.then_inc(s_qT, 1)

            def b_exp(g, u):
                act.wait_ge(s_sub, 2 * g + (u + 1))
                act.activation(probs[:, u, :, :], probs[:, u, :, :], ACT.Exp, scale=SCALE).then_inc(s_exp, 1)

            def b_probsT(g, u):
                act.wait_ge(s_pT_ps, 4 * g + (2 * u + 1))
                if not is_first(g):
                    act.wait_ge(s_c_ps, 2 * g + (u - 1))
                evac(probsT[:, u, 0, :], bank[2]).then_inc(s_pT0, 1)

            def b_ctx(g, u):
                act.wait_ge(s_c_ps, 2 * g + (u + 1))
                evac(ctxT[:, u, :, :], ctx_ps[u][:, 0:256].rearrange("p (c n) -> p c n", c=KC))\
                    .then_inc(s_c, 1)

            def c_xn2T(g):
                act.wait_ge(s_x2T_ps, g + 1)
                if not is_first(g):
                    act.wait_ge(s_st, 48 * g)
                evac(xn2T[:, :, :, :].rearrange("p k u n -> p u k n"),
                     bank[4].rearrange("p (u k n) -> p u k n", u=2, k=KC)).then_inc(s_x2T, 1)
                act.wait_ge(s_l_ps, g + 1)
                evac(logits[:, bass.ds(2 * g, 2), :], bank[5][:, 0:2 * E].rearrange("p (u e) -> p u e", u=2))\
                    .then_inc(s_l, 1)

            a_transposed(0)
            a_squares(0)
            a_kbd(0)
            a_qT(0)

            def body(g, more):
                b_exp(g, 0)
                if more:
                    a_transposed(g + 1)
                b_exp(g, 1)
                if more:
                    a_squares(g + 1)
                b_probsT(g, 0)
                b_ctx(g, 0)
                b_probsT(g, 1)
                b_ctx(g, 1)
                if more:
                    a_kbd(g + 1)
                    a_qT(g + 1)
                c_xn2T(g)

            body(0, True)
            with act.Fori(1, GROUPS - 1) as g:
                body(g, True)
            body(GROUPS - 1, False)

            act.wait_ge(s_st, 48 * GROUPS)
            act.wait_ge(s_l, GROUPS)
            act.activation(sig[:, :, :], logits[:, :, :], ACT.Exp, scale=-1.0).then_inc(s_ex, 1)

            def shared_step(i):
                for j in range(2):
                    for m in range(NM):
                        n = j * NM + m
                        act.wait_ge(s_u_ps, 2 * NM * i + (n + 1))
                        act.activation(relu[:, n % 2, :], bank[m], ACT.Relu).then_inc(s_r, 1)
                        if m == 0 and not is_first(i):
                            act.wait_ge(s_d_ps, 2 * i - 1 + j)
                        act.wait_ge(s_r, 2 * NM * i + (n + 1))
                        act.activation(hid[:, j, m, :], relu[:, n % 2, :], ACT.Square).then_inc(s_hid, 1)

            shared_step(0)
            with act.Fori(1, NCH // 2) as i:
                shared_step(i)

            def tilesT(i):
                act.wait_ge(s_eT_ps, i + 1)
                if not is_first(i):
                    act.wait_ge(s_h_ps, i)
                for n in range(2):
                    last = evac(xtT[:, 2 * n:2 * n + 2, :, :],
                                bank[n].rearrange("p (j k n) -> p j k n", j=2, k=KC))
                last.then_inc(s_eT, 1)

            def hidden(i):
                act.wait_ge(s_h_ps, i + 1)
                if not is_first(i):
                    act.wait_ge(s_ea, i)
                act.activation(er[:, :], bank[2], ACT.Relu).then_inc(s_er, 1)

            def actT(i):
                act.wait_ge(s_aT_ps, i + 1)
                if not is_first(i):
                    act.wait_ge(s_y_ps, i)
                evac(eaT[:, :], bank[3]).then_inc(s_aT, 1)

            tilesT(0)
            hidden(0)
            tilesT(1)
            with act.Fori(0, STEPS - 2) as i:
                actT(i)
                hidden(i + 1)
                tilesT(i + 2)
            actT(STEPS - 2)
            hidden(STEPS - 1)
            actT(STEPS - 1)
            act.wait_ge(s_w2, 64)

        @block.tensor
        def _(pe):
            pe.wait_ge(s_w, 16 * 20)
            pe.wait_ge(s_const, N_CONST)
            pe.transpose(bank[4][:, 0:6], ln_in[:, :], ident[0:6, 0:6])
            for k in range(KC):
                last = pe.transpose(bank[4][:, 16 + k * E:16 + (k + 1) * E], router_in[:, k * P:(k + 1) * P],
                                    ident[0:E, 0:E])
            last.then_inc(s_prep_ps, 1)
            pe.wait_ge(s_prep_ps, 3)

            with pe.Fori(0, PAIRS // 8) as t:
                pe.wait_ge(d_in, 256 * t + 256)
                for b in range(2):
                    last = pe.transpose(bank[4][:, b * P:(b + 1) * P], y_in[:, b, :], ident[:, :])
                last.then_inc(d_yT_ps, 1)
                pe.wait_ge(d_yT, t + 1)
                pe.wait_ge(s_prep, 1)
                for b in range(2):
                    last = pe.matmul(bank[6 + b], yT[:, b, :], wkvd_sb[:, :], start=True, stop=True)
                last.then_inc(d_kv_ps, 1)
                pe.wait_ge(d_kn, t + 1)
                for s in range(SETS):
                    last = pe.transpose(bank[5][:, s * P:(s + 1) * P], kn[:, s * P:(s + 1) * P], ident[:, :])
                last.then_inc(d_kT_ps, 1)
                pe.wait_ge(d_kT, t + 1)

            def a_transposes(g):
                pe.wait_ge(s_in, 96 * g + 96)
                if not is_first(g):
                    pe.wait_ge(s_x2T, g - 1)
                for b in range(2):
                    last = pe.transpose(bank[4][:, b * MR:(b + 1) * MR], y_in[0:MR, b, :], ident[0:MR, 0:MR])
                last.then_inc(s_yT_ps, 1)
                pe.wait_ge(s_xn, g + 1)
                if not is_first(g):
                    pe.wait_ge(s_qT, 2 * g)
                for u in range(2):
                    for k in range(KC):
                        last = pe.transpose(bank[6][:, (u * KC + k) * P:(u * KC + k + 1) * P],
                                            xn[:, u, k * P:(k + 1) * P], ident[:, :])
                last.then_inc(s_xT_ps, 1)

            def a_project(g):
                pe.wait_ge(s_xT, g + 1)
                if not is_first(g):
                    pe.wait_ge(s_l, g - 1)
                for u in range(2):
                    for k in range(KC):
                        last = pe.matmul(bank[5][:, u * D:(u + 1) * D], xnT[:, u, k, :], wq_sb[:, k, :],
                                         start=(k == 0), stop=(k == KC - 1))
                last.then_inc(s_q_ps, 1)
                pe.wait_ge(s_yT, g + 1)
                for b in range(2):
                    last = pe.matmul(bank[6 + b][0:MR, :], yT[:, b, 0:MR], wkv_sb[:, :], start=True, stop=True)
                last.then_inc(s_kv_ps, 1)

            def a_heads(g):
                pe.wait_ge(s_kn, g + 1)
                for s in range(SETS):
                    last = pe.transpose(bank[4][:, s * MR:(s + 1) * MR], kn[0:MR, s * P:(s + 1) * P],
                                        ident[0:MR, 0:MR])
                last.then_inc(s_kT_ps, 1)
                for u in range(2):
                    pe.wait_ge(s_qn, 2 * g + (u + 1))
                    for s in range(SETS):
                        last = pe.transpose(bank[6 + u][:, s * P:(s + 1) * P], qn[:, u, s * P:(s + 1) * P],
                                            ident[:, :])
                    last.then_inc(s_qT_ps, 1)

            def b_scores(g, u):
                pe.wait_ge(s_qT, 2 * g + (u + 1))
                if u == 0:
                    pe.wait_ge(s_kbd, g + 1)
                    pe.wait_ge(s_kbdd, g + 1)
                if u or not is_first(g):
                    pe.wait_ge(s_sub, 2 * g + u)
                for s in range(SETS):
                    last = pe.matmul(score_ps[:, s * CW:(s + 1) * CW], qT[:, u, s, :],
                                     k_bd[:, u, s, :, :].rearrange("p j k -> p (j k)"), start=True, stop=True)
                last.then_inc(s_s_ps, 1)

            def b_probs_v(g, u):
                pe.wait_ge(s_p, 2 * g + (u + 1))
                if u == 0:
                    pe.wait_ge(s_vbd, g + 1)
                if u == 0:
                    if not is_first(g):
                        pe.wait_ge(s_x2, 2 * g)
                else:
                    pe.wait_ge(s_pT0, 2 * g + 1)
                    pe.wait_ge(s_pT1, 2 * g + 1)
                flat = probs[:, u, :, :].rearrange("p h k -> p (h k)")
                for c in range(2):
                    for n in range(HP // 2):
                        i = c * (HP // 2) + n
                        last = pe.transpose(bank[2 + c][:, n * P:(n + 1) * P], flat[:, i * P:(i + 1) * P], ident[:, :])
                    last.then_inc(s_pT_ps, 1)
                for c in range(2):
                    pe.wait_ge(s_pT1 if c else s_pT0, 2 * g + (u + 1))
                    for n in range(HP // 2):
                        for b in range(2):
                            col = P * c + 64 * b
                            last = pe.matmul(ctx_ps[u][32 * n:32 * n + 32, col:col + 64],
                                             v_bd[:, u, b * D + (4 * c + n) * 32:b * D + (4 * c + n) * 32 + 32],
                                             probsT[:, u, c, n * P + 64 * b:n * P + 64 * b + 64],
                                             start=True, stop=True)
                last.then_inc(s_c_ps, 1)

            def c_out(g):
                for u in range(2):
                    pe.wait_ge(s_c, 2 * g + (u + 1))
                    if u == 0:
                        pe.wait_ge(s_pT0, 2 * g + 2)
                        pe.wait_ge(s_pT1, 2 * g + 2)
                    for k in range(KC):
                        last = pe.matmul(bank[2 + u][:, 0:D], ctxT[:, u, k, :], wo_sb[:, k, :],
                                         start=(k == 0), stop=(k == KC - 1))
                    last.then_inc(s_o_ps, 1)

            def c_router(g, more):
                pe.wait_ge(s_xn2, g + 1)
                if more:
                    pe.wait_ge(s_kbd, g + 2)
                for u in range(2):
                    for k in range(KC):
                        last = pe.transpose(bank[4][:, (u * KC + k) * P:(u * KC + k + 1) * P],
                                            xn2[:, u, k * P:(k + 1) * P], ident[:, :])
                last.then_inc(s_x2T_ps, 1)
                pe.wait_ge(s_x2T, g + 1)
                for u in range(2):
                    for k in range(KC):
                        last = pe.matmul(bank[5][:, u * E:(u + 1) * E], xn2T[:, k, u, :], router_sb[:, k, :],
                                         start=(k == 0), stop=(k == KC - 1))
                last.then_inc(s_l_ps, 1)

            a_transposes(0)
            a_project(0)
            a_heads(0)

            def body(g, more):
                b_scores(g, 0)
                if more:
                    a_transposes(g + 1)
                b_scores(g, 1)
                if more:
                    a_project(g + 1)
                    pe.wait_ge(s_q, g + 2)
                    pe.wait_ge(s_kv, g + 2)
                b_probs_v(g, 0)
                b_probs_v(g, 1)
                c_out(g)
                if more:
                    a_heads(g + 1)
                c_router(g, more)

            body(0, True)
            with pe.Fori(1, GROUPS - 1) as g:
                body(g, True)
            body(GROUPS - 1, False)

            pe.wait_ge(s_w2, 64)
            pe.wait_ge(s_l, GROUPS)

            def shared_up(i, j):
                pe.wait_ge(s_xTc[j], 16 * i + 16)
                for m in range(NM):
                    if j or not is_first(i):
                        pe.wait_ge(s_r, 2 * NM * i + (j * NM + m + 1 - NM))
                    for k in range(KC):
                        last = pe.matmul(bank[m], su_sb[:, k, m * P:(m + 1) * P], xT_ch[:, j, k, :],
                                         start=(k == 0), stop=(k == KC - 1))
                    last.then_inc(s_u_ps, 1)

            def shared_down(i, j):
                pe.wait_ge(s_hid, 2 * NM * i + NM * (j + 1))
                if not is_first(i):
                    pe.wait_ge(s_x3, 2 * i - 1 + j)
                for t in range(SCH // P):
                    o = bank[4 + 2 * j + t // 2][:, (t % 2) * D:(t % 2 + 1) * D]
                    for m in range(NM):
                        last = pe.matmul(o, hid[:, j, m, t * P:(t + 1) * P], sd_sb[:, m, :],
                                         start=(m == 0), stop=(m == NM - 1))
                last.then_inc(s_d_ps, 1)

            def shared_step(i):
                shared_up(i, 0)
                shared_up(i, 1)
                shared_down(i, 0)
                shared_down(i, 1)

            shared_step(0)
            pe.wait_ge(s_oh, 1)
            chosen = etmp[:, :, :].rearrange("p t e -> p (t e)")
            pe.wait_ge(s_r, 2 * NM)
            pe.matmul(bank[0], tri[:, :], chosen, start=True, stop=True)
            pe.matmul(bank[1], ones[:, :], chosen, start=True, stop=True).then_inc(s_cnt_ps, 1)
            pe.wait_ge(s_cnt, 1)
            with pe.Fori(1, NCH // 2) as i:
                shared_step(i)

            pe.wait_ge(s_eoff, 1)
            pe.wait_ge(s_r, NM * NCH)
            pe.wait_ge(s_x3, NCH)
            up_w = up_sb[:, :, :, :].rearrange("p e k i -> p (e k i)")
            down_w = down_sb[:, :, :].rearrange("p e d -> p (e d)")

            def tilesT(i):
                pe.wait_ge(s_xt, 16 * i + 16)
                if not is_first(i):
                    pe.wait_ge(s_eT, i)
                for j in range(UNROLL):
                    for k in range(KC):
                        last = pe.transpose(bank[j // 2][:, ((j % 2) * KC + k) * P:((j % 2) * KC + k + 1) * P],
                                            xt[:, j, k * P:(k + 1) * P], ident[:, :])
                last.then_inc(s_eT_ps, 1)

            def expert_offset(i, j):
                return pe.value_load(eoff_i[0:1, bass.ds(UNROLL * i + j, 1)], min_val=0, max_val=(E - 1) * D)

            def up(i):
                pe.wait_ge(s_eT, i + 1)
                if not is_first(i):
                    pe.wait_ge(s_ea, i)
                for j in range(UNROLL):
                    off = expert_offset(i, j)
                    for k in range(KC):
                        last = pe.matmul(bank[2][:, j * MI:(j + 1) * MI], xtT[:, j, k, :],
                                         up_w[:, bass.ds(off + k * MI, MI)], start=(k == 0), stop=(k == KC - 1))
                last.then_inc(s_h_ps, 1)

            def actT(i):
                pe.wait_ge(s_ea, i + 1)
                if not is_first(i):
                    pe.wait_ge(s_aT, i)
                for j in range(UNROLL):
                    last = pe.transpose(bank[3][:, j * P:(j + 1) * P], ea[:, j * MI:(j + 1) * MI], ident[:, :])
                last.then_inc(s_aT_ps, 1)

            def down(i):
                pe.wait_ge(s_aT, i + 1)
                if not is_first(i):
                    pe.wait_ge(s_y, 2 * i)
                for j in range(UNROLL):
                    off = expert_offset(i, j)
                    last = pe.matmul(bank[4 + j // 2][:, (j % 2) * D:(j % 2 + 1) * D], eaT[:, j * P:(j + 1) * P],
                                     down_w[:, bass.ds(off, D)], start=True, stop=True)
                last.then_inc(s_y_ps, 1)

            tilesT(0)
            up(0)
            tilesT(1)
            with pe.Fori(0, STEPS - 2) as i:
                actT(i)
                up(i + 1)
                tilesT(i + 2)
                down(i)
            actT(STEPS - 2)
            up(STEPS - 1)
            down(STEPS - 2)
            actT(STEPS - 1)
            down(STEPS - 1)

        @block.vector
        def _(dve):
            dve.wait_ge(s_w, 16 * 20)
            dve.wait_ge(s_const, N_CONST)
            ch = Chain(dve, s_ch, 17, 0)
            centred = [wq_sb[:, 0, :], wq_sb[:, 1, :], wkvd_sb[:, 0:D], bq_sb[:, :], bkvd_sb[:, 0:D]]
            heads = [w.rearrange("p (h d) -> p h d", h=H) for w in centred] + \
                    [kv_heads(w)[:, 0, :, :] for w in (wkv_sb[:, :], bkv_sb[:, :])]
            for i, w in enumerate(heads):
                k = ch.done(dve.tensor_reduce(wmean[:, i, :], w, AX.X, ALU.add))
            ch.need(k)
            ch.link(dve.tensor_scalar(wmean[:, :, :], wmean[:, :, :], -1.0 / HD, None, ALU.mult))
            for i, w in enumerate(heads):
                k = ch.done(dve.tensor_tensor(w, w, wmean[:, i, :].unsqueeze(2).to_broadcast([P, H, HD]), ALU.add))
            iv = ident[:, :].rearrange("p (j s d) -> p s j d", s=2, d=HD)
            for s in range(2):
                k = ch.done(dve.tensor_reduce(slotm[:, s:s + 1], iv[:, s, :, :], AX.XY, ALU.add))
            dve.wait_ge(s_prep_ps, 3)
            ch.need(k)
            dve.tensor_scalar(q_bias2[:, :], slotm[:, :], ln_col[:, 1:2], None, ALU.mult)
            dve.tensor_scalar(k_w4[:, :], quad[:, :], ln_col[:, 2:3], None, ALU.mult)
            dve.tensor_scalar(k_b4[:, :], quad[:, :], ln_col[:, 3:4], None, ALU.mult).then_inc(s_prep, 1)
            ch.end()

            with dve.Fori(0, PAIRS // 8) as t:
                ch = Chain(dve, s_chd, 12, t)
                dve.wait_ge(d_kv_ps, t + 1)
                dve.wait_ge(d_vst, 32 * t)
                for b in range(2):
                    last = dve.tensor_tensor(kv_sb[:, b, :], bank[6 + b], bkvd_sb[:, :], ALU.add)
                last.then_inc(d_kv, 1)
                dve.wait_ge(d_sq, t + 1)
                ch.link(dve.tensor_reduce(stat[:, 0:32], sq[:, 0, :, :].rearrange("p b (h d) -> p (b h) d", d=HD),
                                          AX.X, ALU.add))
                ch.link(dve.tensor_scalar(rst[:, 0, 0:32], stat[:, 0:32], 1.0 / HD, EPS_HEAD, ALU.mult, ALU.add))
                rsqrt(ch, dve, rst[:, 0, 0:32], rst[:, 1, 0:32], rst[:, 2, 0:32])
                dve.wait_ge(d_kT_ps, t)
                dve.tensor_tensor(kn[:, :].rearrange("p (h b d) -> p b h d", h=H, b=2),
                                  kv_sb[:, :, 0:D].rearrange("p b (h d) -> p b h d", h=H),
                                  rst[:, 1, 0:32].rearrange("p (b h) -> p b h", b=2).unsqueeze(3)
                                  .to_broadcast([P, 2, H, HD]), ALU.mult).then_inc(d_kn, 1)
                ch.end()

            def a_ln1_stats(g, ch):
                dve.wait_ge(s_in, 96 * g + 96)
                for u in range(2):
                    k = ch.done(dve.bn_stats(bn[:, u, :], x_in[:, u, :]))
                ch.need_alone(k)
                for u in range(2):
                    k = ch.done(dve.bn_aggr(mv[:, u, :], bn[:, u, :]))
                ch.need(k)
                ch.link(dve.tensor_scalar(lr[:, 0, :], mv[:, :, 1], EPS_LN, None, ALU.add))

            def a_ln1(g, ch):
                rsqrt(ch, dve, lr[:, 0, :], lr[:, 1, :], lr[:, 2, :])
                if not is_first(g):
                    dve.wait_ge(s_xT_ps, g)
                for u in range(2):
                    last = dve.tensor_scalar(xn[:, u, :], x_in[:, u, :], mv[:, u, 0:1], lr[:, 1, u:u + 1],
                                             ALU.subtract, ALU.mult)
                last.then_inc(s_xn, 1)

            def a_evacuate(g):
                dve.wait_ge(s_q_ps, g + 1)
                if not is_first(g):
                    dve.wait_ge(s_qn, 2 * g)
                dve.tensor_tensor(q_sb[:, :, :], bank[5].rearrange("p (u n) -> p u n", u=2),
                                  bq_sb[:, :].unsqueeze(1).to_broadcast([P, 2, D]), ALU.add).then_inc(s_q, 1)
                dve.wait_ge(s_kv_ps, g + 1)
                if is_first(g):
                    dve.wait_ge(d_vst, 32 * (PAIRS // 8))
                else:
                    dve.wait_ge(s_v, 128 * g)
                for b in range(2):
                    last = dve.tensor_tensor(kv_sb[0:MR, b, :].rearrange("p (c h d) -> p c h d", c=2, h=H),
                                             kv_heads(bank[6 + b][0:MR, :]), kv_heads(bkv_sb[0:MR, :]), ALU.add)
                last.then_inc(s_kv, 1)

            def a_head_vars(g, ch):
                dve.wait_ge(s_sq, 2 * g + 2)
                ch.done(dve.tensor_reduce(stat[:, 32:64], sq[:, 1, :, :].rearrange("p b (h d) -> p (b h) d", d=HD),
                                          AX.X, ALU.add))
                ch.link(dve.tensor_reduce(stat[0:MR, 0:32],
                                          sq[0:MR, 0, :, :].rearrange("p b (h d) -> p (b h) d", d=HD),
                                          AX.X, ALU.add))
                ch.link(dve.tensor_scalar(rst[:, 0, :], stat[:, :], 1.0 / HD, EPS_HEAD, ALU.mult, ALU.add))

            def a_normalise(g, ch):
                rsqrt(ch, dve, rst[:, 0, :], rst[:, 1, :], rst[:, 2, :])
                dve.tensor_tensor(q_rstd2[:, :, :, :].rearrange("p u h s -> p (u h) s"),
                                  rst[:, 1, 32:64].unsqueeze(2).to_broadcast([P, 32, 2]),
                                  half[:, :].unsqueeze(1).to_broadcast([P, 32, 2]), ALU.mult).then_inc(s_rstd, 1)
                if is_first(g):
                    dve.wait_ge(d_kT_ps, PAIRS // 8)
                else:
                    dve.wait_ge(s_kT_ps, g)
                dve.tensor_tensor(kn[0:MR, :].rearrange("p (h b d) -> p b h d", h=H, b=2),
                                  kv_sb[0:MR, :, 0:D].rearrange("p b (h d) -> p b h d", h=H),
                                  rst[0:MR, 1, 0:32].rearrange("p (b h) -> p b h", b=2).unsqueeze(3)
                                  .to_broadcast([MR, 2, H, HD]), ALU.mult).then_inc(s_kn, 1)

            parts = ((0, SM), (SM, SK))
            scores = score_ps[:, :].rearrange("p (h k) -> p h k", k=SK)

            def b_subtract_max(g, u, ch):
                dve.wait_ge(s_s_ps, 2 * g + (u + 1))
                for c, (lo, hi) in enumerate(parts):
                    k = ch.done(dve.tensor_reduce(pmax[:, u, c, :], scores[:, :, lo:hi], AX.X, ALU.max))
                ch.need(k)
                if not is_first(g):
                    dve.wait_ge(s_pT_ps, 4 * g + (2 * u - 2))
                for c, (lo, hi) in enumerate(parts):
                    last = dve.tensor_tensor(probs[:, u, :, lo:hi], scores[:, :, lo:hi],
                                             pmax[:, u, c, :].unsqueeze(2).to_broadcast([P, H, hi - lo]), ALU.subtract)
                last.then_inc(s_sub, 1)

            def b_sums(g, u, ch):
                dve.wait_ge(s_exp, 2 * g + (u + 1))
                for c, (lo, hi) in enumerate(parts):
                    k = ch.done(dve.tensor_reduce(psum_[:, u, c, :], probs[:, u, :, lo:hi], AX.X, ALU.add))
                ch.need(k)
                if not is_first(g):
                    dve.wait_ge(s_p, 2 * g + (u - 1))
                dve.reciprocal(prec[:, u, :, :], psum_[:, u, :, :]).then_inc(s_rsum, 1)

            def b_probsT(g, u):
                dve.wait_ge(s_pT_ps, 4 * g + (2 * u + 2))
                if not is_first(g):
                    dve.wait_ge(s_c_ps, 2 * g + (u - 1))
                dve.tensor_copy(probsT[:, u, 1, :], bank[3]).then_inc(s_pT1, 1)

            def c_residual(g, ch):
                dve.wait_ge(s_xbo, g + 1)
                for u in range(2):
                    dve.wait_ge(s_o_ps, 2 * g + (u + 1))
                    row = X2[:, bass.ds(2 * g + u, 1), :].rearrange("p a n -> p (a n)")
                    dve.tensor_tensor(row, bank[2 + u][:, 0:D], row, ALU.add).then_inc(s_x2, 1)
                    wait_alone(dve, s_x2, 2 * g + (u + 1))
                    k = ch.done(dve.bn_stats(bn2[:, u, :], row))
                ch.need_alone(k)
                for u in range(2):
                    k = ch.done(dve.bn_aggr(mv2[:, u, :], bn2[:, u, :]))
                ch.need(k)
                ch.link(dve.tensor_scalar(lr2[:, 0, :], mv2[:, :, 1], EPS_LN, None, ALU.add))
                rsqrt(ch, dve, lr2[:, 0, :], lr2[:, 1, :], lr2[:, 2, :])
                if not is_first(g):
                    dve.wait_ge(s_x2T_ps, g)
                    dve.wait_ge(s_st, 48 * g)
                for u in range(2):
                    row = X2[:, bass.ds(2 * g + u, 1), :].rearrange("p a n -> p (a n)")
                    last = dve.tensor_scalar(xn2[:, u, :], row, mv2[:, u, 0:1], lr2[:, 1, u:u + 1],
                                             ALU.subtract, ALU.mult)
                last.then_inc(s_xn2, 1)

            NA, NBC = 28, 23
            ch = Chain(dve, s_cha, NA, 0)
            a_ln1_stats(0, ch)
            a_ln1(0, ch)
            a_evacuate(0)
            a_head_vars(0, ch)
            a_normalise(0, ch)
            ch.end()

            def body(g, more):
                ca = Chain(dve, s_cha, NA, g + 1)
                cb = Chain(dve, s_chb, NBC, g)
                b_subtract_max(g, 0, cb)
                if more:
                    a_ln1_stats(g + 1, ca)
                b_sums(g, 0, cb)
                if more:
                    a_ln1(g + 1, ca)
                b_subtract_max(g, 1, cb)
                if more:
                    a_evacuate(g + 1)
                b_sums(g, 1, cb)
                if more:
                    a_head_vars(g + 1, ca)
                b_probsT(g, 0)
                if more:
                    a_normalise(g + 1, ca)
                    ca.end()
                b_probsT(g, 1)
                c_residual(g, cb)
                cb.end()

            body(0, True)
            with dve.Fori(1, GROUPS - 1) as g:
                body(g, True)
            body(GROUPS - 1, False)

            dve.wait_ge(s_st, 48 * GROUPS)
            dve.wait_ge(s_ex, 1)
            dve.wait_ge(s_iota, 2)
            ch = Chain(dve, s_rt, 74, 0)
            link = ch.link

            def by_tile(v, n):
                return v.unsqueeze(2).to_broadcast([P, PAIRS, n])

            link(dve.tensor_scalar(sig[:, :, :], sig[:, :, :], 1.0, None, ALU.add))
            link(dve.reciprocal(sig[:, :, :], sig[:, :, :]))
            link(dve.tensor_tensor(sel[:, :, :], sig[:, :, :],
                                   ebias_sb[:, :].unsqueeze(1).to_broadcast([P, PAIRS, E]), ALU.add))
            s4 = sel[:, :, :].rearrange("p t (g e) -> p (t g) e", e=GSZ)
            ch.done(dve.tensor_tensor(pair_sums[:, :, 0:2], s4[:, :, 0:2], s4[:, :, 2:4], ALU.add))
            ch.done(dve.tensor_tensor(pair_sums[:, :, 2:3], s4[:, :, 0:1], s4[:, :, 3:4], ALU.add))
            ch.done(dve.tensor_tensor(pair_sums[:, :, 3:4], s4[:, :, 1:2], s4[:, :, 2:3], ALU.add))
            link(dve.tensor_tensor(pair_sums[:, :, 4:6], s4[:, :, 0:4:2], s4[:, :, 1:4:2], ALU.add))
            gs = gsum[:, :, :]
            link(dve.tensor_reduce(gs.rearrange("p t g -> p (t g)"), pair_sums[:, :, :], AX.X, ALU.max))

            def argmax(values, tmp, onehot, n):
                first = desc[:, :, E - n:E].to_broadcast([P, PAIRS, n])
                link(dve.tensor_reduce(top[:, :], values, AX.X, ALU.max))
                link(dve.tensor_tensor(tmp, values, by_tile(top[:, :], n), ALU.is_equal))
                link(dve.tensor_tensor(tmp, tmp, first, ALU.mult))
                link(dve.tensor_reduce(top[:, :], tmp, AX.X, ALU.max))
                link(dve.tensor_tensor(onehot, tmp, by_tile(top[:, :], n), ALU.is_equal))

            argmax(gs, gtmp[:, :, :], goh[:, 0, :, :], NG)
            link(dve.scalar_tensor_tensor(gs, goh[:, 0, :, :], -BIG, gs, ALU.mult, ALU.add))
            argmax(gs, gtmp[:, :, :], goh[:, 1, :, :], NG)
            link(dve.tensor_tensor(gtmp[:, :, :], goh[:, 0, :, :], goh[:, 1, :, :], ALU.add))
            link(dve.tensor_tensor(s4, s4, gtmp[:, :, :].rearrange("p t g -> p (t g)").unsqueeze(2)
                                   .to_broadcast([P, PAIRS * NG, GSZ]), ALU.mult))
            argmax(sel[:, :, :], etmp[:, :, :], oh[:, 0, :, :], E)
            link(dve.scalar_tensor_tensor(sel[:, :, :], oh[:, 0, :, :], -BIG, sel[:, :, :], ALU.mult, ALU.add))
            argmax(sel[:, :, :], etmp[:, :, :], oh[:, 1, :, :], E)
            dve.tensor_tensor(etmp[:, :, :], oh[:, 0, :, :], oh[:, 1, :, :], ALU.add).then_inc(s_oh, 1)
            for k in range(2):
                link(dve.tensor_tensor(sel[:, :, :], sig[:, :, :], oh[:, k, :, :], ALU.mult))
                link(dve.tensor_reduce(gate[:, k, :], sel[:, :, :], AX.X, ALU.add))
            link(dve.tensor_tensor(gate[:, 2, :], gate[:, 0, :], gate[:, 1, :], ALU.add))
            link(dve.tensor_scalar(gate[:, 2, :], gate[:, 2, :], 1e-20, None, ALU.add))
            link(dve.reciprocal(gate[:, 2, :], gate[:, 2, :]))
            link(dve.tensor_tensor(gate[:, 0:2, :], gate[:, 0:2, :],
                                   gate[:, 2, :].unsqueeze(1).to_broadcast([P, 2, PAIRS]), ALU.mult))

            def shared_add(i, j):
                dve.wait_ge(s_d_ps, 2 * i + (j + 1))
                for n in range(2):
                    rows = X2[:, bass.ds(8 * i + (4 * j + 2 * n), 2), :]
                    last = dve.tensor_tensor(rows, bank[4 + 2 * j + n].rearrange("p (t d) -> p t d", t=2), rows,
                                             ALU.add)
                last.then_inc(s_x3, 1)

            shared_add(0, 0)
            shared_add(0, 1)

            dve.wait_ge(s_cnt_ps, 1)
            ch.done(dve.tensor_copy(sel[:, :, :].rearrange("p t e -> p (t e)"), bank[0]))
            k = ch.done(dve.tensor_copy(sig[:, :, :].rearrange("p t e -> p (t e)"), bank[1]))
            ch.need(k)
            dve.tensor_copy(etmp[:, 0, :], sig[:, 0, :]).then_inc(s_cnt, 1)
            scan = [sig[:, :, :], etmp[:, :, :]]
            step, cur = 1, 0
            dve.wait_ge(s_cnt, 1)
            third = pair_sums[:, :, :].rearrange("p a b -> p (a b)")[:, 0:PAIRS * E].rearrange("p (t e) -> p t e", e=E)
            src = sig[:, :, :]
            dsts = [etmp[:, :, :], third]
            while step < PAIRS:
                dst = dsts[cur % 2]
                ch.done(dve.tensor_copy(dst[:, 0:step, :], src[:, 0:step, :]))
                link(dve.tensor_tensor(dst[:, step:, :], src[:, step:, :], src[:, 0:PAIRS - step, :], ALU.add))
                src, step, cur = dst, 2 * step, cur + 1
            link(dve.tensor_tensor(sel[:, :, :], sel[:, :, :], src, ALU.add))
            link(dve.tensor_tensor(sel[:, :, :], sel[:, :, :], sig[:, :, :], ALU.subtract))
            link(dve.tensor_scalar(count_i[:, 0, :], src[:, PAIRS - 1, :], float(P - 1), None, ALU.add))
            link(dve.tensor_scalar(count_i[:, 1, :], count_i[:, 0, :], 7, None, ALU.logical_shift_right))
            link(dve.tensor_copy(count[:, 0, :], count_i[:, 1, :]))
            step, cur = 1, 0
            while step < E:
                ch.done(dve.tensor_copy(count[:, cur + 1, 0:step], count[:, cur, 0:step]))
                link(dve.tensor_tensor(count[:, cur + 1, step:], count[:, cur, step:], count[:, cur, 0:E - step],
                                       ALU.add))
                step, cur = 2 * step, cur + 1
            ends = count[:, cur, :]
            link(dve.tensor_tensor(count[:, 5, :], ends, count[:, 0, :], ALU.subtract))
            link(dve.tensor_scalar(count[:, 5, :], count[:, 5, :], float(P), None, ALU.mult))
            link(dve.tensor_tensor(sel[:, :, :], sel[:, :, :],
                                   count[:, 5, :].unsqueeze(1).to_broadcast([P, PAIRS, E]), ALU.add))
            for k in range(2):
                link(dve.tensor_tensor(etmp[:, :, :], sel[:, :, :], oh[:, k, :, :], ALU.mult))
                link(dve.tensor_reduce(slot[:, k, :], etmp[:, :, :], AX.X, ALU.add))
            dve.tensor_copy(slot_i[:, :, :], slot[:, :, :]).then_inc(s_slot, 1)
            link(dve.tensor_tensor(past[:, :, :], tile_no[:, :, :].to_broadcast([1, SLOT_TILES, E]),
                                   ends[0:1, :].unsqueeze(1).to_broadcast([1, SLOT_TILES, E]), ALU.is_ge))
            link(dve.tensor_reduce(eoff[:, :], past[:, :, :], AX.X, ALU.add))
            dve.tensor_scalar(eoff_i[:, :], eoff[:, :], float(E - 1), float(D), ALU.min, ALU.mult).then_inc(s_eoff, 1)
            ch.end()

            with dve.Fori(1, NCH // 2) as i:
                for j in range(2):
                    shared_add(i, j)

            def expert_act(i):
                dve.wait_ge(s_er, i + 1)
                if not is_first(i):
                    dve.wait_ge(s_aT_ps, i)
                dve.scalar_tensor_tensor(ea[:, :], bank[2], 0.0, er[:, :], ALU.max, ALU.mult).then_inc(s_ea, 1)

            def expert_out(i):
                dve.wait_ge(s_y_ps, i + 1)
                if not is_first(i):
                    dve.wait_ge(s_ys, 16 * i)
                for n in range(2):
                    dve.tensor_copy(ey[:, 2 * n:2 * n + 2, :], bank[4 + n].rearrange("p (j d) -> p j d", j=2))\
                       .then_inc(s_y, 1)

            expert_act(0)
            with dve.Fori(0, STEPS - 1) as i:
                expert_act(i + 1)
                expert_out(i)
            expert_out(STEPS - 1)

            with dve.Fori(0, PAIRS // (2 * UNROLL)) as i:
                for h in range(2):
                    dve.wait_ge(s_g[h], 16 * 2 * UNROLL * (i + 1))
                    dve.wait_ge(s_out[h], 16 * i)
                    for j in range(UNROLL):
                        t = 2 * UNROLL * i + (UNROLL * h + j)
                        last = dve.scalar_tensor_tensor(res[:, h, j, :], gath[:, h, 0, j, :], gate[:, 0, bass.ds(t, 1)],
                                                        X2[:, bass.ds(t, 1), :].rearrange("p a d -> p (a d)"),
                                                        ALU.mult, ALU.add)
                    last.then_inc(s_gc, 1)
                    dve.wait_ge(s_gc, 2 * i + (h + 1))
                    for j in range(UNROLL):
                        t = 2 * UNROLL * i + (UNROLL * h + j)
                        last = dve.scalar_tensor_tensor(res[:, h, j, :], gath[:, h, 1, j, :], gate[:, 1, bass.ds(t, 1)],
                                                        res[:, h, j, :], ALU.mult, ALU.add)
                    last.then_inc(s_res, 1)


_INS = ['x', 'ctx_1024', 'L0_xattn_Wq', 'L0_xattn_bq', 'L0_xattn_Wk', 'L0_xattn_bk', 'L0_xattn_Wv', 'L0_xattn_bv',
        'L0_xattn_Wkv_dca', 'L0_xattn_bkv_dca', 'L0_xattn_qn_w', 'L0_xattn_qn_b', 'L0_xattn_kn_w', 'L0_xattn_kn_b',
        'L0_xattn_kn_dca_w', 'L0_xattn_kn_dca_b', 'L0_xattn_Wo', 'L0_xattn_bo', 'L0_ffn_router_weight',
        'L0_ffn_e_bias', 'L0_ffn_w_up', 'L0_ffn_w_down', 'L0_ffn_shared_up', 'L0_ffn_shared_down']


def kernel(**inputs):
    import numpy as _np
    import concourse.bacc as _bacc
    from concourse import mybir as _mybir
    from concourse.bass_utils import run_bass_kernel_spmd as _run

    nc = _bacc.Bacc("TRN2", target_bir_lowering=False, num_devices=1)
    arrays, args = {}, []
    for name in _INS:
        a = _np.ascontiguousarray(inputs[name])
        arrays[f"in_{name}"] = a
        args.append(nc.dram_tensor(f"in_{name}", a.shape, _mybir.dt.from_np(a.dtype), kind="ExternalInput").ap())
    args.append(nc.dram_tensor("out_0", (NB, SQ, D), F32, kind="ExternalOutput").ap())
    xattn_moe(nc, *args)
    r = _run(nc, [arrays], core_ids=[0])
    return r.results[0]["out_0"]
```

```python
from contextlib import ExitStack

import concourse.bass as bass
from concourse import mybir

F32 = mybir.dt.float32
I32 = mybir.dt.int32
ALU = mybir.AluOpType
ACT = mybir.ActivationFunctionType
AX = mybir.AxisListType

P = 128
NB, SQ, D = 64, 64, 256
SK, KD = 64, 128
DCA = 16
SM = SK - DCA
H = 16
HD = D // H
SCALE = HD ** -0.5
EPS_HEAD = 1e-6
EPS_LN = 1e-5
E, MI, SI = 16, 128, 512
NG, GSZ = 4, 4
PAIRS = NB // 2
GROUPS = PAIRS // 2
SETS = H // 4
MR = 2 * SM
CW = 4 * SK
HP = H // 2
SLOT_TILES = 80
N_CONST = 12
DT = PAIRS // 8
UNROLL = 4
SLOTS = SLOT_TILES * P
KC = D // P
SCH = 512
NCH = NB * SQ // SCH
NM = SI // P
STEPS = SLOT_TILES // (2 * UNROLL)
LAST_SH = NCH // 2 - 1
BIG = 1e30


class Chain:

    def __init__(self, eng, sem, per_step, step):
        self.eng, self.sem, self.per, self.n = eng, sem, per_step, 0
        self.base = step * per_step

    def done(self, ins):
        self.n += 1
        ins.then_inc(self.sem, 1)
        return self.n

    def need(self, k):
        self.eng.wait_ge(self.sem, self.base + k)

    def need_alone(self, k):
        self.wait_alone(self.eng, self.sem, self.base + k)

    def link(self, ins):
        self.need(self.done(ins))

    def end(self):
        assert self.n == self.per, (self.n, self.per)


def xattn_moe(nc, x, ctx, Wq, bq, Wk, bk, Wv, bv, Wkvd, bkvd, qn_w, qn_b, kn_w, kn_b, kd_w, kd_b, Wo, bo,
              router, e_bias, w_up, w_down, sh_up, sh_down, out):
    stack = ExitStack()
    with stack:
        def sb(name, shape, dt=F32):
            return stack.enter_context(nc.sbuf_tensor(name, shape, dt))

        def sem(name):
            return stack.enter_context(nc.semaphore(name))

        bank = [stack.enter_context(nc.psum_tensor(f"bank{i}", [P, 512], F32)) for i in range(4, 8)]
        score_ps = stack.enter_context(nc.psum_tensor("score_ps", [P, 2 * 512], F32))
        probsT_ps = stack.enter_context(nc.psum_tensor("probsT_ps", [P, 2, 512], F32))
        bank = [score_ps[:, 0:512], score_ps[:, 512:1024], probsT_ps[:, 0, :], probsT_ps[:, 1, :]] + \
               [b[:, :] for b in bank]

        vd_dram = nc.dram_tensor("vd_dram", [PAIRS * DCA, 2 * D], F32, kind="Internal").ap()
        xn2T_dram = nc.dram_tensor("xn2T_dram", [KC, P, NB * SQ], F32, kind="Internal").ap()
        slot_x = nc.dram_tensor("slot_x", [SLOTS, D], F32, kind="Internal").ap()
        slot_y = nc.dram_tensor("slot_y", [SLOTS, D], F32, kind="Internal").ap()

        ident = sb("ident", [P, P])
        tri = sb("tri", [P, P])
        ones = sb("ones", [P, P])
        zeros = sb("zeros", [P, D])
        half = sb("half", [P, 2])
        slotm = sb("slotm", [P, 2])
        quad = sb("quad", [P, 4])
        wq_sb = sb("wq_sb", [P, KC, D])
        wkv_sb = sb("wkv_sb", [P, 2 * D])
        wkvd_sb = sb("wkvd_sb", [P, 2 * D])
        wo_sb = sb("wo_sb", [P, KC, D])
        bq_sb = sb("bq_sb", [P, D])
        bkv_sb = sb("bkv_sb", [P, 2 * D])
        bkvd_sb = sb("bkvd_sb", [P, 2 * D])
        bo_sb = sb("bo_sb", [P, D])
        router_in = sb("router_in", [E, D])
        router_sb = sb("router_sb", [P, KC, E])
        ebias_sb = sb("ebias_sb", [P, E])
        ln_in = sb("ln_in", [6, P])
        ln_col = sb("ln_col", [P, 6])
        q_bias2 = sb("q_bias2", [P, 2])
        k_w4 = sb("k_w4", [P, 4])
        k_b4 = sb("k_b4", [P, 4])
        su_sb = sb("su_sb", [P, KC, SI])
        sd_sb = sb("sd_sb", [P, SI // P, D])
        wmean = sb("wmean", [P, 7, H])
        X2 = sb("X2", [P, PAIRS, D])
        XN2 = sb("XN2", [P, PAIRS, D])
        logits = sb("logits", [P, PAIRS, E])
        xT_ch = sb("xT_ch", [P, 2, KC, SCH])
        kdT = sb("kdT", [P, PAIRS, SETS, DCA])
        loop_stack = ExitStack()

        def sbl(name, shape, dt=F32):
            return loop_stack.enter_context(nc.sbuf_tensor(name, shape, dt))

        x_in = sbl("x_in", [P, 2, D])
        y_in = sbl("y_in", [P, 2, KD])
        xn = sbl("xn", [P, 2, D])
        xnT = sbl("xnT", [P, 2, KC, P])
        yT = sbl("yT", [P, 2, P])
        q_sb = sbl("q_sb", [P, 2, D])
        kv_sb = sbl("kv_sb", [P, 2, 2 * D])
        sq = sbl("sq", [P, 2, 2, D])
        stat = sbl("stat", [P, 64])
        rst = sbl("rst", [P, 3, 68])
        q_rstd2 = sbl("q_rstd2", [P, 2, H, 2])
        qn = sbl("qn", [P, 2, 2 * D])
        kn = sbl("kn", [P, 2 * D])
        qT = sbl("qT", [P, 2, SETS, P])
        k_bd = sbl("k_bd", [P, 2, SETS, 4, SK])
        v_rep = sbl("v_rep", [P, 2, 2 * D])
        v_bd = sbl("v_bd", [P, 2, 2 * D])
        probs = sbl("probs", [P, 2, H, SK])
        pmax = sbl("pmax", [P, 2, 2, H])
        psum_ = sbl("psum_", [P, 2, 2, H])
        prec = sbl("prec", [P, 2, 2, H])
        probsT = sbl("probsT", [P, 2, 2, 512])
        ctxT = sbl("ctxT", [P, 2, KC, P])
        xn2 = sbl("xn2", [P, 2, D])
        xn2T = sbl("xn2T", [P, KC, 2, P])
        bn = sbl("bn", [P, 2, 6])
        mv = sbl("mv", [P, 2, 2])
        bn2 = sbl("bn2", [P, 2, 6])
        mv2 = sbl("mv2", [P, 2, 2])
        shift = sbl("shift", [P, 4])
        rst_d = sbl("rst_d", [P, 4, 2 * DT * H])
        y_d = X2[:, 0:DT, :].rearrange("p n (c d) -> p (n c) d", c=2)
        yT_d = X2[:, DT:2 * DT, :].rearrange("p n (c d) -> p (n c) d", c=2)
        kv_d = XN2[:, 0:4 * DT, :].rearrange("p (n c) d -> p n (c d)", c=2)
        sq_d = XN2[:, 4 * DT:6 * DT, :]
        kn_d = XN2[:, 6 * DT:8 * DT, :].rearrange("p (t c) d -> p t (c d)", c=2)

        loop_stack.close()
        up_sb = sb("up_sb", [P, E, KC, MI])
        down_sb = sb("down_sb", [P, E, D])
        relu = sb("relu", [P, 2, SCH])
        hid = sb("hid", [P, 2, SI // P, SCH])
        sig = sb("sig", [P, PAIRS, E])
        sel = sb("sel", [P, PAIRS, E])
        pair_sums = sb("pair_sums", [P, PAIRS * NG, 6])
        gsum = sb("gsum", [P, PAIRS, NG])
        gtmp = sb("gtmp", [P, PAIRS, NG])
        goh = sb("goh", [P, 2, PAIRS, NG])
        oh = sb("oh", [P, 2, PAIRS, E])
        etmp = sb("etmp", [P, PAIRS, E])
        tile_cnt = sb("tile_cnt", [P, PAIRS, E])
        top = sb("top", [P, PAIRS])
        gate = sb("gate", [P, 3, PAIRS])
        slot = sb("slot", [P, 2, PAIRS])
        slot_i = sb("slot_i", [P, 2, PAIRS], I32)
        count = sb("count", [P, 6, E])
        count_i = sb("count_i", [P, 2, E], I32)
        tile_no = sb("tile_no", [1, SLOT_TILES, 1])
        past = sb("past", [1, SLOT_TILES, E])
        eoff = sb("eoff", [1, SLOT_TILES // UNROLL, UNROLL])
        digit = sb("digit", [1, 1, UNROLL])
        packed = sb("packed", [1, SLOT_TILES // UNROLL])
        packed_i = sb("packed_i", [1, SLOT_TILES // UNROLL], I32)
        desc = sb("desc", [P, 1, E])
        er = sb("er", [P, 2, UNROLL * MI])
        ea = sb("ea", [P, 2, UNROLL * MI])
        eaT = sb("eaT", [P, 2, UNROLL * P])
        gidx = sb("gidx", [P, 2, 2, UNROLL], I32)
        xt = XN2[:, 0:2 * UNROLL, :].rearrange("p (h j) d -> p h j d", h=2)
        xtT = XN2[:, 2 * UNROLL:4 * UNROLL, :].rearrange("p (h j) (k n) -> p h j k n", h=2, k=KC)
        ey = XN2[:, 4 * UNROLL:6 * UNROLL, :].rearrange("p (h j) d -> p h j d", h=2)
        gath = XN2[:, 0:4 * UNROLL, :].rearrange("p (h k j) d -> p h k j d", h=2, k=2)
        res = XN2[:, 4 * UNROLL:6 * UNROLL, :].rearrange("p (h j) d -> p h j d", h=2)

        s_alone = sem("waits_alone")
        s_wd = sem("dca_weights_loaded")
        s_wl = sem("head_vectors_loaded")
        s_w = sem("projection_weights_loaded")
        s_wo = sem("output_weights_loaded")
        s_w1 = sem("shared_weights_loaded")
        s_w2 = sem("ffn_weights_loaded")
        s_zero = sem("slots_zeroed")
        s_const = sem("constants_ready")
        s_prep = sem("weights_prepared")
        s_prep_ps = sem("prep_transposed")
        s_x = sem("x_loaded")
        s_y_in = sem("context_loaded")
        s_ch = sem("setup_chain")
        s_centred = sem("weights_centred")
        s_ln1 = sem("first_layernorm_stats")
        s_hv = sem("head_variances")
        s_ln2 = sem("second_layernorm_stats")
        s_root = sem("inverse_roots")
        s_shift = sem("layernorm_shifts")
        s_max = sem("score_maxima")
        s_sum = sem("softmax_sums")
        s_xbo = sem("x_plus_bo_stored")
        s_xn = sem("xn_ready")
        s_yT_ps = sem("yT_in_psum")
        s_xT_ps = sem("xT_in_psum")
        s_yT = sem("yT_ready")
        s_xT = sem("xT_ready")
        s_kv_ps = sem("kv_in_psum")
        s_q_ps = sem("q_in_psum")
        s_kv = sem("kv_ready")
        s_q = sem("q_ready")
        s_sq = sem("squares_ready")
        s_rstd = sem("head_rstd_ready")
        s_kn = sem("kn_ready")
        s_qn = sem("qn_ready")
        s_kT_ps = sem("kT_in_psum")
        s_qT_ps = sem("qT_in_psum")
        s_kbd = sem("k_main_blocks_ready")
        s_kbdd = sem("k_dca_blocks_ready")
        s_qT = sem("qT_ready")
        s_v = sem("v_replicated")
        s_vbd = sem("v_blocks_ready")
        s_s_ps = sem("scores_in_psum")
        s_sub = sem("scores_minus_max")
        s_exp = sem("exp_ready")
        s_rsum = sem("inverse_sums_ready")
        s_p = sem("probs_ready")
        s_pT_ps = sem("probsT_in_psum")
        s_pT = sem("probsT_ready")
        s_c_ps = sem("ctxT_in_psum")
        s_c = sem("ctxT_ready")
        s_o_ps = sem("attn_out_in_psum")
        s_x2 = sem("residual_stored")
        s_xn2 = sem("xn2_ready")
        s_x2T_ps = sem("xn2T_in_psum")
        s_x2T = sem("xn2T_ready")
        s_l_ps = sem("logits_in_psum")
        s_l = sem("logits_stored")
        s_stx = sem("xn2_stored")
        s_stT = sem("xn2T_stored")
        d_in = sem("dca_rows_loaded")
        d_yT_ps = sem("dca_yT_in_psum")
        d_yT = sem("dca_yT_ready")
        d_kv_ps = sem("dca_kv_in_psum")
        d_kv = sem("dca_kv_ready")
        d_sq = sem("dca_squares_ready")
        d_kn = sem("dca_kn_ready")
        d_kT_ps = sem("dca_kT_in_psum")
        d_kT = sem("dca_kT_stored")
        d_vst = sem("dca_v_stored")

        s_iota = sem("tile_numbers_ready")
        s_xTc = [sem(f"xT_chunk_loaded{j}") for j in range(2)]
        s_u_ps = sem("shared_up_in_psum")
        s_r = sem("shared_relu_ready")
        s_hid = sem("shared_hidden_ready")
        s_d_ps = sem("shared_down_in_psum")
        s_x3 = sem("shared_added")
        s_ex = sem("router_exp_ready")
        s_oh = sem("experts_chosen")
        s_cnt_ps = sem("ranks_in_psum")
        s_cnt = sem("ranks_copied")
        s_slot = sem("slots_ready")
        s_eoff = sem("tile_experts_ready")
        s_rt = sem("routing_chain")
        s_scat = sem("rows_scattered")
        s_xt = [sem(f"slot_tiles_loaded{h}") for h in range(2)]
        s_eT_ps = sem("slot_tilesT_in_psum")
        s_eT = sem("slot_tilesT_ready")
        s_h_ps = sem("expert_up_in_psum")
        s_er = sem("expert_relu_ready")
        s_ea = sem("expert_act_ready")
        s_aT_ps = sem("expert_actT_in_psum")
        s_aT = sem("expert_actT_ready")
        s_y_ps = sem("expert_out_in_psum")
        s_y = sem("expert_out_ready")
        s_ys = [sem(f"expert_out_stored{h}") for h in range(2)]
        s_gidx = sem("gather_indices_ready")
        s_g = [sem(f"rows_gathered{h}") for h in range(2)]
        s_gc = sem("combine_chain")
        s_res = sem("result_ready")
        s_out = [sem(f"result_stored{h}") for h in range(2)]

        x_rows = x.rearrange("b s d -> (b s) d")
        out_rows = out.rearrange("b s d -> (b s) d")

        def row1(v):
            return v.rearrange("(a n) -> a n", a=1)

        def all_rows(v, n=P):
            return v.partition_broadcast(n)

        def root_guess(dve, v, r):
            return dve.tensor_scalar(r.bitcast(I32), v.bitcast(I32), -0.5, float(0x5F3759DF), ALU.mult, ALU.add)

        def root_square(dve, r, t):
            return dve.tensor_tensor(t, r, r, ALU.mult)

        def root_error(dve, v, t):
            return dve.scalar_tensor_tensor(t, t, -0.5, v, ALU.mult, ALU.mult)

        def root_better(dve, r, t):
            return dve.scalar_tensor_tensor(r, t, 1.5, r, ALU.add, ALU.mult)

        def rsqrt(ch, dve, v, r, t):
            ch.link(root_guess(dve, v, r))
            for _ in range(3):
                ch.link(root_square(dve, r, t))
                ch.link(root_error(dve, v, t))
                ch.link(root_better(dve, r, t))

        def kv_heads(ap):
            return ap.rearrange("p (h c d) -> p c h d", c=2, d=HD)

        def wait_alone(eng, sem_, value):
            eng.wait_ge(sem_, value)
            eng.sem_inc(s_alone, 1)

        Chain.wait_alone = staticmethod(wait_alone)

        def is_first(g):
            return isinstance(g, int) and g == 0

        def active(g):
            return not isinstance(g, int) or 0 <= g < GROUPS

        def since(g, n):
            return not isinstance(g, int) or g >= n

        def main_loop(eng, step):
            for i in range(-1, 3):
                step(i)
            with eng.Fori(3, GROUPS - 3) as i:
                step(i)
            for i in range(GROUPS - 3, GROUPS + 2):
                step(i)

        def expert_loop(eng, step):
            step(0)
            with eng.Fori(1, STEPS - 1) as i:
                step(i)
            step(STEPS - 1)

        def more_experts(i):
            return not isinstance(i, int) or i + 1 < STEPS

        kv_ps = [bank[0], bank[1]]
        dca_bank = [bank[2], bank[3], bank[6], bank[7]]
        ctx_ps = [bank[5], bank[7]]

        block = stack.enter_context(nc.Block())

        @block.sync
        def _(sp):
            ctx_dca = ctx[:, SM:SK, :].rearrange("(t u b) k d -> u b k t d", u=8, b=2)
            blocks = y_d[:, :, :].rearrange("p (t b) d -> p b t d", b=2)
            for u in range(8):
                for b in range(2):
                    sp.dma_start(blocks[u * DCA:(u + 1) * DCA, b, :, :], ctx_dca[u, b]).then_inc(d_in, 16)
            sp.dma_start(wkvd_sb[:, :], Wkvd).then_inc(s_wd, 16)
            sp.dma_start(bkvd_sb[:, :], all_rows(bkvd)).then_inc(s_wd, 16)
            def load_x(g):
                if since(g, 1):
                    sp.wait_ge(s_xn, g)
                    sp.wait_ge(s_xbo, g)
                sp.dma_start(x_in[:, :, :], x_rows[bass.ds(256 * g, 256), :].rearrange("(u p) d -> p u d", p=P))\
                    .then_inc(s_x, 16)

            def load_y(g):
                if since(g, 1):
                    sp.wait_ge(s_yT_ps, g)
                for u in range(2):
                    sp.dma_start(y_in[u * SM:(u + 1) * SM, :, :],
                                 ctx[bass.ds(4 * g + 2 * u, 2), 0:SM, :].rearrange("b k d -> k b d"))\
                        .then_inc(s_y_in, 16)

            load_x(0)
            for k in range(KC):
                sp.dma_start(wq_sb[:, k, :], Wq[k * P:(k + 1) * P, :]).then_inc(s_w, 16)
            sp.dma_start(bq_sb[:, :], all_rows(bq)).then_inc(s_w, 16)
            sp.dma_start(wkv_sb[:, 0:D], Wk).then_inc(s_w, 16)
            sp.dma_start(wkv_sb[:, D:], Wv).then_inc(s_w, 16)
            sp.dma_start(bkv_sb[:, 0:D], all_rows(bk)).then_inc(s_w, 16)
            sp.dma_start(bkv_sb[:, D:], all_rows(bv)).then_inc(s_w, 16)
            load_y(0)
            for i, v in enumerate((qn_w, qn_b, kn_w, kn_b, kd_w, kd_b)):
                sp.dma_start(ln_in[i:i + 1, :].rearrange("a (r d) -> a r d", d=HD),
                             row1(v).unsqueeze(1).to_broadcast([1, P // HD, HD])).then_inc(s_wl, 16)
            sp.dma_start(router_in[:, :], router).then_inc(s_wl, 16)
            sp.dma_start(bo_sb[:, :], all_rows(bo)).then_inc(s_wo, 16)
            for k in range(KC):
                sp.dma_start(wo_sb[:, k, :], Wo[k * P:(k + 1) * P, :]).then_inc(s_wo, 16)
            sp.dma_start(ebias_sb[:, :], all_rows(e_bias)).then_inc(s_wo, 16)

            def store_dca():
                sp.wait_ge(d_kv, 2 * DT)
                values = kv_d[:, :, D:].rearrange("p (t b) n -> p b t n", b=2)
                for b in range(2):
                    sp.dma_start(vd_dram[:, b * D:(b + 1) * D].rearrange("(t p) n -> p t n", p=P), values[:, b, :, :])\
                        .then_inc(d_vst, 16)
                sp.wait_ge(d_vst, 32)

            def replicate_v(g):
                wait_alone(sp, s_kv, g + 1)
                if since(g, 1):
                    sp.wait_ge(s_vbd, g)
                for c in range(2):
                    for u in range(2):
                        sp.dma_start(v_rep[64 * c:64 * c + SM, u, :].rearrange("p (b n) -> p b n", b=2),
                                     kv_sb[u * SM:(u + 1) * SM, :, D:]).then_inc(s_v, 16)
                        sp.dma_start(v_rep[64 * c + SM:64 * c + SK, u, :],
                                     vd_dram[bass.ds(2 * DCA * g + DCA * u, DCA), :]).then_inc(s_v, 16)

            def store_xn2(g):
                sp.wait_ge(s_xn2, g + 1)
                sp.dma_start(XN2[:, bass.ds(2 * g, 2), :], xn2[:, :, :]).then_inc(s_stx, 16)

            def store_xn2T(g):
                sp.wait_ge(s_x2T, g + 1)
                for k in range(KC):
                    sp.dma_start(xn2T_dram[k, :, bass.ds(256 * g, 256)],
                                 xn2T[:, k, :, :].rearrange("p u n -> p (u n)")).then_inc(s_stT, 16)

            def zero_slots(g):
                rows = SLOTS // GROUPS
                sp.dma_start(slot_x[bass.ds(rows * g, rows), :].rearrange("(t p) d -> p t d", p=P),
                             zeros[:, :].unsqueeze(1).to_broadcast([P, rows // P, D])).then_inc(s_zero, 16)

            def step(i):
                if active(i + 1):
                    replicate_v(i + 1)
                if active(i + 3):
                    load_y(i + 3)
                    load_x(i + 3)
                if active(i - 2):
                    store_xn2(i - 2)
                    store_xn2T(i - 2)
                if active(i):
                    zero_slots(i)
                if isinstance(i, int) and i == GROUPS:
                    sp.wait_ge(s_stT, 32 * (GROUPS - 2))
                    load_chunks(0)

            def load_chunks(i):
                for j in range(2):
                    sp.dma_start(xT_ch[:, j, :, :],
                                 xn2T_dram[:, :, bass.ds(SCH * 2 * i + SCH * j, SCH)].rearrange("k p n -> p k n"))\
                        .then_inc(s_xTc[j], 16)

            store_dca()
            load_y(1)
            load_x(1)
            main_loop(sp, step)

            sp.wait_ge(s_stT, 32 * GROUPS)
            sp.wait_ge(s_stx, 16 * GROUPS)
            with sp.Fori(1, NCH // 2) as i:
                sp.wait_ge(s_u_ps, 2 * NM * i)
                load_chunks(i)
            sp.wait_ge(s_scat, 16 * 2 * PAIRS)

            def tiles(dram, i, h):
                return dram[bass.ds(UNROLL * P * (2 * i + h), UNROLL * P), :].rearrange("(j p) d -> p j d", p=P)

            def load_tiles(i, h):
                if since(i, 1):
                    wait_alone(sp, s_eT_ps, 2 * i + (h - 1))
                sp.dma_start(xt[:, h, :, :], tiles(slot_x, i, h)).then_inc(s_xt[h], 16)

            def store_tiles(i, h):
                wait_alone(sp, s_y, 2 * i + (h + 1))
                sp.dma_start(tiles(slot_y, i, h), ey[:, h, :, :]).then_inc(s_ys[h], 16)

            def expert_step(i, more):
                for h in range(2):
                    if more:
                        load_tiles(i + 2, h)
                    store_tiles(i, h)

            for i in range(2):
                for h in range(2):
                    load_tiles(i, h)
            with sp.Fori(0, STEPS - 2) as i:
                expert_step(i, True)
            expert_step(STEPS - 2, False)
            expert_step(STEPS - 1, False)
            with sp.Fori(0, PAIRS // (2 * UNROLL)) as i:
                for h in range(2):
                    sp.wait_ge(s_res, 2 * i + (h + 1))
                    sp.dma_start(out_rows[bass.ds(UNROLL * P * (2 * i + h), UNROLL * P), :]
                                 .rearrange("(j p) d -> p j d", p=P), res[:, h, :, :]).then_inc(s_out[h], 16)
            for h in range(2):
                sp.wait_ge(s_out[h], 16 * (PAIRS // (2 * UNROLL)))
            sp.wait_ge(s_alone, 4 * GROUPS + PAIRS // UNROLL + 4 * STEPS - 2)

        @block.gpsimd
        def _(pool):
            pool.memset(ones[:, :], 1.0).then_inc(s_const, 1)
            pool.memset(zeros[:, :], 0.0).then_inc(s_const, 1)
            pool.memset(ident[:, :], 0.0).then_inc(s_const, 1)
            pool.memset(stat[:, :], 1.0).then_inc(s_const, 1)
            pool.memset(kv_sb[:, :, :], 0.0).then_inc(s_const, 1)
            pool.memset(rst[:, 0, :], 1.0).then_inc(s_const, 1)
            pool.wait_ge(s_const, 6)
            pool.affine_select(out=ident[:, :], in_=ident[:, :], compare_op=ALU.not_equal, fill=1.0, base=0,
                               pattern=[[-1, P]], channel_multiplier=1).then_inc(s_const, 1)
            pool.affine_select(out=tri[:, :], in_=zeros[:, 0:P], compare_op=ALU.is_gt, fill=-1.0, base=0,
                               pattern=[[1, P]], channel_multiplier=-1).then_inc(s_const, 1)
            pool.affine_select(out=half[:, :], in_=ones[:, 0:2], compare_op=ALU.is_ge, fill=0.0, base=0,
                               pattern=[[-64, 2]], channel_multiplier=1).then_inc(s_const, 1)
            pool.affine_select(out=quad[:, :], in_=ones[:, 0:4], compare_op=ALU.is_ge, fill=0.0, base=0,
                               pattern=[[-32, 4]], channel_multiplier=1).then_inc(s_const, 1)
            pool.wait_ge(s_const, 10)
            pool.affine_select(out=half[:, :], in_=half[:, :], compare_op=ALU.is_ge, fill=0.0, base=63,
                               pattern=[[64, 2]], channel_multiplier=-1).then_inc(s_const, 1)
            pool.affine_select(out=quad[:, :], in_=quad[:, :], compare_op=ALU.is_ge, fill=0.0, base=31,
                               pattern=[[32, 4]], channel_multiplier=-1).then_inc(s_const, 1)

            def add_bo(g):
                pool.wait_ge(s_x, 16 * g + 16)
                pool.tensor_tensor(X2[:, bass.ds(2 * g, 2), :], x_in[:, :, :],
                                   bo_sb[:, :].unsqueeze(1).to_broadcast([P, 2, D]), ALU.add).then_inc(s_xbo, 1)

            def normalise_q(g):
                pool.wait_ge(s_rstd, g + 1)
                if since(g, 1):
                    pool.wait_ge(s_qT_ps, 2 * g)
                for u in range(2):
                    pool.tensor_tensor(qn[:, u, :].rearrange("p (h s d) -> p h s d", h=H, s=2),
                                       q_sb[:, u, :].rearrange("p (h d) -> p h d", h=H).unsqueeze(2)
                                       .to_broadcast([P, H, 2, HD]),
                                       q_rstd2[:, u, :, :].unsqueeze(3).to_broadcast([P, H, 2, HD]),
                                       ALU.mult).then_inc(s_qn, 1)

            def dca_blocks(g):
                if is_first(g):
                    pool.wait_ge(d_kT, DT)
                else:
                    pool.wait_ge(s_s_ps, 2 * g)
                for j in range(4):
                    last = pool.tensor_tensor(k_bd[:, :, :, j, SM:SK], kdT[:, bass.ds(2 * g, 2), :, :],
                                              quad[:, j:j + 1].unsqueeze(1).unsqueeze(1)
                                              .to_broadcast([P, 2, SETS, DCA]), ALU.mult)
                last.then_inc(s_kbdd, 1)

            def normalise_probs(g, u):
                pool.wait_ge(s_rsum, 2 * g + (u + 1))
                for c, (lo, hi) in enumerate(((0, SM), (SM, SK))):
                    last = pool.tensor_tensor(probs[:, u, :, lo:hi], probs[:, u, :, lo:hi],
                                              prec[:, u, c, :].unsqueeze(2).to_broadcast([P, H, hi - lo]), ALU.mult)
                last.then_inc(s_p, 1)

            pool.wait_ge(s_wo, 16 * 4)
            pool.wait_ge(d_kv, 2 * DT)
            pool.wait_ge(s_const, N_CONST)

            def step(i):
                if active(i + 1):
                    normalise_q(i + 1)
                if active(i + 2):
                    add_bo(i + 2)
                if active(i + 1):
                    dca_blocks(i + 1)
                if active(i):
                    normalise_probs(i, 0)
                    normalise_probs(i, 1)

            add_bo(0)
            main_loop(pool, step)

            pool.wait_ge(s_l, GROUPS)
            pool.iota(tile_no[:, :, :], pattern=[[1, SLOT_TILES]], base=0, channel_multiplier=0,
                      allow_small_or_imprecise_dtypes=True).then_inc(s_iota, 1)
            for j in range(UNROLL):
                pool.memset(digit[:, :, j:j + 1], float(E ** j)).then_inc(s_iota, 1)
            pool.iota(desc[:, :, :], pattern=[[-1, E]], base=E, channel_multiplier=0,
                      allow_small_or_imprecise_dtypes=True).then_inc(s_iota, 1)
            pool.wait_ge(s_slot, 1)
            pool.wait_ge(s_zero, 16 * GROUPS)
            pool.wait_ge(s_stx, 16 * GROUPS)
            for t in range(PAIRS):
                for k in range(2):
                    pool.indirect_dma_start(slot_x[:, :], bass.IndirectOffsetOnAxis(ap=slot_i[:, k, t:t + 1], axis=0),
                                            XN2[:, t, :], None).then_inc(s_scat, 16)

            for h in range(2):
                pool.wait_ge(s_ys[h], 16 * STEPS)

            def gather(i):
                for h in range(2):
                    if since(i, 1):
                        pool.wait_ge(s_res, 2 * i + (h - 1))
                    pool.tensor_copy(gidx[:, h, :, :], slot_i[:, :, bass.ds(UNROLL * (2 * i + h), UNROLL)])\
                        .then_inc(s_gidx, 1)
                    wait_alone(pool, s_gidx, 2 * i + (h + 1))
                    for j in range(UNROLL):
                        for k in range(2):
                            pool.indirect_dma_start(gath[:, h, k, j, :], None, slot_y[:, :],
                                                    bass.IndirectOffsetOnAxis(ap=gidx[:, h, k, j:j + 1], axis=0))\
                                .then_inc(s_g[h], 16)

            gather(0)
            with pool.Fori(1, PAIRS // (2 * UNROLL)) as i:
                gather(i)

        @block.scalar
        def _(act):
            def evac(dst, src):
                return act.activation(dst, src, ACT.Copy)

            def copy_yT(g):
                act.wait_ge(s_yT_ps, g + 1)
                if since(g, 1):
                    act.wait_ge(s_kv_ps, g)
                evac(yT[:, :, 0:MR], bank[5][:, 0:2 * MR].rearrange("p (b n) -> p b n", b=2)).then_inc(s_yT, 1)

            def copy_xT(g):
                act.wait_ge(s_xT_ps, g + 1)
                if since(g, 1):
                    act.wait_ge(s_q_ps, g)
                evac(xnT[:, :, :, :], bank[6].rearrange("p (u k n) -> p u k n", u=2, k=KC)).then_inc(s_xT, 1)

            def normalise_x(g):
                act.wait_ge(s_shift, g + 1)
                if since(g, 1):
                    act.wait_ge(s_xT_ps, g)
                for u in range(2):
                    last = act.activation(xn[:, u, :], x_in[:, u, :], ACT.Identity, bias=shift[:, u:u + 1],
                                          scale=rst[:, 1, 64 + u:65 + u])
                last.then_inc(s_xn, 1)

            def normalise_x2(g):
                act.wait_ge(s_shift, g + 5)
                if since(g, 1):
                    act.wait_ge(s_x2T_ps, g)
                    act.wait_ge(s_stx, 16 * g)
                for u in range(2):
                    row = X2[:, bass.ds(2 * g + u, 1), :].rearrange("p a n -> p (a n)")
                    last = act.activation(xn2[:, u, :], row, ACT.Identity, bias=shift[:, 2 + u:3 + u],
                                          scale=rst[:, 1, 66 + u:67 + u])
                last.then_inc(s_xn2, 1)

            def squares(g):
                act.wait_ge(s_q, g + 1)
                act.activation(sq[:, 1, :, :], q_sb[:, :, :], ACT.Square).then_inc(s_sq, 1)
                act.wait_ge(s_kv, g + 1)
                act.activation(sq[0:MR, 0, :, :], kv_sb[0:MR, :, 0:D], ACT.Square).then_inc(s_sq, 1)

            def main_blocks(g):
                act.wait_ge(s_kT_ps, g + 1)
                if since(g, 1):
                    act.wait_ge(s_s_ps, 2 * g)
                src = bank[4][:, 0:SETS * MR].rearrange("p (s u k) -> p s u k", s=SETS, u=2)
                for j in range(4):
                    dst = k_bd[:, :, :, j, 0:SM].rearrange("p u s k -> p s u k")
                    last = act.activation(dst, src, ACT.Identity, bias=k_b4[:, j:j + 1], scale=k_w4[:, j:j + 1])
                last.then_inc(s_kbd, 1)

            def copy_qT(g, u):
                act.wait_ge(s_qT_ps, 2 * g + (u + 1))
                src = bank[6 + u].rearrange("p (s n) -> p s n", s=SETS)
                for s in range(2):
                    last = act.activation(qT[:, u, :, 64 * s:64 * s + 64], src[:, :, 64 * s:64 * s + 64],
                                          ACT.Identity, bias=q_bias2[:, s:s + 1], scale=ln_col[:, 0:1])
                last.then_inc(s_qT, 1)

            def mask_v(g):
                act.wait_ge(s_v, 128 * g + 128)
                vr = v_rep[:, :, :].rearrange("p u (n s d) -> p (u n) s d", s=2, d=HD)
                vb = v_bd[:, :, :].rearrange("p u (n s d) -> p (u n) s d", s=2, d=HD)
                for s in range(2):
                    last = act.activation(vb[:, :, s, :], vr[:, :, s, :], ACT.Copy, scale=half[:, s:s + 1])
                last.then_inc(s_vbd, 1)

            def exponent(g, u):
                act.wait_ge(s_sub, 2 * g + (u + 1))
                act.activation(probs[:, u, :, :], probs[:, u, :, :], ACT.Exp, scale=SCALE).then_inc(s_exp, 1)

            def copy_probsT(g, u):
                act.wait_ge(s_pT_ps, 2 * g + (u + 1))
                evac(probsT[:, u, :, :], probsT_ps[:, :, :]).then_inc(s_pT, 1)

            def copy_ctx(g, u):
                act.wait_ge(s_c_ps, 2 * g + (u + 1))
                if since(g, 1):
                    act.wait_ge(s_o_ps, 2 * g + (u - 1))
                evac(ctxT[:, u, :, :], ctx_ps[u][:, 0:256].rearrange("p (c n) -> p c n", c=KC))\
                    .then_inc(s_c, 1)

            def copy_xn2T(g):
                act.wait_ge(s_x2T_ps, g + 1)
                if since(g, 1):
                    act.wait_ge(s_l_ps, g)
                    act.wait_ge(s_stT, 32 * g)
                evac(xn2T[:, :, :, :].rearrange("p k u n -> p u k n"),
                     bank[7].rearrange("p (u k n) -> p u k n", u=2, k=KC)).then_inc(s_x2T, 1)

            def copy_logits(g):
                act.wait_ge(s_l_ps, g + 1)
                evac(logits[:, bass.ds(2 * g, 2), :], bank[4][:, 0:2 * E].rearrange("p (u e) -> p u e", u=2))\
                    .then_inc(s_l, 1)

            def step(i):
                if active(i - 1):
                    copy_ctx(i - 1, 1)
                if active(i):
                    mask_v(i)
                if active(i + 2):
                    copy_yT(i + 2)
                if active(i):
                    exponent(i, 0)
                if active(i + 2):
                    normalise_x(i + 2)
                if active(i - 2):
                    normalise_x2(i - 2)
                if active(i + 2):
                    copy_xT(i + 2)
                if active(i - 2):
                    copy_xn2T(i - 2)
                if active(i + 1):
                    main_blocks(i + 1)
                if active(i + 1):
                    copy_qT(i + 1, 0)
                    copy_qT(i + 1, 1)
                if active(i):
                    exponent(i, 1)
                    copy_probsT(i, 0)
                if active(i + 2):
                    squares(i + 2)
                if active(i - 2):
                    copy_logits(i - 2)
                if active(i):
                    copy_ctx(i, 0)
                    copy_probsT(i, 1)

            for n in range(2):
                act.wait_ge(d_yT_ps, n + 1)
                evac(yT_d[:, DT * n:DT * n + DT, :], bank[n].rearrange("p (n k) -> p n k", n=DT)).then_inc(d_yT, 1)
            for n in range(2):
                act.wait_ge(d_kv, DT * n + DT)
                act.activation(sq_d[:, DT * n:DT * n + DT, :], kv_d[:, DT * n:DT * n + DT, 0:D], ACT.Square)\
                    .then_inc(d_sq, 1)
            copy_yT(0)
            normalise_x(0)
            copy_xT(0)
            act.wait_ge(s_prep_ps, 1)
            evac(ln_col[:, :], bank[4][:, 0:6]).then_inc(s_prep_ps, 1)
            evac(router_sb[:, :, :], bank[4][:, 16:16 + KC * E].rearrange("p (k e) -> p k e", k=KC))\
                .then_inc(s_prep_ps, 1)
            act.wait_ge(s_prep_ps, 3)
            for t in range(DT):
                act.wait_ge(d_kT_ps, t + 1)
                act.activation(kdT[:, 8 * t:8 * t + 8, :, :],
                               dca_bank[t].rearrange("p (s u k) -> p u s k", s=SETS, u=8), ACT.Identity,
                               bias=ln_col[:, 5:6], scale=ln_col[:, 4:5]).then_inc(d_kT, 1)
            squares(0)
            act.dma_start(su_sb[:, :, :], sh_up.rearrange("(k p) n -> p k n", p=P)).then_inc(s_w1, 16)
            act.dma_start(sd_sb[:, :, :], sh_down.rearrange("(k p) n -> p k n", p=P)).then_inc(s_w1, 16)
            act.wait_ge(s_prep, 1)

            main_loop(act, step)

            act.wait_ge(s_stT, 32 * GROUPS)
            act.wait_ge(s_stx, 16 * GROUPS)
            act.wait_ge(s_l, GROUPS)
            act.dma_start(up_sb[:, :, :, :], w_up.rearrange("e (k p) i -> p e k i", p=P)).then_inc(s_w2, 16)
            act.dma_start(down_sb[:, :, :], w_down.rearrange("e i d -> i e d")).then_inc(s_w2, 16)
            act.activation(sig[:, :, :], logits[:, :, :], ACT.Exp, scale=-1.0).then_inc(s_ex, 1)

            def shared_step(i):
                for j in range(2):
                    for m in range(NM):
                        n = j * NM + m
                        act.wait_ge(s_u_ps, 2 * NM * i + (n + 1))
                        act.activation(relu[:, n % 2, :], bank[m], ACT.Relu).then_inc(s_r, 1)
                        if m == 0 and not is_first(i):
                            act.wait_ge(s_d_ps, 2 * i - 1 + j)
                        act.wait_ge(s_r, 2 * NM * i + (n + 1))
                        act.activation(hid[:, j, m, :], relu[:, n % 2, :], ACT.Square).then_inc(s_hid, 1)

            shared_step(0)
            with act.Fori(1, NCH // 2) as i:
                shared_step(i)

            def copy_tilesT(i, h):
                n = 2 * i + h
                act.wait_ge(s_eT_ps, n + 1)
                if since(i, 1):
                    act.wait_ge(s_h_ps, n - 1)
                for c in range(2):
                    last = evac(xtT[:, h, 2 * c:2 * c + 2, :, :],
                                bank[2 + c].rearrange("p (j k n) -> p j k n", j=2, k=KC))
                last.then_inc(s_eT, 1)

            def hidden(i, h):
                act.wait_ge(s_h_ps, 2 * i + (h + 1))
                act.activation(er[:, h, :], bank[h], ACT.Relu).then_inc(s_er, 1)

            def copy_actT(i, h):
                n = 2 * i + h
                act.wait_ge(s_aT_ps, n + 1)
                if since(i, 1):
                    act.wait_ge(s_y_ps, n - 1)
                evac(eaT[:, h, :], bank[h]).then_inc(s_aT, 1)

            def expert_step(i):
                hidden(i, 0)
                hidden(i, 1)
                for h in range(2):
                    copy_actT(i, h)
                    if more_experts(i):
                        copy_tilesT(i + 1, h)

            copy_tilesT(0, 0)
            copy_tilesT(0, 1)
            expert_loop(act, expert_step)

        @block.tensor
        def _(pe):
            pe.wait_ge(s_const, N_CONST)
            pe.wait_ge(d_in, 16 * 16)
            for n in range(2):
                for m in range(DT):
                    last = pe.transpose(bank[n][:, m * P:(m + 1) * P], y_d[:, n * DT + m, :], ident[:, :])
                last.then_inc(d_yT_ps, 1)
            pe.wait_ge(s_centred, 1)
            pe.wait_ge(d_yT, 2)
            for n in range(2 * DT):
                pe.matmul(bank[(2 + n) % 8], yT_d[:, n, :], wkvd_sb[:, :], start=True, stop=True).then_inc(d_kv_ps, 1)

            def transpose_y(g):
                pe.wait_ge(s_y_in, 32 * g + 32)
                if since(g, 3):
                    pe.wait_ge(s_c, 2 * g - 5)
                elif since(g, 1):
                    pe.wait_ge(s_q, g)
                for b in range(2):
                    last = pe.transpose(bank[5][:, b * MR:(b + 1) * MR], y_in[0:MR, b, :], ident[0:MR, 0:MR])
                last.then_inc(s_yT_ps, 1)

            def transpose_x(g):
                pe.wait_ge(s_xn, g + 1)
                for u in range(2):
                    for k in range(KC):
                        last = pe.transpose(bank[6][:, (u * KC + k) * P:(u * KC + k + 1) * P],
                                            xn[:, u, k * P:(k + 1) * P], ident[:, :])
                last.then_inc(s_xT_ps, 1)

            def project_q(g):
                pe.wait_ge(s_yT, g + 1)
                pe.wait_ge(s_xT, g + 1)
                for u in range(2):
                    for k in range(KC):
                        last = pe.matmul(bank[5][:, u * D:(u + 1) * D], xnT[:, u, k, :], wq_sb[:, k, :],
                                         start=(k == 0), stop=(k == KC - 1))
                last.then_inc(s_q_ps, 1)

            def project_kv(g):
                if since(g, 2):
                    pe.wait_ge(s_sub, 2 * g - 2)
                for b in range(2):
                    last = pe.matmul(kv_ps[b][0:MR, :], yT[:, b, 0:MR], wkv_sb[:, :], start=True, stop=True)
                last.then_inc(s_kv_ps, 1)

            def transpose_k(g):
                pe.wait_ge(s_kn, g + 1)
                if since(g, 4):
                    pe.wait_ge(s_l, g - 3)
                for s in range(SETS):
                    last = pe.transpose(bank[4][:, s * MR:(s + 1) * MR], kn[0:MR, s * P:(s + 1) * P],
                                        ident[0:MR, 0:MR])
                last.then_inc(s_kT_ps, 1)

            def transpose_q(g, u):
                pe.wait_ge(s_qn, 2 * g + (u + 1))
                if u == 0 and active(g + 1):
                    pe.wait_ge(s_xT, g + 2)
                if u == 1 and since(g, 3):
                    pe.wait_ge(s_x2T, g - 2)
                for s in range(SETS):
                    last = pe.transpose(bank[6 + u][:, s * P:(s + 1) * P], qn[:, u, s * P:(s + 1) * P],
                                        ident[:, :])
                last.then_inc(s_qT_ps, 1)

            def scores(g, u):
                pe.wait_ge(s_qT, 2 * g + (u + 1))
                if u == 0:
                    pe.wait_ge(s_kbd, g + 1)
                    pe.wait_ge(s_kbdd, g + 1)
                if u == 0 and active(g + 1):
                    pe.wait_ge(s_kv, g + 2)
                else:
                    pe.wait_ge(s_sub, 2 * g + u)
                for s in range(SETS):
                    last = pe.matmul(score_ps[:, s * CW:(s + 1) * CW], qT[:, u, s, :],
                                     k_bd[:, u, s, :, :].rearrange("p j k -> p (j k)"), start=True, stop=True)
                last.then_inc(s_s_ps, 1)

            def transpose_probs(g, u):
                pe.wait_ge(s_p, 2 * g + (u + 1))
                if u == 1:
                    pe.wait_ge(s_pT, 2 * g + 1)
                elif since(g, 1):
                    pe.wait_ge(s_x2, 2 * g)
                flat = probs[:, u, :, :].rearrange("p h k -> p (h k)")
                for n in range(HP):
                    last = pe.transpose(probsT_ps[:, n // 4, (n % 4) * P:(n % 4 + 1) * P], flat[:, n * P:(n + 1) * P],
                                        ident[:, :])
                last.then_inc(s_pT_ps, 1)

            def probs_v(g, u):
                if u == 0:
                    pe.wait_ge(s_vbd, g + 1)
                    if active(g + 2):
                        pe.wait_ge(s_q, g + 3)
                elif active(g + 1):
                    pe.wait_ge(s_qT, 2 * g + 4)
                else:
                    pe.wait_ge(s_x2T, g - 1)
                pe.wait_ge(s_pT, 2 * g + (u + 1))
                for c in range(2):
                    for n in range(HP // 2):
                        for b in range(2):
                            col = P * c + 64 * b
                            last = pe.matmul(ctx_ps[u][32 * n:32 * n + 32, col:col + 64],
                                             v_bd[:, u, b * D + (4 * c + n) * 32:b * D + (4 * c + n) * 32 + 32],
                                             probsT[:, u, c, n * P + 64 * b:n * P + 64 * b + 64],
                                             start=True, stop=True)
                last.then_inc(s_c_ps, 1)

            def attn_out(g):
                for u in range(2):
                    pe.wait_ge(s_c, 2 * g + (u + 1))
                    for k in range(KC):
                        last = pe.matmul(bank[2 + u][:, 0:D], ctxT[:, u, k, :], wo_sb[:, k, :],
                                         start=(k == 0), stop=(k == KC - 1))
                    last.then_inc(s_o_ps, 1)

            def transpose_xn2(g):
                pe.wait_ge(s_xn2, g + 1)
                for u in range(2):
                    for k in range(KC):
                        last = pe.transpose(bank[7][:, (u * KC + k) * P:(u * KC + k + 1) * P],
                                            xn2[:, u, k * P:(k + 1) * P], ident[:, :])
                last.then_inc(s_x2T_ps, 1)

            def route(g):
                pe.wait_ge(s_x2T, g + 1)
                if active(g + 3):
                    pe.wait_ge(s_kbd, g + 4)
                for u in range(2):
                    for k in range(KC):
                        last = pe.matmul(bank[4][:, u * E:(u + 1) * E], xn2T[:, k, u, :], router_sb[:, k, :],
                                         start=(k == 0), stop=(k == KC - 1))
                last.then_inc(s_l_ps, 1)

            def step(i):
                if active(i + 2):
                    transpose_y(i + 2)
                if active(i - 1):
                    attn_out(i - 1)
                if active(i):
                    scores(i, 1)
                if active(i + 1):
                    transpose_k(i + 1)
                if active(i + 2):
                    transpose_x(i + 2)
                if active(i - 2):
                    transpose_xn2(i - 2)
                if active(i + 2):
                    project_q(i + 2)
                if active(i + 1):
                    transpose_q(i + 1, 0)
                    transpose_q(i + 1, 1)
                if active(i + 2):
                    project_kv(i + 2)
                if active(i):
                    transpose_probs(i, 0)
                if active(i - 2):
                    route(i - 2)
                if active(i + 1):
                    scores(i + 1, 0)
                if active(i):
                    probs_v(i, 0)
                    transpose_probs(i, 1)
                    probs_v(i, 1)

            pe.wait_ge(d_kv, 4)
            transpose_y(0)
            pe.wait_ge(d_kv, 2 * DT)
            transpose_x(0)
            pe.wait_ge(s_centred, 2)
            project_q(0)
            project_kv(0)
            pe.wait_ge(s_wl, 16 * 7)
            pe.wait_ge(d_kv, 3)
            pe.transpose(bank[4][:, 0:6], ln_in[:, :], ident[0:6, 0:6])
            for k in range(KC):
                last = pe.transpose(bank[4][:, 16 + k * E:16 + (k + 1) * E], router_in[:, k * P:(k + 1) * P],
                                    ident[0:E, 0:E])
            last.then_inc(s_prep_ps, 1)
            for t in range(DT):
                pe.wait_ge(d_kn, t + 1)
                if t == 2:
                    pe.wait_ge(s_xT, 1)
                for s in range(SETS):
                    last = pe.transpose(dca_bank[t][:, s * P:(s + 1) * P], kn_d[:, t, s * P:(s + 1) * P], ident[:, :])
                last.then_inc(d_kT_ps, 1)
            pe.wait_ge(s_prep_ps, 3)
            pe.wait_ge(d_kT, DT)
            pe.wait_ge(s_wo, 16 * 4)

            main_loop(pe, step)

            pe.wait_ge(s_w1, 32)
            pe.wait_ge(s_l, GROUPS)

            def shared_up(i, j):
                pe.wait_ge(s_xTc[j], 16 * i + 16)
                for m in range(NM):
                    if j or not is_first(i):
                        pe.wait_ge(s_r, 2 * NM * i + (j * NM + m + 1 - NM))
                    for k in range(KC):
                        last = pe.matmul(bank[m], su_sb[:, k, m * P:(m + 1) * P], xT_ch[:, j, k, :],
                                         start=(k == 0), stop=(k == KC - 1))
                    last.then_inc(s_u_ps, 1)

            def shared_down(i, j):
                pe.wait_ge(s_hid, 2 * NM * i + NM * (j + 1))
                if not is_first(i):
                    pe.wait_ge(s_x3, 2 * i - 1 + j)
                for t in range(SCH // P):
                    o = bank[4 + 2 * j + t // 2][:, (t % 2) * D:(t % 2 + 1) * D]
                    for m in range(NM):
                        last = pe.matmul(o, hid[:, j, m, t * P:(t + 1) * P], sd_sb[:, m, :],
                                         start=(m == 0), stop=(m == NM - 1))
                last.then_inc(s_d_ps, 1)

            def ranks():
                pe.wait_ge(s_oh, 1)
                chosen = etmp[:, :, :].rearrange("p t e -> p (t e)")
                pe.wait_ge(s_r, 2 * NM)
                pe.matmul(bank[0], tri[:, :], chosen, start=True, stop=True)
                pe.matmul(bank[1], ones[:, :], chosen, start=True, stop=True).then_inc(s_cnt_ps, 1)

            shared_up(0, 0)
            shared_up(0, 1)
            shared_down(0, 0)
            ranks()
            shared_down(0, 1)
            pe.wait_ge(s_cnt, 1)
            with pe.Fori(1, LAST_SH) as i:
                shared_up(i, 0)
                shared_up(i, 1)
                shared_down(i, 0)
                shared_down(i, 1)
            shared_up(LAST_SH, 0)
            shared_up(LAST_SH, 1)

            pe.wait_ge(s_eoff, 1)
            pe.wait_ge(s_w2, 32)
            pe.wait_ge(s_r, NM * NCH)
            pe.wait_ge(s_x3, 2 * LAST_SH)
            up_w = up_sb[:, :, :, :].rearrange("p e k i -> p (e k i)")
            down_w = down_sb[:, :, :].rearrange("p e d -> p (e d)")

            def tilesT(i, h):
                n = 2 * i + h
                pe.wait_ge(s_xt[h], 16 * i + 16)
                if h or since(i, 1):
                    pe.wait_ge(s_eT, n)
                for j in range(UNROLL):
                    for k in range(KC):
                        last = pe.transpose(bank[2 + j // 2][:, ((j % 2) * KC + k) * P:((j % 2) * KC + k + 1) * P],
                                            xt[:, h, j, k * P:(k + 1) * P], ident[:, :])
                last.then_inc(s_eT_ps, 1)

            def expert_offsets(i, h):
                experts = pe.value_load(packed_i[0:1, bass.ds(2 * i + h, 1)], min_val=0, max_val=E ** UNROLL - 1)
                return [pe.snap(((experts >> (4 * j)) & (E - 1)) * D) for j in range(UNROLL)]

            def up(i, h):
                n = 2 * i + h
                pe.wait_ge(s_eT, n + 1)
                if since(i, 1):
                    pe.wait_ge(s_aT, n - 1)
                offs = expert_offsets(i, h)
                for j in range(UNROLL):
                    for k in range(KC):
                        last = pe.matmul(bank[h][:, j * MI:(j + 1) * MI], xtT[:, h, j, k, :],
                                         up_w[:, bass.ds(offs[j] + k * MI, MI)], start=(k == 0), stop=(k == KC - 1))
                last.then_inc(s_h_ps, 1)
                return offs

            def actT(i, h):
                pe.wait_ge(s_ea, 2 * i + (h + 1))
                for j in range(UNROLL):
                    last = pe.transpose(bank[h][:, j * P:(j + 1) * P], ea[:, h, j * MI:(j + 1) * MI], ident[:, :])
                last.then_inc(s_aT_ps, 1)

            def down(i, h, offs):
                n = 2 * i + h
                pe.wait_ge(s_aT, n + 1)
                if since(i, 1):
                    pe.wait_ge(s_y, n - 1)
                for j in range(UNROLL):
                    last = pe.matmul(bank[4 + 2 * h + j // 2][:, (j % 2) * D:(j % 2 + 1) * D],
                                     eaT[:, h, j * P:(j + 1) * P], down_w[:, bass.ds(offs[j], D)],
                                     start=True, stop=True)
                last.then_inc(s_y_ps, 1)

            def expert_step(i):
                offs = [up(i, h) for h in range(2)]
                for h in range(2):
                    actT(i, h)
                    if more_experts(i):
                        tilesT(i + 1, h)
                    down(i, h, offs[h])

            tilesT(0, 0)
            tilesT(0, 1)
            expert_loop(pe, expert_step)
            pe.wait_ge(s_y, 2 * STEPS)
            shared_down(LAST_SH, 0)
            shared_down(LAST_SH, 1)

        @block.vector
        def _(dve):
            def heads_of(w):
                return w.rearrange("p (h d) -> p h d", h=H)

            ch = Chain(dve, s_ch, 31, 0)

            def centre(first, heads):
                means = wmean[:, first:first + len(heads), :]
                for i, w in enumerate(heads):
                    k = ch.done(dve.tensor_reduce(means[:, i, :], w, AX.X, ALU.add))
                ch.need(k)
                ch.link(dve.tensor_scalar(means, means, -1.0 / HD, None, ALU.mult))
                for i, w in enumerate(heads):
                    k = ch.done(dve.tensor_tensor(w, w, means[:, i, :].unsqueeze(2).to_broadcast([P, H, HD]), ALU.add))
                return k

            dve.wait_ge(s_wd, 16 * 2)
            ch.need(centre(0, [heads_of(wkvd_sb[:, 0:D]), heads_of(bkvd_sb[:, 0:D])]))
            dve.sem_inc(s_centred, 1)
            dve.wait_ge(s_w, 16 * 7)
            ch.need(centre(2, [heads_of(wq_sb[:, 0, :]), heads_of(wq_sb[:, 1, :]), heads_of(bq_sb[:, :])] +
                   [kv_heads(w)[:, 0, :, :] for w in (wkv_sb[:, :], bkv_sb[:, :])]))
            dve.sem_inc(s_centred, 1)

            N_LN, N_HV, N_ROOT = 5, 3, 10

            def ln_var(sem_, g, rows, bn_, mv_, col):
                ch = Chain(dve, sem_, N_LN, g)
                for u in range(2):
                    k = ch.done(dve.bn_stats(bn_[:, u, :], rows(u)))
                ch.need_alone(k)
                for u in range(2):
                    k = ch.done(dve.bn_aggr(mv_[:, u, :], bn_[:, u, :]))
                ch.need(k)
                ch.done(dve.tensor_scalar(rst[:, 0, col:col + 2], mv_[:, :, 1], EPS_LN, None, ALU.add))
                ch.end()

            def x_stats(g):
                dve.wait_ge(s_x, 16 * g + 16)
                ln_var(s_ln1, g, lambda u: x_in[:, u, :], bn, mv, 64)

            def head_vars(g):
                ch = Chain(dve, s_hv, N_HV, g)
                dve.wait_ge(s_sq, 2 * g + 2)
                ch.done(dve.tensor_reduce(stat[:, 32:64], sq[:, 1, :, :].rearrange("p b (h d) -> p (b h) d", d=HD),
                                          AX.X, ALU.add))
                ch.link(dve.tensor_reduce(stat[0:MR, 0:32],
                                          sq[0:MR, 0, :, :].rearrange("p b (h d) -> p (b h) d", d=HD),
                                          AX.X, ALU.add))
                ch.done(dve.tensor_scalar(rst[:, 0, 0:64], stat[:, :], 1.0 / HD, EPS_HEAD, ALU.mult, ALU.add))
                ch.end()

            def inverse_roots(i):
                if active(i + 2):
                    dve.wait_ge(s_ln1, N_LN * (i + 3))
                if active(i + 1):
                    dve.wait_ge(s_hv, N_HV * (i + 2))
                if active(i - 2):
                    dve.wait_ge(s_ln2, N_LN * (i - 1))
                if active(i + 1):
                    dve.wait_ge(s_xn, i + 2)
                if active(i - 3):
                    dve.wait_ge(s_xn2, i - 2)
                ch = Chain(dve, s_root, N_ROOT, i + 2)
                v, r, t = rst[:, 0, :], rst[:, 1, :], rst[:, 2, :]
                k = ch.done(root_guess(dve, v, r))
                if active(i):
                    score_max(i, 0, 0)
                ch.need(k)
                k = ch.done(root_square(dve, r, t))
                if active(i):
                    score_max(i, 0, 1)
                ch.need(k)
                k = ch.done(root_error(dve, v, t))
                if active(i):
                    subtract_max(i, 0, 0)
                ch.need(k)
                k = ch.done(root_better(dve, r, t))
                if active(i):
                    subtract_max(i, 0, 1)
                ch.need(k)
                for _ in range(2):
                    ch.link(root_square(dve, r, t))
                    ch.link(root_error(dve, v, t))
                    ch.link(root_better(dve, r, t))
                ch.end()
                for n, (g, mean) in enumerate(((i + 2, mv), (i - 2, mv2))):
                    if active(g):
                        last = dve.scalar_tensor_tensor(shift[:, 2 * n:2 * n + 2], mean[:, :, 0], -1.0,
                                                        rst[:, 1, 64 + 2 * n:66 + 2 * n], ALU.mult, ALU.mult)
                last.then_inc(s_shift, 1)

            def copy_qkv(g):
                dve.wait_ge(s_q_ps, g + 1)
                if since(g, 1):
                    dve.wait_ge(s_qn, 2 * g)
                dve.tensor_tensor(q_sb[:, :, :], bank[5].rearrange("p (u n) -> p u n", u=2),
                                  bq_sb[:, :].unsqueeze(1).to_broadcast([P, 2, D]), ALU.add).then_inc(s_q, 1)
                dve.wait_ge(s_kv_ps, g + 1)
                if since(g, 1):
                    dve.wait_ge(s_v, 128 * g)
                for b in range(2):
                    last = dve.tensor_tensor(kv_sb[0:MR, b, :].rearrange("p (c h d) -> p c h d", c=2, h=H),
                                             kv_heads(kv_ps[b][0:MR, :]), kv_heads(bkv_sb[0:MR, :]), ALU.add)
                last.then_inc(s_kv, 1)

            def normalise_k(g):
                if since(g, 1):
                    dve.wait_ge(s_qn, 2 * g)
                dve.tensor_tensor(q_rstd2[:, :, :, :].rearrange("p u h s -> p (u h) s"),
                                  rst[:, 1, 32:64].unsqueeze(2).to_broadcast([P, 32, 2]),
                                  half[:, :].unsqueeze(1).to_broadcast([P, 32, 2]), ALU.mult).then_inc(s_rstd, 1)
                if since(g, 1):
                    dve.wait_ge(s_kT_ps, g)
                dve.tensor_tensor(kn[0:MR, :].rearrange("p (h b d) -> p b h d", h=H, b=2),
                                  kv_sb[0:MR, :, 0:D].rearrange("p b (h d) -> p b h d", h=H),
                                  rst[0:MR, 1, 0:32].rearrange("p (b h) -> p b h", b=2).unsqueeze(3)
                                  .to_broadcast([MR, 2, H, HD]), ALU.mult).then_inc(s_kn, 1)

            parts = ((0, SM), (SM, SK))
            score_cols = score_ps[:, :].rearrange("p (h k) -> p h k", k=SK)

            def score_max(g, u, c):
                if c == 0:
                    dve.wait_ge(s_s_ps, 2 * g + (u + 1))
                lo, hi = parts[c]
                dve.tensor_reduce(pmax[:, u, c, :], score_cols[:, :, lo:hi], AX.X, ALU.max).then_inc(s_max, 1)

            def subtract_max(g, u, c):
                if c == 0:
                    if since(g, 1):
                        dve.wait_ge(s_pT_ps, 2 * g + (u - 1))
                    elif u == 0:
                        dve.wait_ge(d_vst, 32)
                dve.wait_ge(s_max, 4 * g + (2 * u + c + 1))
                lo, hi = parts[c]
                last = dve.tensor_tensor(probs[:, u, :, lo:hi], score_cols[:, :, lo:hi],
                                         pmax[:, u, c, :].unsqueeze(2).to_broadcast([P, H, hi - lo]), ALU.subtract)
                if c == 1:
                    last.then_inc(s_sub, 1)

            def inverse_sums(g, u):
                dve.wait_ge(s_exp, 2 * g + (u + 1))
                for c, (lo, hi) in enumerate(parts):
                    dve.tensor_reduce(psum_[:, u, c, :], probs[:, u, :, lo:hi], AX.X, ALU.add).then_inc(s_sum, 1)
                if since(g, 1):
                    dve.wait_ge(s_p, 2 * g + (u - 1))
                dve.wait_ge(s_sum, 4 * g + (2 * u + 2))
                dve.reciprocal(prec[:, u, :, :], psum_[:, u, :, :]).then_inc(s_rsum, 1)

            def residual(g):
                dve.wait_ge(s_xbo, g + 1)
                for u in range(2):
                    dve.wait_ge(s_o_ps, 2 * g + (u + 1))
                    row = X2[:, bass.ds(2 * g + u, 1), :].rearrange("p a n -> p (a n)")
                    dve.tensor_tensor(row, bank[2 + u][:, 0:D], row, ALU.add).then_inc(s_x2, 1)

            def residual_stats(g):
                wait_alone(dve, s_x2, 2 * g + 2)
                ln_var(s_ln2, g, lambda u: X2[:, bass.ds(2 * g + u, 1), :].rearrange("p a n -> p (a n)"), bn2, mv2, 66)

            def step(i):
                inverse_roots(i)
                if active(i + 1):
                    normalise_k(i + 1)
                if active(i):
                    inverse_sums(i, 0)
                if active(i - 1):
                    residual(i - 1)
                if active(i):
                    for c in range(2):
                        score_max(i, 1, c)
                    for c in range(2):
                        subtract_max(i, 1, c)
                if active(i - 1):
                    residual_stats(i - 1)
                if active(i + 2):
                    copy_qkv(i + 2)
                if active(i):
                    inverse_sums(i, 1)
                if active(i + 3):
                    x_stats(i + 3)
                if active(i + 2):
                    head_vars(i + 2)

            dve.wait_ge(s_const, N_CONST)
            x_stats(0)
            for n in range(2 * DT):
                dve.wait_ge(d_kv_ps, n + 1)
                dve.tensor_tensor(kv_d[:, n, :], bank[(2 + n) % 8], bkvd_sb[:, :], ALU.add).then_inc(d_kv, 1)
            inverse_roots(-2)
            for n in range(2):
                dve.wait_ge(d_sq, n + 1)
                cols = slice(n * DT * H, (n + 1) * DT * H)
                k = ch.done(dve.tensor_reduce(rst_d[:, 3, cols], sq_d[:, n * DT:(n + 1) * DT, :]
                                              .rearrange("p n (h d) -> p (n h) d", d=HD), AX.X, ALU.add))
            ch.need(k)
            ch.link(dve.tensor_scalar(rst_d[:, 0, :], rst_d[:, 3, :], 1.0 / HD, EPS_HEAD, ALU.mult, ALU.add))
            rsqrt(ch, dve, rst_d[:, 0, :], rst_d[:, 1, :], rst_d[:, 2, :])
            for t in range(DT):
                dve.tensor_tensor(kn_d[:, t, :].rearrange("p (h b d) -> p b h d", h=H, b=2),
                                  kv_d[:, 2 * t:2 * t + 2, 0:D].rearrange("p b (h d) -> p b h d", h=H),
                                  rst_d[:, 1, 2 * t * H:2 * (t + 1) * H].rearrange("p (b h) -> p b h", b=2).unsqueeze(3)
                                  .to_broadcast([P, 2, H, HD]), ALU.mult).then_inc(d_kn, 1)
            iv = ident[:, :].rearrange("p (j s d) -> p s j d", s=2, d=HD)
            for s in range(2):
                k = ch.done(dve.tensor_reduce(slotm[:, s:s + 1], iv[:, s, :, :], AX.XY, ALU.add))
            dve.wait_ge(s_prep_ps, 3)
            ch.need(k)
            dve.tensor_scalar(q_bias2[:, :], slotm[:, :], ln_col[:, 1:2], None, ALU.mult)
            dve.tensor_scalar(k_w4[:, :], quad[:, :], ln_col[:, 2:3], None, ALU.mult)
            dve.tensor_scalar(k_b4[:, :], quad[:, :], ln_col[:, 3:4], None, ALU.mult).then_inc(s_prep, 1)
            ch.end()
            copy_qkv(0)
            x_stats(1)
            head_vars(0)
            main_loop(dve, step)

            dve.wait_ge(s_stT, 32 * GROUPS)
            dve.wait_ge(s_stx, 16 * GROUPS)
            dve.wait_ge(s_ex, 1)
            dve.wait_ge(s_wo, 16 * 4)
            dve.wait_ge(s_iota, 2 + UNROLL)
            ch = Chain(dve, s_rt, 74, 0)
            link = ch.link

            def by_tile(v, n):
                return v.unsqueeze(2).to_broadcast([P, PAIRS, n])

            link(dve.tensor_scalar(sig[:, :, :], sig[:, :, :], 1.0, None, ALU.add))
            link(dve.reciprocal(sig[:, :, :], sig[:, :, :]))
            link(dve.tensor_tensor(sel[:, :, :], sig[:, :, :],
                                   ebias_sb[:, :].unsqueeze(1).to_broadcast([P, PAIRS, E]), ALU.add))
            s4 = sel[:, :, :].rearrange("p t (g e) -> p (t g) e", e=GSZ)
            ch.done(dve.tensor_tensor(pair_sums[:, :, 0:2], s4[:, :, 0:2], s4[:, :, 2:4], ALU.add))
            ch.done(dve.tensor_tensor(pair_sums[:, :, 2:3], s4[:, :, 0:1], s4[:, :, 3:4], ALU.add))
            ch.done(dve.tensor_tensor(pair_sums[:, :, 3:4], s4[:, :, 1:2], s4[:, :, 2:3], ALU.add))
            link(dve.tensor_tensor(pair_sums[:, :, 4:6], s4[:, :, 0:4:2], s4[:, :, 1:4:2], ALU.add))
            gs = gsum[:, :, :]
            link(dve.tensor_reduce(gs.rearrange("p t g -> p (t g)"), pair_sums[:, :, :], AX.X, ALU.max))

            def argmax(values, tmp, onehot, n):
                first = desc[:, :, E - n:E].to_broadcast([P, PAIRS, n])
                link(dve.tensor_reduce(top[:, :], values, AX.X, ALU.max))
                link(dve.tensor_tensor(tmp, values, by_tile(top[:, :], n), ALU.is_equal))
                link(dve.tensor_tensor(tmp, tmp, first, ALU.mult))
                link(dve.tensor_reduce(top[:, :], tmp, AX.X, ALU.max))
                link(dve.tensor_tensor(onehot, tmp, by_tile(top[:, :], n), ALU.is_equal))

            argmax(gs, gtmp[:, :, :], goh[:, 0, :, :], NG)
            link(dve.scalar_tensor_tensor(gs, goh[:, 0, :, :], -BIG, gs, ALU.mult, ALU.add))
            argmax(gs, gtmp[:, :, :], goh[:, 1, :, :], NG)
            link(dve.tensor_tensor(gtmp[:, :, :], goh[:, 0, :, :], goh[:, 1, :, :], ALU.add))
            link(dve.tensor_tensor(s4, s4, gtmp[:, :, :].rearrange("p t g -> p (t g)").unsqueeze(2)
                                   .to_broadcast([P, PAIRS * NG, GSZ]), ALU.mult))
            argmax(sel[:, :, :], etmp[:, :, :], oh[:, 0, :, :], E)
            link(dve.scalar_tensor_tensor(sel[:, :, :], oh[:, 0, :, :], -BIG, sel[:, :, :], ALU.mult, ALU.add))
            argmax(sel[:, :, :], etmp[:, :, :], oh[:, 1, :, :], E)
            dve.tensor_tensor(etmp[:, :, :], oh[:, 0, :, :], oh[:, 1, :, :], ALU.add).then_inc(s_oh, 1)
            def shared_add(i, j):
                dve.wait_ge(s_d_ps, 2 * i + (j + 1))
                for n in range(2):
                    rows = X2[:, bass.ds(8 * i + (4 * j + 2 * n), 2), :]
                    last = dve.tensor_tensor(rows, bank[4 + 2 * j + n].rearrange("p (t d) -> p t d", t=2), rows,
                                             ALU.add)
                last.then_inc(s_x3, 1)

            dve.wait_ge(s_cnt_ps, 1)
            ch.done(dve.tensor_copy(sel[:, :, :].rearrange("p t e -> p (t e)"), bank[0]))
            dve.tensor_copy(tile_cnt[:, :, :].rearrange("p t e -> p (t e)"), bank[1]).then_inc(s_cnt, 1)
            step, cur = 1, 0
            dve.wait_ge(s_cnt, 1)
            third = pair_sums[:, :, :].rearrange("p a b -> p (a b)")[:, 0:PAIRS * E].rearrange("p (t e) -> p t e", e=E)
            src = tile_cnt[:, :, :]
            dsts = [etmp[:, :, :], third]
            while step < PAIRS:
                dst = dsts[cur % 2]
                ch.done(dve.tensor_copy(dst[:, 0:step, :], src[:, 0:step, :]))
                link(dve.tensor_tensor(dst[:, step:, :], src[:, step:, :], src[:, 0:PAIRS - step, :], ALU.add))
                src, step, cur = dst, 2 * step, cur + 1
            link(dve.tensor_tensor(sel[:, :, :], sel[:, :, :], src, ALU.add))
            link(dve.tensor_scalar(count_i[:, 0, :], src[:, PAIRS - 1, :], float(P - 1), None, ALU.add))
            link(dve.tensor_scalar(count_i[:, 1, :], count_i[:, 0, :], 7, None, ALU.logical_shift_right))
            link(dve.tensor_copy(count[:, 0, :], count_i[:, 1, :]))
            step, cur = 1, 0
            while step < E:
                ch.done(dve.tensor_copy(count[:, cur + 1, 0:step], count[:, cur, 0:step]))
                link(dve.tensor_tensor(count[:, cur + 1, step:], count[:, cur, step:], count[:, cur, 0:E - step],
                                       ALU.add))
                step, cur = 2 * step, cur + 1
            ends = count[:, cur, :]
            link(dve.tensor_tensor(count[:, 5, :], ends, count[:, 0, :], ALU.subtract))
            link(dve.tensor_scalar(count[:, 5, :], count[:, 5, :], float(P), None, ALU.mult))
            link(dve.tensor_tensor(sel[:, :, :], sel[:, :, :],
                                   count[:, 5, :].unsqueeze(1).to_broadcast([P, PAIRS, E]), ALU.add))
            for k in range(2):
                link(dve.tensor_tensor(etmp[:, :, :], sel[:, :, :], oh[:, k, :, :], ALU.mult))
                link(dve.tensor_reduce(slot[:, k, :], etmp[:, :, :], AX.X, ALU.add))
            dve.tensor_copy(slot_i[:, :, :], slot[:, :, :]).then_inc(s_slot, 1)
            link(dve.tensor_tensor(past[:, :, :], tile_no[:, :, :].to_broadcast([1, SLOT_TILES, E]),
                                   ends[0:1, :].unsqueeze(1).to_broadcast([1, SLOT_TILES, E]), ALU.is_ge))
            link(dve.tensor_reduce(eoff[:, :, :].rearrange("a s j -> a (s j)"), past[:, :, :], AX.X, ALU.add))
            link(dve.scalar_tensor_tensor(eoff[:, :, :], eoff[:, :, :], float(E - 1), digit[:, :, :]
                                          .to_broadcast([1, SLOT_TILES // UNROLL, UNROLL]), ALU.min, ALU.mult))
            link(dve.tensor_reduce(packed[:, :], eoff[:, :, :], AX.X, ALU.add))
            dve.tensor_copy(packed_i[:, :], packed[:, :]).then_inc(s_eoff, 1)
            for k in range(2):
                link(dve.tensor_tensor(sel[:, :, :], sig[:, :, :], oh[:, k, :, :], ALU.mult))
                link(dve.tensor_reduce(gate[:, k, :], sel[:, :, :], AX.X, ALU.add))
            link(dve.tensor_tensor(gate[:, 2, :], gate[:, 0, :], gate[:, 1, :], ALU.add))
            link(dve.tensor_scalar(gate[:, 2, :], gate[:, 2, :], 1e-20, None, ALU.add))
            link(dve.reciprocal(gate[:, 2, :], gate[:, 2, :]))
            link(dve.tensor_tensor(gate[:, 0:2, :], gate[:, 0:2, :],
                                   gate[:, 2, :].unsqueeze(1).to_broadcast([P, 2, PAIRS]), ALU.mult))
            ch.end()

            shared_add(0, 0)
            shared_add(0, 1)
            with dve.Fori(1, LAST_SH) as i:
                for j in range(2):
                    shared_add(i, j)

            def expert_act(i, h):
                dve.wait_ge(s_er, 2 * i + (h + 1))
                if since(i, 1):
                    dve.wait_ge(s_aT_ps, 2 * i + (h - 1))
                dve.scalar_tensor_tensor(ea[:, h, :], bank[h], 0.0, er[:, h, :], ALU.max, ALU.mult).then_inc(s_ea, 1)

            def expert_out(i, h):
                dve.wait_ge(s_y_ps, 2 * i + (h + 1))
                if since(i, 1):
                    dve.wait_ge(s_ys[h], 16 * i)
                for c in range(2):
                    last = dve.tensor_copy(ey[:, h, 2 * c:2 * c + 2, :],
                                           bank[4 + 2 * h + c].rearrange("p (j d) -> p j d", j=2))
                last.then_inc(s_y, 1)

            def expert_step(i):
                expert_act(i, 0)
                expert_act(i, 1)
                expert_out(i, 0)
                expert_out(i, 1)

            expert_loop(dve, expert_step)
            shared_add(LAST_SH, 0)
            shared_add(LAST_SH, 1)

            def combine(i):
                for h in range(2):
                    dve.wait_ge(s_g[h], 16 * 2 * UNROLL * (i + 1))
                    if since(i, 1):
                        dve.wait_ge(s_out[h], 16 * i)
                    for j in range(UNROLL):
                        t = 2 * UNROLL * i + (UNROLL * h + j)
                        last = dve.scalar_tensor_tensor(res[:, h, j, :], gath[:, h, 0, j, :], gate[:, 0, bass.ds(t, 1)],
                                                        X2[:, bass.ds(t, 1), :].rearrange("p a d -> p (a d)"),
                                                        ALU.mult, ALU.add)
                    last.then_inc(s_gc, 1)
                    dve.wait_ge(s_gc, 2 * i + (h + 1))
                    for j in range(UNROLL):
                        t = 2 * UNROLL * i + (UNROLL * h + j)
                        last = dve.scalar_tensor_tensor(res[:, h, j, :], gath[:, h, 1, j, :], gate[:, 1, bass.ds(t, 1)],
                                                        res[:, h, j, :], ALU.mult, ALU.add)
                    last.then_inc(s_res, 1)

            combine(0)
            with dve.Fori(1, PAIRS // (2 * UNROLL)) as i:
                combine(i)


_INS = ['x', 'ctx_1024', 'L0_xattn_Wq', 'L0_xattn_bq', 'L0_xattn_Wk', 'L0_xattn_bk', 'L0_xattn_Wv', 'L0_xattn_bv',
        'L0_xattn_Wkv_dca', 'L0_xattn_bkv_dca', 'L0_xattn_qn_w', 'L0_xattn_qn_b', 'L0_xattn_kn_w', 'L0_xattn_kn_b',
        'L0_xattn_kn_dca_w', 'L0_xattn_kn_dca_b', 'L0_xattn_Wo', 'L0_xattn_bo', 'L0_ffn_router_weight',
        'L0_ffn_e_bias', 'L0_ffn_w_up', 'L0_ffn_w_down', 'L0_ffn_shared_up', 'L0_ffn_shared_down']


def kernel(**inputs):
    import numpy as _np
    import concourse.bacc as _bacc
    from concourse import mybir as _mybir
    from concourse.bass_utils import run_bass_kernel_spmd as _run

    nc = _bacc.Bacc("TRN2", target_bir_lowering=False, num_devices=1)
    arrays, args = {}, []
    for name in _INS:
        a = _np.ascontiguousarray(inputs[name])
        arrays[f"in_{name}"] = a
        args.append(nc.dram_tensor(f"in_{name}", a.shape, _mybir.dt.from_np(a.dtype), kind="ExternalInput").ap())
    args.append(nc.dram_tensor("out_0", (NB, SQ, D), F32, kind="ExternalOutput").ap())
    xattn_moe(nc, *args)
    r = _run(nc, [arrays], core_ids=[0])
    return r.results[0]["out_0"]
```

```python
from contextlib import ExitStack

import concourse.bass as bass
from concourse import mybir

F32 = mybir.dt.float32
I32 = mybir.dt.int32
ALU = mybir.AluOpType
ACT = mybir.ActivationFunctionType
AX = mybir.AxisListType

P = 128
NB, SQ, D = 64, 64, 256
SK, KD = 64, 128
DCA = 16
SM = SK - DCA
H = 16
HD = D // H
SCALE = HD ** -0.5
EPS_HEAD = 1e-6
EPS_LN = 1e-5
E, MI, SI = 16, 128, 512
NG, GSZ = 4, 4
PAIRS = NB // 2
GROUPS = PAIRS // 2
SETS = H // 4
MR = 2 * SM
CW = 4 * SK
HP = H // 2
TT = PAIRS // 2
SLOT_TILES = 48
N_CONST = 12
DT = PAIRS // 8
UNROLL = 4
GT = 2
SLOTS = SLOT_TILES * P
KC = D // P
SCH = 512
NCH = NB * SQ // SCH
NM = SI // P
HSTEPS = SLOT_TILES // (2 * UNROLL)
STEPS = 2 * HSTEPS
GSTEPS = TT // (2 * GT)
COMBINE = HSTEPS + 1
SH_FIRST = NCH // 4
BIG = 1e30


class Chain:

    def __init__(self, eng, sem, per_step, step):
        self.eng, self.sem, self.per, self.n = eng, sem, per_step, 0
        self.base = step * per_step

    def done(self, ins):
        self.n += 1
        ins.then_inc(self.sem, 1)
        return self.n

    def need(self, k):
        self.eng.wait_ge(self.sem, self.base + k)

    def need_alone(self, k):
        self.wait_alone(self.eng, self.sem, self.base + k)

    def link(self, ins):
        self.need(self.done(ins))

    def end(self):
        assert self.n == self.per, (self.n, self.per)


def xattn_moe(nc, x, ctx, Wq, bq, Wk, bk, Wv, bv, Wkvd, bkvd, qn_w, qn_b, kn_w, kn_b, kd_w, kd_b, Wo, bo,
              router, e_bias, w_up, w_down, sh_up, sh_down, out):
    stack = ExitStack()
    with stack:
        def sb(name, shape, dt=F32):
            return stack.enter_context(nc.sbuf_tensor(name, shape, dt))

        def sem(name):
            return stack.enter_context(nc.semaphore(name))

        bank = [stack.enter_context(nc.psum_tensor(f"bank{i}", [P, 512], F32)) for i in range(4, 8)]
        score_ps = stack.enter_context(nc.psum_tensor("score_ps", [P, 2 * 512], F32))
        probsT_ps = stack.enter_context(nc.psum_tensor("probsT_ps", [P, 2, 512], F32))
        bank = [score_ps[:, 0:512], score_ps[:, 512:1024], probsT_ps[:, 0, :], probsT_ps[:, 1, :]] + \
               [b[:, :] for b in bank]

        vd_dram = nc.dram_tensor("vd_dram", [PAIRS * DCA, 2 * D], F32, kind="Internal").ap()
        vd_blocks = vd_dram.rearrange("(u t k) n -> t u k n", u=8, k=DCA)
        xn2T_dram = nc.dram_tensor("xn2T_dram", [KC, P, NB * SQ], F32, kind="Internal").ap()
        slot_x = [nc.dram_tensor(f"slot_x{f}", [SLOTS, D], F32, kind="Internal").ap() for f in range(2)]
        slot_y = [nc.dram_tensor(f"slot_y{f}", [SLOTS, D], F32, kind="Internal").ap() for f in range(2)]

        ident = sb("ident", [P, P])
        tri = sb("tri", [P, P])
        ones = sb("ones", [P, P])
        zeros = sb("zeros", [P, D])
        half = sb("half", [P, 2])
        slotm = sb("slotm", [P, 2])
        quad = sb("quad", [P, 4])
        wq_sb = sb("wq_sb", [P, KC, D])
        wkv_sb = sb("wkv_sb", [P, 2 * D])
        wkvd_sb = sb("wkvd_sb", [P, 2 * D])
        wo_sb = sb("wo_sb", [P, KC, D])
        bq_sb = sb("bq_sb", [P, D])
        bkv_sb = sb("bkv_sb", [P, 2 * D])
        bkvd_sb = sb("bkvd_sb", [P, 2 * D])
        bo_sb = sb("bo_sb", [P, D])
        router_in = sb("router_in", [E, D])
        router_sb = sb("router_sb", [P, KC, E])
        ebias_sb = sb("ebias_sb", [P, E])
        ln_in = sb("ln_in", [6, P])
        ln_col = sb("ln_col", [P, 6])
        q_bias2 = sb("q_bias2", [P, 2])
        k_w4 = sb("k_w4", [P, 4])
        k_b4 = sb("k_b4", [P, 4])
        su_sb = sb("su_sb", [P, KC, SI])
        sd_sb = sb("sd_sb", [P, SI // P, D])
        wmean = sb("wmean", [P, 7, H])
        X2 = sb("X2", [P, PAIRS, D])
        XN2 = sb("XN2", [P, PAIRS, D])
        logits = sb("logits", [P, PAIRS, E])
        xT_ch = sb("xT_ch", [P, 2, KC, SCH])
        kdT = sb("kdT", [P, PAIRS, SETS, DCA])
        sig = sb("sig", [P, PAIRS, E])
        sel = sb("sel", [P, PAIRS, E])
        pair_sums = sb("pair_sums", [P, TT * NG, 6])
        gsum = sb("gsum", [P, TT, NG])
        gtmp = sb("gtmp", [P, TT, NG])
        goh = sb("goh", [P, 2, TT, NG])
        oh = sb("oh", [P, 2, PAIRS, E])
        etmp = sb("etmp", [P, PAIRS, E])
        tile_cnt = sb("tile_cnt", [P, PAIRS, E])
        top = sb("top", [P, TT])
        gate = sb("gate", [P, 3, PAIRS])
        slot = sb("slot", [P, 2, PAIRS])
        slot_i = sb("slot_i", [P, 2, PAIRS], I32)
        count = sb("count", [P, 6, E])
        count_i = sb("count_i", [P, 2, E], I32)
        tile_no = sb("tile_no", [1, SLOT_TILES, 1])
        past = sb("past", [1, SLOT_TILES, E])
        eoff = sb("eoff", [1, SLOT_TILES // UNROLL, UNROLL])
        digit = sb("digit", [1, 1, UNROLL])
        packed = sb("packed", [1, 2 * HSTEPS])
        packed_i = sb("packed_i", [1, HSTEPS, 2], I32)
        experts_i = sb("experts_i", [1, STEPS], I32)
        desc = sb("desc", [P, 1, E])
        loop_stack = ExitStack()

        def sbl(name, shape, dt=F32):
            return loop_stack.enter_context(nc.sbuf_tensor(name, shape, dt))

        x_in = sbl("x_in", [P, 2, D])
        y_in = sbl("y_in", [P, 2, KD])
        xn = sbl("xn", [P, 2, D])
        xnT = sbl("xnT", [P, 2, KC, P])
        yT = sbl("yT", [P, 2, P])
        q_sb = sbl("q_sb", [P, 2, D])
        kv_sb = sbl("kv_sb", [P, 2, 2 * D])
        sq = sbl("sq", [P, 2, 2, D])
        qn = sbl("qn", [P, 2, 2 * D])
        kn = sbl("kn", [P, 2 * D])
        stat = sbl("stat", [P, 64])
        rst = sbl("rst", [P, 3, 68])
        q_rstd2 = sbl("q_rstd2", [P, 2, H, 2])
        qT = sbl("qT", [P, 2, SETS, P])
        k_bd = sbl("k_bd", [P, 2, SETS, 4, SK])
        v_rep = sbl("v_rep", [P, 2, 2 * D])
        v_bd = sbl("v_bd", [P, 2, 2 * D])
        probs = sbl("probs", [P, 2, H, SK])
        pmax = sbl("pmax", [P, 2, 2, H])
        psum_ = sbl("psum_", [P, 2, 2, H])
        prec = sbl("prec", [P, 2, 2, H])
        probsT = sbl("probsT", [P, 2, 2, 512])
        ctxT = sbl("ctxT", [P, 2, KC, P])
        xn2 = sbl("xn2", [P, 2, D])
        xn2T = sbl("xn2T", [P, KC, 2, P])
        bn = sbl("bn", [P, 2, 6])
        mv = sbl("mv", [P, 2, 2])
        bn2 = sbl("bn2", [P, 2, 6])
        mv2 = sbl("mv2", [P, 2, 2])
        shift = sbl("shift", [P, 4])
        rst_d = sbl("rst_d", [P, 4, 2 * DT * H])
        y_d = X2[:, 0:DT, :].rearrange("p n (c d) -> p (n c) d", c=2)
        yT_d = X2[:, DT:2 * DT, :].rearrange("p n (c d) -> p (n c) d", c=2)
        kv_d = XN2[:, 0:4 * DT, :].rearrange("p (n c) d -> p n (c d)", c=2)
        sq_d = XN2[:, 4 * DT:6 * DT, :]
        kn_d = XN2[:, 6 * DT:8 * DT, :].rearrange("p (t c) d -> p t (c d)", c=2)

        loop_stack.close()
        relu = sb("relu", [P, 2, SCH])
        hid = sb("hid", [P, 2, SI // P, SCH])
        up_sb = sb("up_sb", [P, E, KC, MI])
        down_sb = sb("down_sb", [P, E, D])
        er = [wkv_sb[:, :], wkvd_sb[:, :]]
        ea = sb("ea", [P, 2, UNROLL * P])
        tile_w = sb("tile_w", [P, 2, UNROLL, KC * MI])
        gidx = sb("gidx", [P, 2, 2, 2, GT], I32)
        xt = XN2[:, 0:2 * UNROLL, :].rearrange("p (h j) d -> p h j d", h=2)
        xtT = XN2[:, 2 * UNROLL:4 * UNROLL, :].rearrange("p (h j) (k n) -> p h j k n", h=2, k=KC)
        ey = sb("ey", [P, 2, UNROLL, D])
        gath = [kdT[:, :, :, :].rearrange("p (h k j t) s d -> p h k j (t s d)", h=2, k=2, j=GT),
                XN2[:, 4 * UNROLL:4 * UNROLL + 4 * GT, :].rearrange("p (h k j) d -> p h k j d", h=2, k=2)]
        res = sb("res", [P, 2, GT, D])

        s_alone = sem("waits_alone")
        s_wd = sem("dca_weights_loaded")
        s_wl = sem("head_vectors_loaded")
        s_w = sem("projection_weights_loaded")
        s_wo = sem("output_weights_loaded")
        s_w1 = sem("shared_weights_loaded")
        s_w2 = sem("ffn_weights_loaded")
        s_zero = sem("slots_zeroed")
        s_const = sem("constants_ready")
        s_prep = sem("weights_prepared")
        s_prep_ps = sem("prep_transposed")
        s_x = sem("x_loaded")
        s_y_in = sem("context_loaded")
        s_ch = sem("setup_chain")
        s_centred = sem("weights_centred")
        s_ln1 = sem("first_layernorm_stats")
        s_hv = sem("head_variances")
        s_ln2 = sem("second_layernorm_stats")
        s_root = sem("inverse_roots")
        s_shift = sem("layernorm_shifts")
        s_max = sem("score_maxima")
        s_sum = sem("softmax_sums")
        s_xbo = sem("x_plus_bo_stored")
        s_xn = sem("xn_ready")
        s_yT_ps = sem("yT_in_psum")
        s_xT_ps = sem("xT_in_psum")
        s_yT = sem("yT_ready")
        s_xT = sem("xT_ready")
        s_kv_ps = sem("kv_in_psum")
        s_q_ps = sem("q_in_psum")
        s_kv = sem("kv_ready")
        s_q = sem("q_ready")
        s_sq = sem("squares_ready")
        s_rstd = sem("head_rstd_ready")
        s_kn = sem("kn_ready")
        s_qn = sem("qn_ready")
        s_kT_ps = sem("kT_in_psum")
        s_qT_ps = sem("qT_in_psum")
        s_kbd = sem("k_main_blocks_ready")
        s_kbdd = sem("k_dca_blocks_ready")
        s_qT = sem("qT_ready")
        s_v = sem("v_replicated")
        s_vbd = sem("v_blocks_ready")
        s_s_ps = sem("scores_in_psum")
        s_sub = sem("scores_minus_max")
        s_exp = sem("exp_ready")
        s_rsum = sem("inverse_sums_ready")
        s_p = sem("probs_ready")
        s_pT_ps = sem("probsT_in_psum")
        s_pT = sem("probsT_ready")
        s_c_ps = sem("ctxT_in_psum")
        s_c = sem("ctxT_ready")
        s_o_ps = sem("attn_out_in_psum")
        s_x2 = sem("residual_stored")
        s_xn2 = sem("xn2_ready")
        s_x2T_ps = sem("xn2T_in_psum")
        s_x2T = sem("xn2T_ready")
        s_l_ps = sem("logits_in_psum")
        s_l = sem("logits_stored")
        s_stx = sem("xn2_stored")
        s_stT = sem("xn2T_stored")
        d_in = sem("dca_rows_loaded")
        d_yT_ps = sem("dca_yT_in_psum")
        d_yT = sem("dca_yT_ready")
        d_kv_ps = sem("dca_kv_in_psum")
        d_kv = sem("dca_kv_ready")
        d_sq = sem("dca_squares_ready")
        d_kn = sem("dca_kn_ready")
        d_kT_ps = sem("dca_kT_in_psum")
        d_kT = sem("dca_kT_stored")
        d_vst = sem("dca_v_stored")

        s_iota = sem("tile_numbers_ready")
        s_xTc = [sem(f"xT_chunk_loaded{j}") for j in range(2)]
        s_u_ps = sem("shared_up_in_psum")
        s_r = sem("shared_relu_ready")
        s_hid = sem("shared_hidden_ready")
        s_d_ps = sem("shared_down_in_psum")
        s_x3 = sem("shared_added")
        s_ex = sem("router_exp_ready")
        s_oh = sem("experts_chosen")
        s_cnt_ps = sem("ranks_in_psum")
        s_cnt = sem("ranks_copied")
        s_slot = sem("slots_ready")
        s_eoff = sem("tile_experts_ready")
        s_rt = sem("routing_chain")
        s_scat = [sem(f"rows_scattered{f}") for f in range(2)]
        s_xt = [sem(f"slot_tiles_loaded{h}") for h in range(2)]
        s_eT_ps = sem("slot_tilesT_in_psum")
        s_eT = sem("slot_tilesT_ready")
        s_h_ps = sem("expert_up_in_psum")
        s_er = sem("expert_relu_ready")
        s_ea = sem("expert_act_ready")
        s_tw = sem("tile_weights_copied")
        s_y_ps = sem("expert_out_in_psum")
        s_y = sem("expert_out_ready")
        s_ys = [sem(f"expert_out_stored{h}") for h in range(2)]
        s_gidx = sem("gather_indices_ready")
        s_g = [[sem(f"rows_gathered{b}{h}") for h in range(2)] for b in range(2)]
        s_gc = sem("first_rows_added")
        s_used = sem("gathered_rows_used")
        s_res = sem("result_ready")
        s_out = [sem(f"result_stored{h}") for h in range(2)]

        x_rows = x.rearrange("b s d -> (b s) d")
        out_rows = out.rearrange("b s d -> (b s) d")

        def row1(v):
            return v.rearrange("(a n) -> a n", a=1)

        def all_rows(v, n=P):
            return v.partition_broadcast(n)

        def root_guess(dve, v, r):
            return dve.tensor_scalar(r.bitcast(I32), v.bitcast(I32), -0.5, float(0x5F3759DF), ALU.mult, ALU.add)

        def root_square(dve, r, t):
            return dve.tensor_tensor(t, r, r, ALU.mult)

        def root_error(dve, v, t):
            return dve.scalar_tensor_tensor(t, t, -0.5, v, ALU.mult, ALU.mult)

        def root_better(dve, r, t):
            return dve.scalar_tensor_tensor(r, t, 1.5, r, ALU.add, ALU.mult)

        def rsqrt(ch, dve, v, r, t):
            ch.link(root_guess(dve, v, r))
            for _ in range(3):
                ch.link(root_square(dve, r, t))
                ch.link(root_error(dve, v, t))
                ch.link(root_better(dve, r, t))

        def kv_heads(ap):
            return ap.rearrange("p (h c d) -> p c h d", c=2, d=HD)

        def wait_alone(eng, sem_, value):
            eng.wait_ge(sem_, value)
            eng.sem_inc(s_alone, 1)

        Chain.wait_alone = staticmethod(wait_alone)

        def is_first(g):
            return isinstance(g, int) and g == 0

        def active(g):
            return not isinstance(g, int) or 0 <= g < GROUPS

        def since(g, n):
            return not isinstance(g, int) or g >= n

        def main_loop(eng, step):
            for i in range(-1, 3):
                step(i)
            with eng.Fori(3, GROUPS - 3) as i:
                step(i)
            for i in range(GROUPS - 3, GROUPS + 2):
                step(i)

        def expert_loop(eng, step):
            step(0)
            with eng.Fori(1, STEPS - 1) as i:
                step(i)
            step(STEPS - 1)

        def tile_experts(eng, i):
            experts = eng.value_load(experts_i[0:1, bass.ds(i, 1)])
            return [[eng.snap(((experts >> (4 * (UNROLL * h + j))) & (E - 1)) * D) for j in range(UNROLL)]
                    for h in range(2)]

        def more_experts(i):
            return not isinstance(i, int) or i + 1 < STEPS

        kv_ps = [bank[0], bank[1]]
        rank_ps = [[bank[5], bank[6]], [bank[0], bank[1]]]
        dca_bank = [bank[2], bank[3], bank[6], bank[7]]
        ctx_ps = [bank[5], bank[7]]

        block = stack.enter_context(nc.Block())

        @block.sync
        def _(sp):
            sp.dma_start(wkvd_sb[:, :], Wkvd).then_inc(s_wd, 16)
            sp.dma_start(bkvd_sb[:, :], all_rows(bkvd)).then_inc(s_wd, 16)
            for u in range(8):
                sp.dma_start(y_d[u * DCA:(u + 1) * DCA, :, :],
                             ctx[8 * u:8 * u + 8, SM:SK, :].rearrange("n k d -> k n d")).then_inc(d_in, 16)

            def load_x(g):
                if since(g, 1):
                    sp.wait_ge(s_xn, g)
                    sp.wait_ge(s_xbo, g)
                sp.dma_start(x_in[:, :, :], x_rows[bass.ds(256 * g, 256), :].rearrange("(u p) d -> p u d", p=P))\
                    .then_inc(s_x, 16)

            def load_y(g):
                if since(g, 1):
                    sp.wait_ge(s_yT_ps, g)
                for u in range(2):
                    sp.dma_start(y_in[u * SM:(u + 1) * SM, :, :],
                                 ctx[bass.ds(4 * g + 2 * u, 2), 0:SM, :].rearrange("b k d -> k b d"))\
                        .then_inc(s_y_in, 16)

            load_x(0)
            for k in range(KC):
                sp.dma_start(wq_sb[:, k, :], Wq[k * P:(k + 1) * P, :]).then_inc(s_w, 16)
            sp.dma_start(bq_sb[:, :], all_rows(bq)).then_inc(s_w, 16)
            sp.dma_start(wkv_sb[:, 0:D], Wk).then_inc(s_w, 16)
            sp.dma_start(wkv_sb[:, D:], Wv).then_inc(s_w, 16)
            sp.dma_start(bkv_sb[:, 0:D], all_rows(bk)).then_inc(s_w, 16)
            sp.dma_start(bkv_sb[:, D:], all_rows(bv)).then_inc(s_w, 16)
            load_y(0)
            for i, v in enumerate((qn_w, qn_b, kn_w, kn_b, kd_w, kd_b)):
                sp.dma_start(ln_in[i:i + 1, :].rearrange("a (r d) -> a r d", d=HD),
                             row1(v).unsqueeze(1).to_broadcast([1, P // HD, HD])).then_inc(s_wl, 16)
            sp.dma_start(router_in[:, :], router).then_inc(s_wl, 16)
            sp.dma_start(bo_sb[:, :], all_rows(bo)).then_inc(s_wo, 16)
            for k in range(KC):
                sp.dma_start(wo_sb[:, k, :], Wo[k * P:(k + 1) * P, :]).then_inc(s_wo, 16)
            sp.dma_start(ebias_sb[:, :], all_rows(e_bias)).then_inc(s_wo, 16)

            def store_dca():
                sp.wait_ge(d_kv, 2 * DT)
                for t in range(DT):
                    for b in range(2):
                        sp.dma_start(vd_blocks[t, :, :, b * D:(b + 1) * D], kv_d[:, 2 * t + b, D:]).then_inc(d_vst, 16)
                sp.wait_ge(d_vst, 16 * 2 * DT)

            def replicate_v(g):
                wait_alone(sp, s_kv, g + 1)
                if since(g, 1):
                    sp.wait_ge(s_vbd, g)
                for c in range(2):
                    for u in range(2):
                        sp.dma_start(v_rep[64 * c:64 * c + SM, u, :].rearrange("p (b n) -> p b n", b=2),
                                     kv_sb[u * SM:(u + 1) * SM, :, D:]).then_inc(s_v, 16)
                        sp.dma_start(v_rep[64 * c + SM:64 * c + SK, u, :],
                                     vd_dram[bass.ds(2 * DCA * g + DCA * u, DCA), :]).then_inc(s_v, 16)

            def store_xn2(g):
                sp.wait_ge(s_xn2, g + 1)
                sp.dma_start(XN2[:, bass.ds(2 * g, 2), :], xn2[:, :, :]).then_inc(s_stx, 16)

            def store_xn2T(g):
                sp.wait_ge(s_x2T, g + 1)
                for k in range(KC):
                    sp.dma_start(xn2T_dram[k, :, bass.ds(256 * g, 256)],
                                 xn2T[:, k, :, :].rearrange("p u n -> p (u n)")).then_inc(s_stT, 16)

            def zero_slots(g):
                rows = SLOTS // GROUPS
                for f in range(2):
                    sp.dma_start(slot_x[f][bass.ds(rows * g, rows), :].rearrange("(t p) d -> p t d", p=P),
                                 zeros[:, :].unsqueeze(1).to_broadcast([P, rows // P, D])).then_inc(s_zero, 16)

            def step(i):
                if active(i + 1):
                    replicate_v(i + 1)
                if active(i + 3):
                    load_y(i + 3)
                    load_x(i + 3)
                if active(i - 2):
                    store_xn2(i - 2)
                    store_xn2T(i - 2)
                if active(i):
                    zero_slots(i)
                if isinstance(i, int) and i == GROUPS - 1:
                    sp.wait_ge(s_stT, 32 * (GROUPS - 3))
                    load_chunks(0)

            def load_chunks(i):
                for j in range(2):
                    sp.dma_start(xT_ch[:, j, :, :],
                                 xn2T_dram[:, :, bass.ds(SCH * 2 * i + SCH * j, SCH)].rearrange("k p n -> p k n"))\
                        .then_inc(s_xTc[j], 16)

            store_dca()
            load_y(1)
            load_x(1)
            main_loop(sp, step)

            sp.wait_ge(s_stT, 32 * GROUPS)
            sp.wait_ge(s_stx, 16 * GROUPS)
            for i in range(1, SH_FIRST + 1):
                sp.wait_ge(s_u_ps, 2 * NM * i)
                load_chunks(i)

            def tiles(dram, n):
                return dram[bass.ds(UNROLL * P * n, UNROLL * P), :].rearrange("(j p) d -> p j d", p=P)

            def load_tiles(f, i, h):
                if since(i, 1):
                    wait_alone(sp, s_eT_ps, 2 * i + (h - 1))
                sp.dma_start(xt[:, h, :, :], tiles(slot_x[f], 2 * i + (h - 2 * HSTEPS * f))).then_inc(s_xt[h], 16)

            def store_tiles(f, i, h):
                wait_alone(sp, s_y, 2 * i + (h + 1))
                sp.dma_start(tiles(slot_y[f], 2 * i + (h - 2 * HSTEPS * f)), ey[:, h, :, :]).then_inc(s_ys[h], 16)

            def store_out(n, h, rows):
                sp.dma_start(out_rows[bass.ds(2 * GT * P * n + GT * P * h, GT * P), :]
                             .rearrange("(j p) d -> p j d", p=P), rows).then_inc(s_out[h], 16)

            sp.wait_ge(s_scat[0], 16 * 2 * TT)
            for i in range(2):
                for h in range(2):
                    load_tiles(0, i, h)
            with sp.Fori(0, HSTEPS - 2) as i:
                for h in range(2):
                    load_tiles(0, i + 2, h)
                    store_tiles(0, i, h)
            sp.wait_ge(s_scat[1], 16 * 2 * TT)
            for i in range(HSTEPS - 2, HSTEPS):
                for h in range(2):
                    load_tiles(1, i + 2, h)
                    store_tiles(0, i, h)
            with sp.Fori(HSTEPS, STEPS - 2) as i:
                for h in range(2):
                    load_tiles(1, i + 2, h)
                    store_tiles(1, i, h)
            for i in range(STEPS - 2, STEPS):
                for h in range(2):
                    store_tiles(1, i, h)
            with sp.Fori(0, GSTEPS) as n:
                for h in range(2):
                    sp.wait_ge(s_used, 2 * n + (h + 1))
                    store_out(n, h, X2[:, bass.ds(2 * GT * n + GT * h, GT), :])
            for i in range(SH_FIRST + 1, NCH // 2):
                sp.wait_ge(s_u_ps, 2 * NM * i)
                load_chunks(i)
            with sp.Fori(GSTEPS, 2 * GSTEPS) as n:
                for h in range(2):
                    sp.wait_ge(s_res, 2 * n + (h + 1 - 2 * GSTEPS))
                    store_out(n, h, res[:, h, :, :])
            for h in range(2):
                sp.wait_ge(s_out[h], 16 * 2 * GSTEPS)
            sp.wait_ge(s_alone, 4 * GROUPS + 4 * GSTEPS + 4 * STEPS - 2)

        @block.gpsimd
        def _(pool):
            pool.memset(ones[:, :], 1.0).then_inc(s_const, 1)
            pool.memset(zeros[:, :], 0.0).then_inc(s_const, 1)
            pool.memset(ident[:, :], 0.0).then_inc(s_const, 1)
            pool.memset(stat[:, :], 1.0).then_inc(s_const, 1)
            pool.memset(kv_sb[:, :, :], 0.0).then_inc(s_const, 1)
            pool.memset(rst[:, 0, :], 1.0).then_inc(s_const, 1)
            pool.wait_ge(s_const, 6)
            pool.affine_select(out=ident[:, :], in_=ident[:, :], compare_op=ALU.not_equal, fill=1.0, base=0,
                               pattern=[[-1, P]], channel_multiplier=1).then_inc(s_const, 1)
            pool.affine_select(out=tri[:, :], in_=zeros[:, 0:P], compare_op=ALU.is_gt, fill=-1.0, base=0,
                               pattern=[[1, P]], channel_multiplier=-1).then_inc(s_const, 1)
            pool.affine_select(out=half[:, :], in_=ones[:, 0:2], compare_op=ALU.is_ge, fill=0.0, base=0,
                               pattern=[[-64, 2]], channel_multiplier=1).then_inc(s_const, 1)
            pool.affine_select(out=quad[:, :], in_=ones[:, 0:4], compare_op=ALU.is_ge, fill=0.0, base=0,
                               pattern=[[-32, 4]], channel_multiplier=1).then_inc(s_const, 1)
            pool.wait_ge(s_const, 10)
            pool.affine_select(out=half[:, :], in_=half[:, :], compare_op=ALU.is_ge, fill=0.0, base=63,
                               pattern=[[64, 2]], channel_multiplier=-1).then_inc(s_const, 1)
            pool.affine_select(out=quad[:, :], in_=quad[:, :], compare_op=ALU.is_ge, fill=0.0, base=31,
                               pattern=[[32, 4]], channel_multiplier=-1).then_inc(s_const, 1)

            pool.iota(tile_no[:, :, :], pattern=[[1, SLOT_TILES]], base=0, channel_multiplier=0,
                      allow_small_or_imprecise_dtypes=True).then_inc(s_iota, 1)
            for j in range(UNROLL):
                pool.memset(digit[:, :, j:j + 1], float(E ** j)).then_inc(s_iota, 1)
            pool.iota(desc[:, :, :], pattern=[[-1, E]], base=E, channel_multiplier=0,
                      allow_small_or_imprecise_dtypes=True).then_inc(s_iota, 1)

            def add_bo(g):
                pool.wait_ge(s_x, 16 * g + 16)
                pool.tensor_tensor(X2[:, bass.ds(2 * g, 2), :], x_in[:, :, :],
                                   bo_sb[:, :].unsqueeze(1).to_broadcast([P, 2, D]), ALU.add).then_inc(s_xbo, 1)

            def normalise_k(g):
                pool.wait_ge(s_rstd, g + 1)
                if since(g, 1):
                    pool.wait_ge(s_kT_ps, g)
                pool.tensor_tensor(kn[0:MR, :].rearrange("p (h b d) -> p b h d", h=H, b=2),
                                  kv_sb[0:MR, :, 0:D].rearrange("p b (h d) -> p b h d", h=H),
                                  rst[0:MR, 1, 0:32].rearrange("p (b h) -> p b h", b=2).unsqueeze(3)
                                  .to_broadcast([MR, 2, H, HD]), ALU.mult).then_inc(s_kn, 1)

            def normalise_q(g):
                pool.wait_ge(s_rstd, g + 1)
                if since(g, 1):
                    pool.wait_ge(s_qT_ps, 2 * g)
                for u in range(2):
                    pool.tensor_tensor(qn[:, u, :].rearrange("p (h s d) -> p h s d", h=H, s=2),
                                       q_sb[:, u, :].rearrange("p (h d) -> p h d", h=H).unsqueeze(2)
                                       .to_broadcast([P, H, 2, HD]),
                                       q_rstd2[:, u, :, :].unsqueeze(3).to_broadcast([P, H, 2, HD]),
                                       ALU.mult).then_inc(s_qn, 1)

            def dca_blocks(g):
                if is_first(g):
                    pool.wait_ge(d_kT, DT)
                else:
                    pool.wait_ge(s_s_ps, 2 * g)
                for j in range(4):
                    last = pool.tensor_tensor(k_bd[:, :, :, j, SM:SK], kdT[:, bass.ds(2 * g, 2), :, :],
                                              quad[:, j:j + 1].unsqueeze(1).unsqueeze(1)
                                              .to_broadcast([P, 2, SETS, DCA]), ALU.mult)
                last.then_inc(s_kbdd, 1)

            def normalise_probs(g, u):
                pool.wait_ge(s_rsum, 2 * g + (u + 1))
                for c, (lo, hi) in enumerate(((0, SM), (SM, SK))):
                    last = pool.tensor_tensor(probs[:, u, :, lo:hi], probs[:, u, :, lo:hi],
                                              prec[:, u, c, :].unsqueeze(2).to_broadcast([P, H, hi - lo]), ALU.mult)
                last.then_inc(s_p, 1)

            pool.wait_ge(s_wo, 16 * 4)
            pool.wait_ge(d_kv, 2 * DT)
            pool.wait_ge(s_const, N_CONST)

            def step(i):
                if active(i + 1):
                    normalise_k(i + 1)
                    normalise_q(i + 1)
                if active(i):
                    normalise_probs(i, 0)
                if active(i + 2):
                    add_bo(i + 2)
                if active(i + 1):
                    dca_blocks(i + 1)
                if active(i):
                    normalise_probs(i, 1)

            add_bo(0)
            main_loop(pool, step)

            pool.wait_ge(s_zero, 32 * GROUPS)
            pool.wait_ge(s_stx, 16 * GROUPS)
            for f in range(2):
                pool.wait_ge(s_slot, f + 1)
                for t in range(TT * f, TT * f + TT):
                    for k in range(2):
                        pool.indirect_dma_start(slot_x[f][:, :],
                                                bass.IndirectOffsetOnAxis(ap=slot_i[:, k, t:t + 1], axis=0),
                                                XN2[:, t, :], None).then_inc(s_scat[f], 16)

            def gather(f, m):
                for b in range(2):
                    n = 2 * m + b
                    for h in range(2):
                        if since(m, 1):
                            pool.wait_ge(s_used, 2 * n + (h - 3))
                        pool.tensor_copy(gidx[:, b, h, :, :], slot_i[:, :, bass.ds(2 * GT * n + GT * h, GT)])\
                            .then_inc(s_gidx, 1)
                        wait_alone(pool, s_gidx, 2 * n + (h + 1))
                        for j in range(GT):
                            for k in range(2):
                                pool.indirect_dma_start(gath[b][:, h, k, j, :], None, slot_y[f][:, :],
                                                        bass.IndirectOffsetOnAxis(ap=gidx[:, b, h, k, j:j + 1], axis=0))\
                                    .then_inc(s_g[b][h], 16)

            for h in range(2):
                pool.wait_ge(s_ys[h], 16 * HSTEPS)
            pool.wait_ge(s_scat[1], 16 * 2 * TT)
            gather(0, 0)
            with pool.Fori(1, GSTEPS // 2) as m:
                gather(0, m)
            for h in range(2):
                pool.wait_ge(s_ys[h], 16 * STEPS)
            with pool.Fori(GSTEPS // 2, GSTEPS) as m:
                gather(1, m)

        @block.scalar
        def _(act):
            def evac(dst, src):
                return act.activation(dst, src, ACT.Copy)

            def copy_yT(g):
                act.wait_ge(s_yT_ps, g + 1)
                if since(g, 1):
                    act.wait_ge(s_kv_ps, g)
                evac(yT[:, :, 0:MR], bank[5][:, 0:2 * MR].rearrange("p (b n) -> p b n", b=2)).then_inc(s_yT, 1)

            def copy_xT(g):
                act.wait_ge(s_xT_ps, g + 1)
                if since(g, 1):
                    act.wait_ge(s_q_ps, g)
                evac(xnT[:, :, :, :], bank[6].rearrange("p (u k n) -> p u k n", u=2, k=KC)).then_inc(s_xT, 1)

            def normalise_x(g):
                act.wait_ge(s_shift, g + 1)
                if since(g, 1):
                    act.wait_ge(s_xT_ps, g)
                for u in range(2):
                    last = act.activation(xn[:, u, :], x_in[:, u, :], ACT.Identity, bias=shift[:, u:u + 1],
                                          scale=rst[:, 1, 64 + u:65 + u])
                last.then_inc(s_xn, 1)

            def normalise_x2(g):
                act.wait_ge(s_shift, g + 5)
                if since(g, 1):
                    act.wait_ge(s_x2T_ps, g)
                    act.wait_ge(s_stx, 16 * g)
                for u in range(2):
                    row = X2[:, bass.ds(2 * g + u, 1), :].rearrange("p a n -> p (a n)")
                    last = act.activation(xn2[:, u, :], row, ACT.Identity, bias=shift[:, 2 + u:3 + u],
                                          scale=rst[:, 1, 66 + u:67 + u])
                last.then_inc(s_xn2, 1)

            def squares(g):
                act.wait_ge(s_q, g + 1)
                act.activation(sq[:, 1, :, :], q_sb[:, :, :], ACT.Square).then_inc(s_sq, 1)
                act.wait_ge(s_kv, g + 1)
                act.activation(sq[0:MR, 0, :, :], kv_sb[0:MR, :, 0:D], ACT.Square).then_inc(s_sq, 1)

            def main_blocks(g):
                act.wait_ge(s_kT_ps, g + 1)
                if since(g, 1):
                    act.wait_ge(s_s_ps, 2 * g)
                src = bank[4][:, 0:SETS * MR].rearrange("p (s u k) -> p s u k", s=SETS, u=2)
                for j in range(4):
                    dst = k_bd[:, :, :, j, 0:SM].rearrange("p u s k -> p s u k")
                    last = act.activation(dst, src, ACT.Identity, bias=k_b4[:, j:j + 1], scale=k_w4[:, j:j + 1])
                last.then_inc(s_kbd, 1)

            def copy_qT(g, u):
                act.wait_ge(s_qT_ps, 2 * g + (u + 1))
                src = bank[6 + u].rearrange("p (s n) -> p s n", s=SETS)
                for s in range(2):
                    last = act.activation(qT[:, u, :, 64 * s:64 * s + 64], src[:, :, 64 * s:64 * s + 64],
                                          ACT.Identity, bias=q_bias2[:, s:s + 1], scale=ln_col[:, 0:1])
                last.then_inc(s_qT, 1)

            def mask_v(g):
                act.wait_ge(s_v, 128 * g + 128)
                vr = v_rep[:, :, :].rearrange("p u (n s d) -> p (u n) s d", s=2, d=HD)
                vb = v_bd[:, :, :].rearrange("p u (n s d) -> p (u n) s d", s=2, d=HD)
                for s in range(2):
                    last = act.activation(vb[:, :, s, :], vr[:, :, s, :], ACT.Copy, scale=half[:, s:s + 1])
                last.then_inc(s_vbd, 1)

            def exponent(g, u):
                act.wait_ge(s_sub, 2 * g + (u + 1))
                act.activation(probs[:, u, :, :], probs[:, u, :, :], ACT.Exp, scale=SCALE).then_inc(s_exp, 1)

            def copy_probsT(g, u):
                act.wait_ge(s_pT_ps, 2 * g + (u + 1))
                evac(probsT[:, u, :, :], probsT_ps[:, :, :]).then_inc(s_pT, 1)

            def copy_ctx(g, u):
                act.wait_ge(s_c_ps, 2 * g + (u + 1))
                if since(g, 1):
                    act.wait_ge(s_o_ps, 2 * g + (u - 1))
                evac(ctxT[:, u, :, :], ctx_ps[u][:, 0:256].rearrange("p (c n) -> p c n", c=KC))\
                    .then_inc(s_c, 1)

            def copy_xn2T(g):
                act.wait_ge(s_x2T_ps, g + 1)
                if since(g, 1):
                    act.wait_ge(s_l_ps, g)
                    act.wait_ge(s_stT, 32 * g)
                evac(xn2T[:, :, :, :].rearrange("p k u n -> p u k n"),
                     bank[7].rearrange("p (u k n) -> p u k n", u=2, k=KC)).then_inc(s_x2T, 1)

            def copy_logits(g):
                act.wait_ge(s_l_ps, g + 1)
                evac(logits[:, bass.ds(2 * g, 2), :], bank[4][:, 0:2 * E].rearrange("p (u e) -> p u e", u=2))\
                    .then_inc(s_l, 1)

            def router_exp(f):
                act.wait_ge(s_l, GROUPS // 2 * (f + 1))
                act.activation(sig[:, TT * f:TT * f + TT, :], logits[:, TT * f:TT * f + TT, :], ACT.Exp, scale=-1.0)\
                    .then_inc(s_ex, 1)

            def step(i):
                if active(i - 1):
                    copy_ctx(i - 1, 1)
                if active(i):
                    mask_v(i)
                    exponent(i, 0)
                if active(i + 2):
                    normalise_x(i + 2)
                    copy_yT(i + 2)
                if active(i - 2):
                    normalise_x2(i - 2)
                if active(i + 2):
                    copy_xT(i + 2)
                if active(i - 2):
                    copy_xn2T(i - 2)
                if active(i + 1):
                    main_blocks(i + 1)
                if active(i):
                    exponent(i, 1)
                if active(i + 1):
                    copy_qT(i + 1, 0)
                if active(i):
                    copy_probsT(i, 0)
                if active(i + 2):
                    squares(i + 2)
                if active(i + 1):
                    copy_qT(i + 1, 1)
                if active(i - 2):
                    copy_logits(i - 2)
                if active(i):
                    copy_ctx(i, 0)
                    copy_probsT(i, 1)
                if isinstance(i, int) and i == GROUPS:
                    router_exp(0)

            for n in range(2):
                act.wait_ge(d_yT_ps, n + 1)
                evac(yT_d[:, DT * n:DT * n + DT, :], bank[n].rearrange("p (n k) -> p n k", n=DT)).then_inc(d_yT, 1)
            for n in range(2):
                act.wait_ge(d_kv, DT * n + DT)
                act.activation(sq_d[:, DT * n:DT * n + DT, :], kv_d[:, DT * n:DT * n + DT, 0:D], ACT.Square)\
                    .then_inc(d_sq, 1)
            copy_yT(0)
            normalise_x(0)
            copy_xT(0)
            act.wait_ge(s_prep_ps, 1)
            evac(ln_col[:, :], bank[4][:, 0:6]).then_inc(s_prep_ps, 1)
            evac(router_sb[:, :, :], bank[4][:, 16:16 + KC * E].rearrange("p (k e) -> p k e", k=KC))\
                .then_inc(s_prep_ps, 1)
            act.wait_ge(s_prep_ps, 3)
            for t in range(DT):
                act.wait_ge(d_kT_ps, t + 1)
                act.activation(kdT[:, :, :, :].rearrange("p (u t) s k -> p t u s k", t=DT)[:, t, :, :, :],
                               dca_bank[t].rearrange("p (s u k) -> p u s k", s=SETS, u=8), ACT.Identity,
                               bias=ln_col[:, 5:6], scale=ln_col[:, 4:5]).then_inc(d_kT, 1)
            squares(0)
            act.dma_start(su_sb[:, :, :], sh_up.rearrange("(k p) n -> p k n", p=P)).then_inc(s_w1, 16)
            act.dma_start(sd_sb[:, :, :], sh_down.rearrange("(k p) n -> p k n", p=P)).then_inc(s_w1, 16)
            act.wait_ge(s_prep, 1)

            main_loop(act, step)

            router_exp(1)

            def shared_step(i):
                for j in range(2):
                    for m in range(NM):
                        n = j * NM + m
                        act.wait_ge(s_u_ps, 2 * NM * i + (n + 1))
                        act.activation(relu[:, n % 2, :], bank[m], ACT.Relu).then_inc(s_r, 1)
                        if m == 0 and not is_first(i):
                            act.wait_ge(s_d_ps, 2 * i - 1 + j)
                        act.wait_ge(s_r, 2 * NM * i + (n + 1))
                        act.activation(hid[:, j, m, :], relu[:, n % 2, :], ACT.Square).then_inc(s_hid, 1)

            shared_step(0)
            act.wait_ge(s_stT, 32 * GROUPS)
            act.wait_ge(s_stx, 16 * GROUPS)
            act.dma_start(up_sb[:, :, :, :], w_up.rearrange("e (k p) i -> p e k i", p=P)).then_inc(s_w2, 16)
            act.dma_start(down_sb[:, :, :], w_down.rearrange("e i d -> i e d")).then_inc(s_w2, 16)
            for i in range(1, SH_FIRST):
                shared_step(i)

            def copy_tilesT(i, h):
                n = 2 * i + h
                act.wait_ge(s_eT_ps, n + 1)
                if since(i, 1):
                    act.wait_ge(s_h_ps, n - 1)
                for c in range(2):
                    last = evac(xtT[:, h, 2 * c:2 * c + 2, :, :],
                                bank[2 + c].rearrange("p (j k n) -> p j k n", j=2, k=KC))
                last.then_inc(s_eT, 1)

            up_w = up_sb[:, :, :, :].rearrange("p e k i -> p (e k i)")

            def copy_weights(h, offs):
                for j in range(UNROLL):
                    last = evac(tile_w[:, h, j, :], up_w[:, bass.ds(offs[j], KC * MI)])
                last.then_inc(s_tw, 1)

            def hidden(i, h):
                act.wait_ge(s_h_ps, 2 * i + (h + 1))
                act.activation(er[h], bank[h], ACT.Relu).then_inc(s_er, 1)

            def expert_step(i):
                if more_experts(i):
                    offs = tile_experts(act, i + 1)
                hidden(i, 0)
                if more_experts(i):
                    copy_weights(0, offs[0])
                hidden(i, 1)
                if more_experts(i):
                    copy_tilesT(i + 1, 0)
                    copy_weights(1, offs[1])
                    copy_tilesT(i + 1, 1)

            act.wait_ge(s_eoff, 2)
            act.wait_ge(s_w2, 32)
            offs = tile_experts(act, 0)
            for h in range(2):
                copy_weights(h, offs[h])
                copy_tilesT(0, h)
            expert_loop(act, expert_step)
            with act.Fori(SH_FIRST, NCH // 2) as i:
                shared_step(i)

        @block.tensor
        def _(pe):
            pe.wait_ge(s_const, N_CONST)
            pe.wait_ge(d_in, 16 * 8)
            for n in range(2):
                for m in range(DT):
                    last = pe.transpose(bank[n][:, m * P:(m + 1) * P], y_d[:, n * DT + m, :], ident[:, :])
                last.then_inc(d_yT_ps, 1)
            pe.wait_ge(s_centred, 1)
            pe.wait_ge(d_yT, 2)
            for n in range(2 * DT):
                pe.matmul(bank[(2 + n) % 8], yT_d[:, n, :], wkvd_sb[:, :], start=True, stop=True).then_inc(d_kv_ps, 1)

            def transpose_y(g):
                pe.wait_ge(s_y_in, 32 * g + 32)
                if since(g, 3):
                    pe.wait_ge(s_c, 2 * g - 5)
                elif since(g, 1):
                    pe.wait_ge(s_q, g)
                for b in range(2):
                    last = pe.transpose(bank[5][:, b * MR:(b + 1) * MR], y_in[0:MR, b, :], ident[0:MR, 0:MR])
                last.then_inc(s_yT_ps, 1)

            def transpose_x(g):
                pe.wait_ge(s_xn, g + 1)
                for u in range(2):
                    for k in range(KC):
                        last = pe.transpose(bank[6][:, (u * KC + k) * P:(u * KC + k + 1) * P],
                                            xn[:, u, k * P:(k + 1) * P], ident[:, :])
                last.then_inc(s_xT_ps, 1)

            def project_q(g):
                pe.wait_ge(s_yT, g + 1)
                pe.wait_ge(s_xT, g + 1)
                for u in range(2):
                    for k in range(KC):
                        last = pe.matmul(bank[5][:, u * D:(u + 1) * D], xnT[:, u, k, :], wq_sb[:, k, :],
                                         start=(k == 0), stop=(k == KC - 1))
                last.then_inc(s_q_ps, 1)

            def project_kv(g):
                if since(g, 2):
                    pe.wait_ge(s_sub, 2 * g - 2)
                for b in range(2):
                    last = pe.matmul(kv_ps[b][0:MR, :], yT[:, b, 0:MR], wkv_sb[:, :], start=True, stop=True)
                last.then_inc(s_kv_ps, 1)

            def transpose_k(g):
                pe.wait_ge(s_kn, g + 1)
                if since(g, 4):
                    pe.wait_ge(s_l, g - 3)
                for s in range(SETS):
                    last = pe.transpose(bank[4][:, s * MR:(s + 1) * MR], kn[0:MR, s * P:(s + 1) * P],
                                        ident[0:MR, 0:MR])
                last.then_inc(s_kT_ps, 1)

            def transpose_q(g, u):
                pe.wait_ge(s_qn, 2 * g + (u + 1))
                if u == 0 and active(g + 1):
                    pe.wait_ge(s_xT, g + 2)
                if u == 1 and since(g, 3):
                    pe.wait_ge(s_x2T, g - 2)
                for s in range(SETS):
                    last = pe.transpose(bank[6 + u][:, s * P:(s + 1) * P], qn[:, u, s * P:(s + 1) * P],
                                        ident[:, :])
                last.then_inc(s_qT_ps, 1)

            def scores(g, u):
                pe.wait_ge(s_qT, 2 * g + (u + 1))
                if u == 0:
                    pe.wait_ge(s_kbd, g + 1)
                    pe.wait_ge(s_kbdd, g + 1)
                if u == 0 and active(g + 1):
                    pe.wait_ge(s_kv, g + 2)
                else:
                    pe.wait_ge(s_sub, 2 * g + u)
                for s in range(SETS):
                    last = pe.matmul(score_ps[:, s * CW:(s + 1) * CW], qT[:, u, s, :],
                                     k_bd[:, u, s, :, :].rearrange("p j k -> p (j k)"), start=True, stop=True)
                last.then_inc(s_s_ps, 1)

            def transpose_probs(g, u):
                pe.wait_ge(s_p, 2 * g + (u + 1))
                if u == 1:
                    pe.wait_ge(s_pT, 2 * g + 1)
                elif since(g, 1):
                    pe.wait_ge(s_x2, 2 * g)
                flat = probs[:, u, :, :].rearrange("p h k -> p (h k)")
                for n in range(HP):
                    last = pe.transpose(probsT_ps[:, n // 4, (n % 4) * P:(n % 4 + 1) * P], flat[:, n * P:(n + 1) * P],
                                        ident[:, :])
                last.then_inc(s_pT_ps, 1)

            def probs_v(g, u):
                if u == 0:
                    pe.wait_ge(s_vbd, g + 1)
                    if active(g + 2):
                        pe.wait_ge(s_q, g + 3)
                elif active(g + 1):
                    pe.wait_ge(s_qT, 2 * g + 4)
                else:
                    pe.wait_ge(s_x2T, g - 1)
                pe.wait_ge(s_pT, 2 * g + (u + 1))
                for c in range(2):
                    for n in range(HP // 2):
                        for b in range(2):
                            col = P * c + 64 * b
                            last = pe.matmul(ctx_ps[u][32 * n:32 * n + 32, col:col + 64],
                                             v_bd[:, u, b * D + (4 * c + n) * 32:b * D + (4 * c + n) * 32 + 32],
                                             probsT[:, u, c, n * P + 64 * b:n * P + 64 * b + 64],
                                             start=True, stop=True)
                last.then_inc(s_c_ps, 1)

            def attn_out(g):
                for u in range(2):
                    pe.wait_ge(s_c, 2 * g + (u + 1))
                    for k in range(KC):
                        last = pe.matmul(bank[2 + u][:, 0:D], ctxT[:, u, k, :], wo_sb[:, k, :],
                                         start=(k == 0), stop=(k == KC - 1))
                    last.then_inc(s_o_ps, 1)

            def transpose_xn2(g):
                pe.wait_ge(s_xn2, g + 1)
                for u in range(2):
                    for k in range(KC):
                        last = pe.transpose(bank[7][:, (u * KC + k) * P:(u * KC + k + 1) * P],
                                            xn2[:, u, k * P:(k + 1) * P], ident[:, :])
                last.then_inc(s_x2T_ps, 1)

            def route(g):
                pe.wait_ge(s_x2T, g + 1)
                if active(g + 3):
                    pe.wait_ge(s_kbd, g + 4)
                for u in range(2):
                    for k in range(KC):
                        last = pe.matmul(bank[4][:, u * E:(u + 1) * E], xn2T[:, k, u, :], router_sb[:, k, :],
                                         start=(k == 0), stop=(k == KC - 1))
                last.then_inc(s_l_ps, 1)

            def step(i):
                if isinstance(i, int) and i == GROUPS + 1:
                    pe.wait_ge(s_w1, 32)
                    pe.wait_ge(s_x2, 2 * GROUPS)
                    shared_up(0, 0)
                if active(i + 2):
                    transpose_y(i + 2)
                if active(i - 1):
                    attn_out(i - 1)
                if active(i):
                    scores(i, 1)
                if active(i + 2):
                    transpose_x(i + 2)
                if active(i + 1):
                    transpose_k(i + 1)
                if active(i - 2):
                    transpose_xn2(i - 2)
                if active(i + 2):
                    project_q(i + 2)
                if active(i + 1):
                    transpose_q(i + 1, 0)
                if active(i + 2):
                    project_kv(i + 2)
                if active(i + 1):
                    transpose_q(i + 1, 1)
                if active(i):
                    transpose_probs(i, 0)
                if active(i - 2):
                    route(i - 2)
                if active(i):
                    probs_v(i, 0)
                if active(i + 1):
                    scores(i + 1, 0)
                if active(i):
                    transpose_probs(i, 1)
                    probs_v(i, 1)

            def shared_up(i, j, blocks=range(NM)):
                pe.wait_ge(s_xTc[j], 16 * i + 16)
                for m in blocks:
                    if j or not is_first(i):
                        pe.wait_ge(s_r, 2 * NM * i + (j * NM + m + 1 - NM))
                    for k in range(KC):
                        last = pe.matmul(bank[m], su_sb[:, k, m * P:(m + 1) * P], xT_ch[:, j, k, :],
                                         start=(k == 0), stop=(k == KC - 1))
                    last.then_inc(s_u_ps, 1)

            def shared_down(i, j):
                pe.wait_ge(s_hid, 2 * NM * i + NM * (j + 1))
                if since(i, SH_FIRST + 1):
                    pe.wait_ge(s_res, 4 * (i - SH_FIRST) + (2 * j - 2))
                elif since(i, 1):
                    pe.wait_ge(s_x3, 2 * i - 1 + j)
                for t in range(SCH // P):
                    o = bank[4 + 2 * j + t // 2][:, (t % 2) * D:(t % 2 + 1) * D]
                    for m in range(NM):
                        last = pe.matmul(o, hid[:, j, m, t * P:(t + 1) * P], sd_sb[:, m, :],
                                         start=(m == 0), stop=(m == NM - 1))
                last.then_inc(s_d_ps, 1)

            pe.wait_ge(d_kv, 4)
            transpose_y(0)
            pe.wait_ge(d_kv, 2 * DT)
            transpose_x(0)
            pe.wait_ge(s_centred, 2)
            project_q(0)
            project_kv(0)
            pe.wait_ge(s_wl, 16 * 7)
            pe.wait_ge(d_kv, 3)
            pe.transpose(bank[4][:, 0:6], ln_in[:, :], ident[0:6, 0:6])
            for k in range(KC):
                last = pe.transpose(bank[4][:, 16 + k * E:16 + (k + 1) * E], router_in[:, k * P:(k + 1) * P],
                                    ident[0:E, 0:E])
            last.then_inc(s_prep_ps, 1)
            for t in range(DT):
                pe.wait_ge(d_kn, t + 1)
                if t == 2:
                    pe.wait_ge(s_xT, 1)
                for s in range(SETS):
                    last = pe.transpose(dca_bank[t][:, s * P:(s + 1) * P], kn_d[:, t, s * P:(s + 1) * P], ident[:, :])
                last.then_inc(d_kT_ps, 1)
            pe.wait_ge(s_prep_ps, 3)
            pe.wait_ge(d_kT, DT)
            pe.wait_ge(s_wo, 16 * 4)

            main_loop(pe, step)

            def ranks(f):
                pe.wait_ge(s_oh, f + 1)
                chosen = etmp[:, TT * f:TT * f + TT, :].rearrange("p t e -> p (t e)")
                for n, counts in enumerate((tri, ones)):
                    last = pe.matmul(rank_ps[f][n][:, 0:TT * E], counts[:, :], chosen, start=True, stop=True)
                last.then_inc(s_cnt_ps, 1)

            shared_up(0, 1, range(NM - 1))
            ranks(0)
            shared_up(0, 1, range(NM - 1, NM))
            pe.wait_ge(s_cnt, 1)
            pe.wait_ge(s_l, GROUPS)
            shared_down(0, 0)
            shared_down(0, 1)
            shared_up(1, 0)
            shared_up(1, 1)
            pe.wait_ge(s_r, 4 * NM)
            ranks(1)
            shared_down(1, 0)
            shared_down(1, 1)

            down_w = down_sb[:, :, :].rearrange("p e d -> p (e d)")

            def tilesT(i, h):
                n = 2 * i + h
                pe.wait_ge(s_xt[h], 16 * i + 16)
                if h or since(i, 1):
                    pe.wait_ge(s_eT, n)
                for j in range(UNROLL):
                    for k in range(KC):
                        last = pe.transpose(bank[2 + j // 2][:, ((j % 2) * KC + k) * P:((j % 2) * KC + k + 1) * P],
                                            xt[:, h, j, k * P:(k + 1) * P], ident[:, :])
                last.then_inc(s_eT_ps, 1)

            def up(i, h):
                n = 2 * i + h
                pe.wait_ge(s_tw, n + 1)
                pe.wait_ge(s_eT, n + 1)
                if since(i, 1):
                    pe.wait_ge(s_ea, n - 1)
                for j in range(UNROLL):
                    for k in range(KC):
                        last = pe.matmul(bank[h][:, j * P:(j + 1) * P], tile_w[:, h, j, k * MI:(k + 1) * MI],
                                         xtT[:, h, j, k, :], start=(k == 0), stop=(k == KC - 1))
                last.then_inc(s_h_ps, 1)

            def down(i, h, offs):
                n = 2 * i + h
                pe.wait_ge(s_ea, n + 1)
                if since(i, 1):
                    pe.wait_ge(s_y, n - 1)
                else:
                    pe.wait_ge(s_x3, 2 * SH_FIRST - 1 + h)
                for j in range(UNROLL):
                    last = pe.matmul(bank[4 + 2 * h + j // 2][:, (j % 2) * D:(j % 2 + 1) * D],
                                     ea[:, h, j * P:(j + 1) * P], down_w[:, bass.ds(offs[j], D)],
                                     start=True, stop=True)
                last.then_inc(s_y_ps, 1)

            def expert_step(i):
                offs = tile_experts(pe, i)
                for h in range(2):
                    up(i, h)
                for h in range(2):
                    if more_experts(i):
                        tilesT(i + 1, h)
                    down(i, h, offs[h])

            pe.wait_ge(s_r, 2 * NM * SH_FIRST)
            tilesT(0, 0)
            tilesT(0, 1)
            pe.wait_ge(s_eoff, 2)
            pe.wait_ge(s_w2, 32)
            expert_loop(pe, expert_step)
            for i in range(SH_FIRST, NCH // 2):
                shared_up(i, 0)
                shared_up(i, 1)
                if i == SH_FIRST:
                    pe.wait_ge(s_y, 2 * STEPS)
                shared_down(i, 0)
                shared_down(i, 1)

        @block.vector
        def _(dve):
            def heads_of(w):
                return w.rearrange("p (h d) -> p h d", h=H)

            ch = Chain(dve, s_ch, 31, 0)

            def centre(first, heads):
                means = wmean[:, first:first + len(heads), :]
                for i, w in enumerate(heads):
                    k = ch.done(dve.tensor_reduce(means[:, i, :], w, AX.X, ALU.add))
                ch.need(k)
                ch.link(dve.tensor_scalar(means, means, -1.0 / HD, None, ALU.mult))
                for i, w in enumerate(heads):
                    k = ch.done(dve.tensor_tensor(w, w, means[:, i, :].unsqueeze(2).to_broadcast([P, H, HD]), ALU.add))
                return k

            dve.wait_ge(s_wd, 16 * 2)
            ch.need(centre(0, [heads_of(wkvd_sb[:, 0:D]), heads_of(bkvd_sb[:, 0:D])]))
            dve.sem_inc(s_centred, 1)
            dve.wait_ge(s_w, 16 * 7)
            ch.need(centre(2, [heads_of(wq_sb[:, 0, :]), heads_of(wq_sb[:, 1, :]), heads_of(bq_sb[:, :])] +
                   [kv_heads(w)[:, 0, :, :] for w in (wkv_sb[:, :], bkv_sb[:, :])]))
            dve.sem_inc(s_centred, 1)

            N_LN, N_HV, N_ROOT = 5, 3, 10

            def ln_var(sem_, g, rows, bn_, mv_, col):
                ch = Chain(dve, sem_, N_LN, g)
                for u in range(2):
                    k = ch.done(dve.bn_stats(bn_[:, u, :], rows(u)))
                ch.need_alone(k)
                for u in range(2):
                    k = ch.done(dve.bn_aggr(mv_[:, u, :], bn_[:, u, :]))
                ch.need(k)
                ch.done(dve.tensor_scalar(rst[:, 0, col:col + 2], mv_[:, :, 1], EPS_LN, None, ALU.add))
                ch.end()

            def x_stats(g):
                dve.wait_ge(s_x, 16 * g + 16)
                ln_var(s_ln1, g, lambda u: x_in[:, u, :], bn, mv, 64)

            def head_vars(g):
                ch = Chain(dve, s_hv, N_HV, g)
                dve.wait_ge(s_sq, 2 * g + 2)
                ch.done(dve.tensor_reduce(stat[:, 32:64], sq[:, 1, :, :].rearrange("p b (h d) -> p (b h) d", d=HD),
                                          AX.X, ALU.add))
                ch.link(dve.tensor_reduce(stat[0:MR, 0:32],
                                          sq[0:MR, 0, :, :].rearrange("p b (h d) -> p (b h) d", d=HD),
                                          AX.X, ALU.add))
                ch.done(dve.tensor_scalar(rst[:, 0, 0:64], stat[:, :], 1.0 / HD, EPS_HEAD, ALU.mult, ALU.add))
                ch.end()

            def inverse_roots(i):
                if active(i + 2):
                    dve.wait_ge(s_ln1, N_LN * (i + 3))
                if active(i + 1):
                    dve.wait_ge(s_hv, N_HV * (i + 2))
                if active(i - 2):
                    dve.wait_ge(s_ln2, N_LN * (i - 1))
                if active(i + 1):
                    dve.wait_ge(s_xn, i + 2)
                if active(i) and active(i + 1):
                    dve.wait_ge(s_kn, i + 1)
                if active(i - 3):
                    dve.wait_ge(s_xn2, i - 2)
                ch = Chain(dve, s_root, N_ROOT, i + 2)
                v, r, t = rst[:, 0, :], rst[:, 1, :], rst[:, 2, :]
                k = ch.done(root_guess(dve, v, r))
                if active(i):
                    score_max(i, 0, 0)
                ch.need(k)
                k = ch.done(root_square(dve, r, t))
                if active(i):
                    score_max(i, 0, 1)
                ch.need(k)
                k = ch.done(root_error(dve, v, t))
                if active(i):
                    subtract_max(i, 0, 0)
                ch.need(k)
                k = ch.done(root_better(dve, r, t))
                if active(i):
                    subtract_max(i, 0, 1)
                ch.need(k)
                for _ in range(2):
                    ch.link(root_square(dve, r, t))
                    ch.link(root_error(dve, v, t))
                    ch.link(root_better(dve, r, t))
                ch.end()
                for n, (g, mean) in enumerate(((i + 2, mv), (i - 2, mv2))):
                    if active(g):
                        last = dve.scalar_tensor_tensor(shift[:, 2 * n:2 * n + 2], mean[:, :, 0], -1.0,
                                                        rst[:, 1, 64 + 2 * n:66 + 2 * n], ALU.mult, ALU.mult)
                last.then_inc(s_shift, 1)

            def copy_qkv(g):
                dve.wait_ge(s_q_ps, g + 1)
                if since(g, 1):
                    dve.wait_ge(s_qn, 2 * g)
                dve.tensor_tensor(q_sb[:, :, :], bank[5].rearrange("p (u n) -> p u n", u=2),
                                  bq_sb[:, :].unsqueeze(1).to_broadcast([P, 2, D]), ALU.add).then_inc(s_q, 1)
                dve.wait_ge(s_kv_ps, g + 1)
                if since(g, 1):
                    dve.wait_ge(s_v, 128 * g)
                    dve.wait_ge(s_kn, g)
                for b in range(2):
                    last = dve.tensor_tensor(kv_sb[0:MR, b, :].rearrange("p (c h d) -> p c h d", c=2, h=H),
                                             kv_heads(kv_ps[b][0:MR, :]), kv_heads(bkv_sb[0:MR, :]), ALU.add)
                last.then_inc(s_kv, 1)

            def spread_roots(g):
                if since(g, 1):
                    dve.wait_ge(s_qn, 2 * g)
                dve.tensor_tensor(q_rstd2[:, :, :, :].rearrange("p u h s -> p (u h) s"),
                                  rst[:, 1, 32:64].unsqueeze(2).to_broadcast([P, 32, 2]),
                                  half[:, :].unsqueeze(1).to_broadcast([P, 32, 2]), ALU.mult).then_inc(s_rstd, 1)

            parts = ((0, SM), (SM, SK))
            score_cols = score_ps[:, :].rearrange("p (h k) -> p h k", k=SK)

            def score_max(g, u, c):
                if c == 0:
                    dve.wait_ge(s_s_ps, 2 * g + (u + 1))
                lo, hi = parts[c]
                dve.tensor_reduce(pmax[:, u, c, :], score_cols[:, :, lo:hi], AX.X, ALU.max).then_inc(s_max, 1)

            def subtract_max(g, u, c):
                if c == 0:
                    if since(g, 1):
                        dve.wait_ge(s_pT_ps, 2 * g + (u - 1))
                    elif u == 0:
                        dve.wait_ge(d_vst, 16 * 2 * DT)
                dve.wait_ge(s_max, 4 * g + (2 * u + c + 1))
                lo, hi = parts[c]
                last = dve.tensor_tensor(probs[:, u, :, lo:hi], score_cols[:, :, lo:hi],
                                         pmax[:, u, c, :].unsqueeze(2).to_broadcast([P, H, hi - lo]), ALU.subtract)
                if c == 1:
                    last.then_inc(s_sub, 1)

            def inverse_sums(g, u):
                dve.wait_ge(s_exp, 2 * g + (u + 1))
                for c, (lo, hi) in enumerate(parts):
                    dve.tensor_reduce(psum_[:, u, c, :], probs[:, u, :, lo:hi], AX.X, ALU.add).then_inc(s_sum, 1)
                if since(g, 1):
                    dve.wait_ge(s_p, 2 * g + (u - 1))
                dve.wait_ge(s_sum, 4 * g + (2 * u + 2))
                dve.reciprocal(prec[:, u, :, :], psum_[:, u, :, :]).then_inc(s_rsum, 1)

            def residual(g):
                dve.wait_ge(s_xbo, g + 1)
                for u in range(2):
                    dve.wait_ge(s_o_ps, 2 * g + (u + 1))
                    row = X2[:, bass.ds(2 * g + u, 1), :].rearrange("p a n -> p (a n)")
                    dve.tensor_tensor(row, bank[2 + u][:, 0:D], row, ALU.add).then_inc(s_x2, 1)

            def residual_stats(g):
                wait_alone(dve, s_x2, 2 * g + 2)
                ln_var(s_ln2, g, lambda u: X2[:, bass.ds(2 * g + u, 1), :].rearrange("p a n -> p (a n)"), bn2, mv2, 66)

            def step(i):
                inverse_roots(i)
                if active(i - 1):
                    residual(i - 1)
                if active(i + 1):
                    spread_roots(i + 1)
                if active(i):
                    inverse_sums(i, 0)
                    for c in range(2):
                        score_max(i, 1, c)
                    for c in range(2):
                        subtract_max(i, 1, c)
                if active(i - 1):
                    residual_stats(i - 1)
                if active(i + 2):
                    copy_qkv(i + 2)
                if active(i):
                    inverse_sums(i, 1)
                if active(i + 3):
                    x_stats(i + 3)
                if active(i + 2):
                    head_vars(i + 2)

            dve.wait_ge(s_const, N_CONST)
            x_stats(0)
            for n in range(2 * DT):
                dve.wait_ge(d_kv_ps, n + 1)
                dve.tensor_tensor(kv_d[:, n, :], bank[(2 + n) % 8], bkvd_sb[:, :], ALU.add).then_inc(d_kv, 1)
            inverse_roots(-2)
            for n in range(2):
                dve.wait_ge(d_sq, n + 1)
                cols = slice(n * DT * H, (n + 1) * DT * H)
                k = ch.done(dve.tensor_reduce(rst_d[:, 3, cols], sq_d[:, n * DT:(n + 1) * DT, :]
                                              .rearrange("p n (h d) -> p (n h) d", d=HD), AX.X, ALU.add))
            ch.need(k)
            ch.link(dve.tensor_scalar(rst_d[:, 0, :], rst_d[:, 3, :], 1.0 / HD, EPS_HEAD, ALU.mult, ALU.add))
            rsqrt(ch, dve, rst_d[:, 0, :], rst_d[:, 1, :], rst_d[:, 2, :])
            for t in range(DT):
                dve.tensor_tensor(kn_d[:, t, :].rearrange("p (h b d) -> p b h d", h=H, b=2),
                                  kv_d[:, 2 * t:2 * t + 2, 0:D].rearrange("p b (h d) -> p b h d", h=H),
                                  rst_d[:, 1, 2 * t * H:2 * (t + 1) * H].rearrange("p (b h) -> p b h", b=2).unsqueeze(3)
                                  .to_broadcast([P, 2, H, HD]), ALU.mult).then_inc(d_kn, 1)
            iv = ident[:, :].rearrange("p (j s d) -> p s j d", s=2, d=HD)
            for s in range(2):
                k = ch.done(dve.tensor_reduce(slotm[:, s:s + 1], iv[:, s, :, :], AX.XY, ALU.add))
            dve.wait_ge(s_prep_ps, 3)
            ch.need(k)
            dve.tensor_scalar(q_bias2[:, :], slotm[:, :], ln_col[:, 1:2], None, ALU.mult)
            dve.tensor_scalar(k_w4[:, :], quad[:, :], ln_col[:, 2:3], None, ALU.mult)
            dve.tensor_scalar(k_b4[:, :], quad[:, :], ln_col[:, 3:4], None, ALU.mult).then_inc(s_prep, 1)
            ch.end()
            copy_qkv(0)
            x_stats(1)
            head_vars(0)
            main_loop(dve, step)

            def by_tile(v, n):
                return v.unsqueeze(2).to_broadcast([P, TT, n])

            def argmax(link, values, tmp, onehot, n):
                first = desc[:, :, E - n:E].to_broadcast([P, TT, n])
                link(dve.tensor_reduce(top[:, :], values, AX.X, ALU.max))
                link(dve.tensor_tensor(tmp, values, by_tile(top[:, :], n), ALU.is_equal))
                link(dve.tensor_tensor(tmp, tmp, first, ALU.mult))
                link(dve.tensor_reduce(top[:, :], tmp, AX.X, ALU.max))
                link(dve.tensor_tensor(onehot, tmp, by_tile(top[:, :], n), ALU.is_equal))

            def choose(f, ch):
                link = ch.link
                half_tiles = slice(TT * f, TT * f + TT)
                score, choice, tmp = (b[:, half_tiles, :] for b in (sig, sel, etmp))
                first, second = oh[:, 0, half_tiles, :], oh[:, 1, half_tiles, :]
                dve.wait_ge(s_ex, f + 1)
                link(dve.tensor_scalar(score, score, 1.0, None, ALU.add))
                link(dve.reciprocal(score, score))
                link(dve.tensor_tensor(choice, score, ebias_sb[:, :].unsqueeze(1).to_broadcast([P, TT, E]), ALU.add))
                s4 = choice.rearrange("p t (g e) -> p (t g) e", e=GSZ)
                ch.done(dve.tensor_tensor(pair_sums[:, :, 0:2], s4[:, :, 0:2], s4[:, :, 2:4], ALU.add))
                ch.done(dve.tensor_tensor(pair_sums[:, :, 2:3], s4[:, :, 0:1], s4[:, :, 3:4], ALU.add))
                ch.done(dve.tensor_tensor(pair_sums[:, :, 3:4], s4[:, :, 1:2], s4[:, :, 2:3], ALU.add))
                link(dve.tensor_tensor(pair_sums[:, :, 4:6], s4[:, :, 0:4:2], s4[:, :, 1:4:2], ALU.add))
                gs = gsum[:, :, :]
                link(dve.tensor_reduce(gs.rearrange("p t g -> p (t g)"), pair_sums[:, :, :], AX.X, ALU.max))
                argmax(link, gs, gtmp[:, :, :], goh[:, 0, :, :], NG)
                link(dve.scalar_tensor_tensor(gs, goh[:, 0, :, :], -BIG, gs, ALU.mult, ALU.add))
                argmax(link, gs, gtmp[:, :, :], goh[:, 1, :, :], NG)
                link(dve.tensor_tensor(gtmp[:, :, :], goh[:, 0, :, :], goh[:, 1, :, :], ALU.add))
                link(dve.tensor_tensor(s4, s4, gtmp[:, :, :].rearrange("p t g -> p (t g)").unsqueeze(2)
                                       .to_broadcast([P, TT * NG, GSZ]), ALU.mult))
                argmax(link, choice, tmp, first, E)
                link(dve.scalar_tensor_tensor(choice, first, -BIG, choice, ALU.mult, ALU.add))
                argmax(link, choice, tmp, second, E)
                dve.tensor_tensor(tmp, first, second, ALU.add).then_inc(s_oh, 1)

            def place(f, ch):
                link = ch.link
                half_tiles = slice(TT * f, TT * f + TT)
                score, choice, tmp, cnt = (b[:, half_tiles, :] for b in (sig, sel, etmp, tile_cnt))
                first, second = oh[:, 0, half_tiles, :], oh[:, 1, half_tiles, :]
                dve.wait_ge(s_cnt_ps, f + 1)
                ch.done(dve.tensor_copy(choice.rearrange("p t e -> p (t e)"), rank_ps[f][0][:, 0:TT * E]))
                dve.tensor_copy(cnt.rearrange("p t e -> p (t e)"), rank_ps[f][1][:, 0:TT * E]).then_inc(s_cnt, 1)
                third = pair_sums[:, :, :].rearrange("p a b -> p (a b)")[:, 0:TT * E].rearrange("p (t e) -> p t e", e=E)
                src, dsts, step, cur = cnt, [tmp, third], 1, 0
                dve.wait_ge(s_cnt, f + 1)
                while step < TT:
                    dst = dsts[cur % 2]
                    ch.done(dve.tensor_copy(dst[:, 0:step, :], src[:, 0:step, :]))
                    link(dve.tensor_tensor(dst[:, step:, :], src[:, step:, :], src[:, 0:TT - step, :], ALU.add))
                    src, step, cur = dst, 2 * step, cur + 1
                link(dve.tensor_tensor(choice, choice, src, ALU.add))
                link(dve.tensor_scalar(count_i[:, 0, :], src[:, TT - 1, :], float(P - 1), None, ALU.add))
                link(dve.tensor_scalar(count_i[:, 1, :], count_i[:, 0, :], 7, None, ALU.logical_shift_right))
                link(dve.tensor_copy(count[:, 0, :], count_i[:, 1, :]))
                step, cur = 1, 0
                while step < E:
                    ch.done(dve.tensor_copy(count[:, cur + 1, 0:step], count[:, cur, 0:step]))
                    link(dve.tensor_tensor(count[:, cur + 1, step:], count[:, cur, step:], count[:, cur, 0:E - step],
                                           ALU.add))
                    step, cur = 2 * step, cur + 1
                ends = count[:, cur, :]
                link(dve.tensor_tensor(count[:, 5, :], ends, count[:, 0, :], ALU.subtract))
                link(dve.tensor_scalar(count[:, 5, :], count[:, 5, :], float(P), None, ALU.mult))
                link(dve.tensor_tensor(choice, choice, count[:, 5, :].unsqueeze(1).to_broadcast([P, TT, E]), ALU.add))
                for k, onehot in enumerate((first, second)):
                    link(dve.tensor_tensor(tmp, choice, onehot, ALU.mult))
                    link(dve.tensor_reduce(slot[:, k, half_tiles], tmp, AX.X, ALU.add))
                dve.tensor_copy(slot_i[:, :, half_tiles], slot[:, :, half_tiles]).then_inc(s_slot, 1)
                link(dve.tensor_tensor(past[:, :, :], tile_no[:, :, :].to_broadcast([1, SLOT_TILES, E]),
                                       ends[0:1, :].unsqueeze(1).to_broadcast([1, SLOT_TILES, E]), ALU.is_ge))
                link(dve.tensor_reduce(eoff[:, :, :].rearrange("a s j -> a (s j)"), past[:, :, :], AX.X, ALU.add))
                link(dve.scalar_tensor_tensor(eoff[:, :, :], eoff[:, :, :], float(E - 1), digit[:, :, :]
                                              .to_broadcast([1, SLOT_TILES // UNROLL, UNROLL]), ALU.min, ALU.mult))
                link(dve.tensor_reduce(packed[:, :], eoff[:, :, :], AX.X, ALU.add))
                link(dve.tensor_copy(packed_i[:, :, :].rearrange("a s h -> a (s h)"), packed[:, :]))
                link(dve.tensor_scalar(packed_i[:, :, 1], packed_i[:, :, 1], 4 * UNROLL, None, ALU.logical_shift_left))
                dve.tensor_tensor(experts_i[:, HSTEPS * f:HSTEPS * (f + 1)], packed_i[:, :, 0], packed_i[:, :, 1],
                                  ALU.bitwise_or).then_inc(s_eoff, 1)
                for k, onehot in enumerate((first, second)):
                    link(dve.tensor_tensor(choice, score, onehot, ALU.mult))
                    link(dve.tensor_reduce(gate[:, k, half_tiles], choice, AX.X, ALU.add))
                total = gate[:, 2, half_tiles]
                link(dve.tensor_tensor(total, gate[:, 0, half_tiles], gate[:, 1, half_tiles], ALU.add))
                link(dve.tensor_scalar(total, total, 1e-20, None, ALU.add))
                link(dve.reciprocal(total, total))
                link(dve.tensor_tensor(gate[:, 0:2, half_tiles], gate[:, 0:2, half_tiles],
                                       total.unsqueeze(1).to_broadcast([P, 2, TT]), ALU.mult))
                ch.end()

            dve.wait_ge(s_wo, 16 * 4)
            dve.wait_ge(s_iota, 2 + UNROLL)
            def shared_add(i, j):
                dve.wait_ge(s_d_ps, 2 * i + (j + 1))
                for n in range(2):
                    rows = X2[:, bass.ds(8 * i + (4 * j + 2 * n), 2), :]
                    last = dve.tensor_tensor(rows, bank[4 + 2 * j + n].rearrange("p (t d) -> p t d", t=2), rows,
                                             ALU.add)
                last.then_inc(s_x3, 1)

            for f in range(2):
                ch = Chain(dve, s_rt, 74, f)
                choose(f, ch)
                if f == 1:
                    for j in range(2):
                        shared_add(0, j)
                place(f, ch)
            for i in range(1, SH_FIRST):
                for j in range(2):
                    shared_add(i, j)

            def expert_act(i, h):
                dve.wait_ge(s_er, 2 * i + (h + 1))
                if since(i, 1):
                    dve.wait_ge(s_y_ps, 2 * i + (h - 1))
                dve.scalar_tensor_tensor(ea[:, h, :], bank[h], 0.0, er[h], ALU.max, ALU.mult).then_inc(s_ea, 1)

            def expert_out(i, h):
                dve.wait_ge(s_y_ps, 2 * i + (h + 1))
                if since(i, 1):
                    dve.wait_ge(s_ys[h], 16 * i)
                for c in range(2):
                    last = dve.tensor_copy(ey[:, h, 2 * c:2 * c + 2, :],
                                           bank[4 + 2 * h + c].rearrange("p (j d) -> p j d", j=2))
                last.then_inc(s_y, 1)

            def combine(m, b, h):
                n = 2 * m + b
                dve.wait_ge(s_g[b][h], 16 * 2 * GT * (m + 1))
                for k in range(2):
                    if k:
                        dve.wait_ge(s_gc, 2 * n + (h + 1))
                    for j in range(GT):
                        t = 2 * GT * n + (GT * h + j)
                        row = X2[:, bass.ds(t, 1), :].rearrange("p a d -> p (a d)")
                        last = dve.scalar_tensor_tensor(row, gath[b][:, h, k, j, :], gate[:, k, bass.ds(t, 1)],
                                                        row, ALU.mult, ALU.add)
                    last.then_inc(s_used if k else s_gc, 1)

            def expert_step(i):
                for h in range(2):
                    expert_act(i, h)
                for h in range(2):
                    expert_out(i, h)

            def combining_steps(m):
                for b in range(2):
                    i = 2 * m + (COMBINE + b)
                    for h in range(2):
                        expert_act(i, h)
                    for h in range(2):
                        combine(m, b, h)
                        expert_out(i, h)

            expert_step(0)
            with dve.Fori(1, COMBINE) as i:
                expert_step(i)
            combining_steps(0)
            with dve.Fori(1, GSTEPS // 2) as m:
                combining_steps(m)
            for i in range(COMBINE + GSTEPS, STEPS):
                expert_step(i)
            with dve.Fori(GSTEPS // 2, GSTEPS - 1) as m:
                for b in range(2):
                    for h in range(2):
                        combine(m, b, h)
            for h in range(2):
                combine(GSTEPS - 1, 0, h)
            for i in range(SH_FIRST, NCH // 2):
                if i > SH_FIRST:
                    for h in range(2):
                        combine(GSTEPS - 1, 1, h)
                for j in range(2):
                    dve.wait_ge(s_d_ps, 2 * i + (j + 1))
                    dve.wait_ge(s_used, 4 * i + (2 * j + 2))
                    for h in range(2):
                        dve.wait_ge(s_out[h], 32 * i + 16 * j)
                        last = dve.tensor_tensor(res[:, h, :, :],
                                                 bank[4 + 2 * j + h].rearrange("p (t d) -> p t d", t=2),
                                                 X2[:, bass.ds(8 * i + (4 * j + 2 * h), 2), :], ALU.add)
                        last.then_inc(s_res, 1)


_INS = ['x', 'ctx_1024', 'L0_xattn_Wq', 'L0_xattn_bq', 'L0_xattn_Wk', 'L0_xattn_bk', 'L0_xattn_Wv', 'L0_xattn_bv',
        'L0_xattn_Wkv_dca', 'L0_xattn_bkv_dca', 'L0_xattn_qn_w', 'L0_xattn_qn_b', 'L0_xattn_kn_w', 'L0_xattn_kn_b',
        'L0_xattn_kn_dca_w', 'L0_xattn_kn_dca_b', 'L0_xattn_Wo', 'L0_xattn_bo', 'L0_ffn_router_weight',
        'L0_ffn_e_bias', 'L0_ffn_w_up', 'L0_ffn_w_down', 'L0_ffn_shared_up', 'L0_ffn_shared_down']


def kernel(**inputs):
    import numpy as _np
    import concourse.bacc as _bacc
    from concourse import mybir as _mybir
    from concourse.bass_utils import run_bass_kernel_spmd as _run

    nc = _bacc.Bacc("TRN2", target_bir_lowering=False, num_devices=1)
    arrays, args = {}, []
    for name in _INS:
        a = _np.ascontiguousarray(inputs[name])
        arrays[f"in_{name}"] = a
        args.append(nc.dram_tensor(f"in_{name}", a.shape, _mybir.dt.from_np(a.dtype), kind="ExternalInput").ap())
    args.append(nc.dram_tensor("out_0", (NB, SQ, D), F32, kind="ExternalOutput").ap())
    xattn_moe(nc, *args)
    r = _run(nc, [arrays], core_ids=[0])
    return r.results[0]["out_0"]
```
